# Optimizing a Trainium2 kernel written in Bass

```python
import numpy as np
import jax
import jax.numpy as jnp

def _softmax(x, axis=-1):
    return jax.nn.softmax(x, axis=axis)

def _gelu(x):
    return jax.nn.gelu(x, approximate=True)

def _silu(x):
    return jax.nn.silu(x)

def _sigmoid(x):
    return jax.nn.sigmoid(x)

def _layernorm(x, axis=-1, eps=1e-05):
    m = jnp.mean(x, axis=axis, keepdims=True)
    v = jnp.var(x, axis=axis, keepdims=True)
    return (x - m) / jnp.sqrt(v + eps)

def _scatter_add(tgt, idx, src, axis=0):
    return tgt.at[idx].add(src)

def _segment_sum(src, seg, n):
    return jax.ops.segment_sum(src, seg, n)
kernel_name = 'mk_gnn_ffn_d2_gnn_r16_11a3be'

def setup_inputs(seed: int=0):
    np.random.seed(seed)
    _w = jnp.asarray

    def _rec_inputs():
        import jax
        import jax.numpy as jnp
        _gk = jax.random.key(seed)
        x = -0.0003713 + 1 * jax.random.normal(jax.random.fold_in(_gk, 1), (3125, 256), jnp.float32)
        _s = jax.random.randint(jax.random.fold_in(_gk, 2), (25000,), 0, 3125, jnp.int32)
        _d = jax.random.randint(jax.random.fold_in(_gk, 3), (25000,), 0, 3125, jnp.int32)
        _loop = jnp.arange(3125, dtype=jnp.int32)
        src = jnp.concatenate([_s, _d, _loop])
        dst = jnp.concatenate([_d, _s, _loop])
        _o = jnp.argsort(dst, stable=True)
        src = src[_o]
        dst = dst[_o]
        return (x, src, dst)
    x, src, dst = _rec_inputs()

    def _L0_gnn_setup():
        import jax, jax.numpy as jnp
        import numpy as np
        import math
        N_NODES = 3125
        N_EDGES = 100000
        C = 256
        H = 8
        HD = C // H

        def _layernorm(x, g, b, eps=1e-05):
            mu = jnp.mean(x, axis=-1, keepdims=True)
            var = jnp.mean(jnp.square(x - mu), axis=-1, keepdims=True)
            return (x - mu) * jax.lax.rsqrt(var + eps) * g + b
        key = jax.random.key(seed)
        ks = jax.random.split(key, 16)
        s = 0.02
        d = {'feat': jax.random.normal(ks[0], (N_NODES, C), jnp.float32), 'edge_src': jax.random.randint(ks[1], (N_EDGES,), 0, N_NODES), 'edge_dst': jax.random.randint(ks[2], (N_EDGES,), 0, N_NODES), 'Wq': jax.random.normal(ks[3], (C, C), jnp.float32) * s, 'bq': jnp.zeros((C,), jnp.float32), 'Wk': jax.random.normal(ks[4], (C, C), jnp.float32) * s, 'bk': jnp.zeros((C,), jnp.float32), 'Wv': jax.random.normal(ks[5], (C, C), jnp.float32) * s, 'bv': jnp.zeros((C,), jnp.float32), 'Wp': jax.random.normal(ks[6], (C, C), jnp.float32) * s, 'bp': jnp.zeros((C,), jnp.float32), 'ln_g': jnp.ones((C,), jnp.float32), 'ln_b': jnp.zeros((C,), jnp.float32), 'W1': jax.random.normal(ks[7], (4 * C, C), jnp.float32) * s, 'b1': jnp.zeros((4 * C,), jnp.float32), 'W2': jax.random.normal(ks[8], (C, 4 * C), jnp.float32) * s, 'b2': jnp.zeros((C,), jnp.float32)}
        return d
    _L0_gnn_all = _L0_gnn_setup()
    _L0_gnn_in = {k: v for k, v in _L0_gnn_all.items() if k in ('Wq', 'bq', 'Wk', 'bk', 'Wv', 'bv', 'Wp', 'bp', 'ln_g', 'ln_b', 'W1', 'b1', 'W2', 'b2')}
    del _L0_gnn_all

    def _L0_ffn_setup():
        import jax, jax.numpy as jnp
        import numpy as np
        TOP_K = 2
        key = jax.random.key(seed)
        ks = jax.random.split(key, 4)
        B, L, D, H, E = (8, 256, 256, 1024, 8)
        s = 0.02
        return {'x': jax.random.normal(ks[0], (B, L, D), jnp.float32), 'Wg': jax.random.normal(ks[1], (D, E), jnp.float32) * s, 'bg': jnp.zeros((E,), jnp.float32), 'W1': jax.random.normal(ks[2], (E, D, H), jnp.float32) * s, 'b1': jnp.zeros((E, H), jnp.float32), 'W2': jax.random.normal(ks[3], (E, H, D), jnp.float32) * s, 'b2': jnp.zeros((E, D), jnp.float32)}
    _L0_ffn_all = _L0_ffn_setup()
    _L0_ffn_in = {k: v for k, v in _L0_ffn_all.items() if k in ('Wg', 'bg', 'W1', 'b1', 'W2', 'b2')}
    del _L0_ffn_all

    def _L1_gnn_setup():
        import jax, jax.numpy as jnp
        import numpy as np
        N, E = (3125, 50000)
        IN, HID, OUT, HEADS = (256, 128, 256, 4)
        CAT = HEADS * HID

        def _gat(x, ei_src, ei_dst, W, a_src, a_dst, b, heads, out_ch, concat):
            n = x.shape[0]
            loop = jnp.arange(n, dtype=ei_src.dtype)
            src = jnp.concatenate([ei_src, loop])
            dst = jnp.concatenate([ei_dst, loop])
            h = (x @ W).reshape(n, heads, out_ch)
            al_s = jnp.einsum('nhc,hc->nh', h, a_src)
            al_d = jnp.einsum('nhc,hc->nh', h, a_dst)
            e = jax.nn.leaky_relu(al_s[src] + al_d[dst], 0.2)
            emax = jax.ops.segment_max(e, dst, num_segments=n)
            ee = jnp.exp(e - emax[dst])
            denom = jax.ops.segment_sum(ee, dst, num_segments=n)
            alpha = ee / (denom[dst] + 1e-16)
            out = jax.ops.segment_sum(h[src] * alpha[:, :, None], dst, num_segments=n)
            out = out.reshape(n, heads * out_ch) if concat else out.mean(axis=1)
            return out + b
        key = jax.random.key(seed)
        ks = jax.random.split(key, 20)
        g = lambda k, shape, fan: (jax.random.normal(k, shape, jnp.float32) / np.sqrt(fan)).astype(jnp.float32)
        return {'x': jax.random.normal(ks[0], (N, IN), jnp.float32), 'edge_index': jax.random.randint(ks[1], (2, E), 0, N, dtype=jnp.int32), 'W1': g(ks[2], (IN, CAT), IN), 'a_src1': g(ks[3], (HEADS, HID), HID), 'a_dst1': g(ks[4], (HEADS, HID), HID), 'b1': jnp.zeros((CAT,), jnp.float32), 'W2': g(ks[5], (CAT, CAT), CAT), 'a_src2': g(ks[6], (HEADS, HID), HID), 'a_dst2': g(ks[7], (HEADS, HID), HID), 'b2': jnp.zeros((CAT,), jnp.float32), 'W3': g(ks[8], (CAT, OUT), CAT), 'a_src3': g(ks[9], (1, OUT), OUT), 'a_dst3': g(ks[10], (1, OUT), OUT), 'b3': jnp.zeros((OUT,), jnp.float32), 'M1': g(ks[11], (OUT, 2 * HID), OUT), 'mb1': jnp.zeros((2 * HID,), jnp.float32), 'M2': g(ks[12], (2 * HID, HID), 2 * HID), 'mb2': jnp.zeros((HID,), jnp.float32), 'M3': g(ks[13], (HID, OUT), HID), 'mb3': jnp.zeros((OUT,), jnp.float32)}
    _L1_gnn_all = _L1_gnn_setup()
    _L1_gnn_in = {k: v for k, v in _L1_gnn_all.items() if k in ('W1', 'a_src1', 'a_dst1', 'b1', 'W2', 'a_src2', 'a_dst2', 'b2', 'W3', 'a_src3', 'a_dst3', 'b3', 'M1', 'mb1', 'M2', 'mb2', 'M3', 'mb3')}
    del _L1_gnn_all

    def _L1_ffn_setup():
        import jax, jax.numpy as jnp
        import numpy as np
        TOP_K = 2
        LN_EPS = 1e-05
        key = jax.random.key(seed)
        ks = jax.random.split(key, 8)
        B, S, D, E, H = (16, 1024, 256, 8, 1024)
        x = jax.random.normal(ks[0], (B, S, D), dtype=jnp.float32)
        Wr = jax.random.normal(ks[1], (D, E), dtype=jnp.float32) * 0.1
        br = jnp.zeros((E,), dtype=jnp.float32)
        ln_g = jnp.ones((E, D), dtype=jnp.float32)
        ln_b = jnp.zeros((E, D), dtype=jnp.float32)
        W1 = jax.random.normal(ks[2], (E, D, H), dtype=jnp.float32) * (1.0 / np.sqrt(D))
        b1 = jnp.zeros((E, H), dtype=jnp.float32)
        W2 = jax.random.normal(ks[3], (E, H, D), dtype=jnp.float32) * (1.0 / np.sqrt(H))
        b2 = jnp.zeros((E, D), dtype=jnp.float32)
        return {'x': x, 'Wr': Wr, 'br': br, 'ln_g': ln_g, 'ln_b': ln_b, 'W1': W1, 'b1': b1, 'W2': W2, 'b2': b2}
    _L1_ffn_all = _L1_ffn_setup()
    _L1_ffn_in = {k: v for k, v in _L1_ffn_all.items() if k in ('Wr', 'br', 'ln_g', 'ln_b', 'W1', 'b1', 'W2', 'b2')}
    del _L1_ffn_all
    return {'x': x, 'src': src, 'dst': dst, 'L0_gnn_Wq': _L0_gnn_in['Wq'], 'L0_gnn_bq': _L0_gnn_in['bq'], 'L0_gnn_Wk': _L0_gnn_in['Wk'], 'L0_gnn_bk': _L0_gnn_in['bk'], 'L0_gnn_Wv': _L0_gnn_in['Wv'], 'L0_gnn_bv': _L0_gnn_in['bv'], 'L0_gnn_Wp': _L0_gnn_in['Wp'], 'L0_gnn_bp': _L0_gnn_in['bp'], 'L0_gnn_ln_g': _L0_gnn_in['ln_g'], 'L0_gnn_ln_b': _L0_gnn_in['ln_b'], 'L0_gnn_W1': _L0_gnn_in['W1'], 'L0_gnn_b1': _L0_gnn_in['b1'], 'L0_gnn_W2': _L0_gnn_in['W2'], 'L0_gnn_b2': _L0_gnn_in['b2'], 'L0_ffn_Wg': _L0_ffn_in['Wg'], 'L0_ffn_bg': _L0_ffn_in['bg'], 'L0_ffn_W1': _L0_ffn_in['W1'], 'L0_ffn_b1': _L0_ffn_in['b1'], 'L0_ffn_W2': _L0_ffn_in['W2'], 'L0_ffn_b2': _L0_ffn_in['b2'], 'L1_gnn_W1': _L1_gnn_in['W1'], 'L1_gnn_a_src1': _L1_gnn_in['a_src1'], 'L1_gnn_a_dst1': _L1_gnn_in['a_dst1'], 'L1_gnn_b1': _L1_gnn_in['b1'], 'L1_gnn_W2': _L1_gnn_in['W2'], 'L1_gnn_a_src2': _L1_gnn_in['a_src2'], 'L1_gnn_a_dst2': _L1_gnn_in['a_dst2'], 'L1_gnn_b2': _L1_gnn_in['b2'], 'L1_gnn_W3': _L1_gnn_in['W3'], 'L1_gnn_a_src3': _L1_gnn_in['a_src3'], 'L1_gnn_a_dst3': _L1_gnn_in['a_dst3'], 'L1_gnn_b3': _L1_gnn_in['b3'], 'L1_gnn_M1': _L1_gnn_in['M1'], 'L1_gnn_mb1': _L1_gnn_in['mb1'], 'L1_gnn_M2': _L1_gnn_in['M2'], 'L1_gnn_mb2': _L1_gnn_in['mb2'], 'L1_gnn_M3': _L1_gnn_in['M3'], 'L1_gnn_mb3': _L1_gnn_in['mb3'], 'L1_ffn_Wr': _L1_ffn_in['Wr'], 'L1_ffn_br': _L1_ffn_in['br'], 'L1_ffn_ln_g': _L1_ffn_in['ln_g'], 'L1_ffn_ln_b': _L1_ffn_in['ln_b'], 'L1_ffn_W1': _L1_ffn_in['W1'], 'L1_ffn_b1': _L1_ffn_in['b1'], 'L1_ffn_W2': _L1_ffn_in['W2'], 'L1_ffn_b2': _L1_ffn_in['b2']}

def reference(x, src, dst, L0_gnn_Wq, L0_gnn_bq, L0_gnn_Wk, L0_gnn_bk, L0_gnn_Wv, L0_gnn_bv, L0_gnn_Wp, L0_gnn_bp, L0_gnn_ln_g, L0_gnn_ln_b, L0_gnn_W1, L0_gnn_b1, L0_gnn_W2, L0_gnn_b2, L0_ffn_Wg, L0_ffn_bg, L0_ffn_W1, L0_ffn_b1, L0_ffn_W2, L0_ffn_b2, L1_gnn_W1, L1_gnn_a_src1, L1_gnn_a_dst1, L1_gnn_b1, L1_gnn_W2, L1_gnn_a_src2, L1_gnn_a_dst2, L1_gnn_b2, L1_gnn_W3, L1_gnn_a_src3, L1_gnn_a_dst3, L1_gnn_b3, L1_gnn_M1, L1_gnn_mb1, L1_gnn_M2, L1_gnn_mb2, L1_gnn_M3, L1_gnn_mb3, L1_ffn_Wr, L1_ffn_br, L1_ffn_ln_g, L1_ffn_ln_b, L1_ffn_W1, L1_ffn_b1, L1_ffn_W2, L1_ffn_b2):
    import jax
    import jax.numpy as jnp

    def _L0_gnn_ref(feat, edge_src, edge_dst, Wq, bq, Wk, bk, Wv, bv, Wp, bp, ln_g, ln_b, W1, b1, W2, b2):
        import jax, jax.numpy as jnp
        import numpy as np
        import math
        N_NODES = 3125
        N_EDGES = 100000
        C = 256
        H = 8
        HD = C // H

        def _layernorm(x, g, b, eps=1e-05):
            mu = jnp.mean(x, axis=-1, keepdims=True)
            var = jnp.mean(jnp.square(x - mu), axis=-1, keepdims=True)
            return (x - mu) * jax.lax.rsqrt(var + eps) * g + b
        n = feat.shape[0]
        q = (feat @ Wq.T + bq).reshape(n, H, HD)
        k = (feat @ Wk.T + bk).reshape(n, H, HD)
        v = (feat @ Wv.T + bv).reshape(n, H, HD)
        score = jnp.einsum('ehd,ehd->eh', q[edge_dst], k[edge_src])
        score = jnp.clip(score / math.sqrt(HD), -10.0, 10.0)
        smax = jax.ops.segment_max(score, edge_dst, num_segments=n)
        smax = jnp.where(jnp.isfinite(smax), smax, 0.0)
        ex = jnp.exp(score - smax[edge_dst])
        den = jax.ops.segment_sum(ex, edge_dst, num_segments=n)
        alpha = ex / den[edge_dst]
        wv = jax.ops.segment_sum(alpha[:, :, None] * v[edge_src], edge_dst, num_segments=n).reshape(n, C)
        y = wv @ Wp.T + bp
        x = feat + y
        h = _layernorm(x, ln_g, ln_b)
        h = jax.nn.gelu(h @ W1.T + b1, approximate=False) @ W2.T + b2
        return x + h

    def _L0_ffn_ref(x, Wg, bg, W1, b1, W2, b2):
        import jax, jax.numpy as jnp
        import numpy as np
        TOP_K = 2
        B, L, D = x.shape
        E = W1.shape[0]
        xf = x.reshape(-1, D)
        gate_logits = xf @ Wg + bg
        top_w, top_i = jax.lax.top_k(gate_logits, TOP_K)
        top_w = jax.nn.softmax(top_w, axis=-1)
        w_dense = jnp.sum(jax.nn.one_hot(top_i, E, dtype=xf.dtype) * top_w[..., None], axis=1)
        out = jnp.zeros_like(xf)
        for e in range(E):
            h = jax.nn.gelu(xf @ W1[e] + b1[e], approximate=False)
            out = out + w_dense[:, e:e + 1] * (h @ W2[e] + b2[e])
        return out.reshape(B, L, D)

    def _L1_gnn_ref(x, edge_index, W1, a_src1, a_dst1, b1, W2, a_src2, a_dst2, b2, W3, a_src3, a_dst3, b3, M1, mb1, M2, mb2, M3, mb3):
        import jax, jax.numpy as jnp
        import numpy as np
        N, E = (3125, 50000)
        IN, HID, OUT, HEADS = (256, 128, 256, 4)
        CAT = HEADS * HID

        def _gat(x, ei_src, ei_dst, W, a_src, a_dst, b, heads, out_ch, concat):
            n = x.shape[0]
            loop = jnp.arange(n, dtype=ei_src.dtype)
            src = jnp.concatenate([ei_src, loop])
            dst = jnp.concatenate([ei_dst, loop])
            h = (x @ W).reshape(n, heads, out_ch)
            al_s = jnp.einsum('nhc,hc->nh', h, a_src)
            al_d = jnp.einsum('nhc,hc->nh', h, a_dst)
            e = jax.nn.leaky_relu(al_s[src] + al_d[dst], 0.2)
            emax = jax.ops.segment_max(e, dst, num_segments=n)
            ee = jnp.exp(e - emax[dst])
            denom = jax.ops.segment_sum(ee, dst, num_segments=n)
            alpha = ee / (denom[dst] + 1e-16)
            out = jax.ops.segment_sum(h[src] * alpha[:, :, None], dst, num_segments=n)
            out = out.reshape(n, heads * out_ch) if concat else out.mean(axis=1)
            return out + b
        src, dst = (edge_index[0], edge_index[1])
        h = _gat(x, src, dst, W1, a_src1, a_dst1, b1, HEADS, HID, True)
        h = jax.nn.elu(h)
        h = _gat(h, src, dst, W2, a_src2, a_dst2, b2, HEADS, HID, True)
        h = jax.nn.elu(h)
        h = _gat(h, src, dst, W3, a_src3, a_dst3, b3, 1, OUT, False)
        r = jax.nn.relu(h @ M1 + mb1)
        r = jax.nn.relu(r @ M2 + mb2)
        return r @ M3 + mb3

    def _L1_ffn_ref(x, Wr, br, ln_g, ln_b, W1, b1, W2, b2):
        import jax, jax.numpy as jnp
        import numpy as np
        TOP_K = 2
        LN_EPS = 1e-05
        B, S, D = x.shape
        N = B * S
        xt = x.reshape(N, D)
        logits = xt @ Wr + br
        probs = jax.nn.softmax(logits, axis=-1)
        top_p, top_idx = jax.lax.top_k(probs, TOP_K)
        weights = top_p / top_p.sum(axis=-1, keepdims=True)
        mu = xt.mean(axis=-1, keepdims=True)
        var = ((xt - mu) ** 2).mean(axis=-1, keepdims=True)
        xn = (xt - mu) * jax.lax.rsqrt(var + LN_EPS)
        xe = xn[None, :, :] * ln_g[:, None, :] + ln_b[:, None, :]
        h = jax.nn.gelu(jnp.einsum('end,edh->enh', xe, W1) + b1[:, None, :], approximate=False)
        y = jnp.einsum('enh,ehd->end', h, W2) + b2[:, None, :]
        y_tok = jnp.transpose(y, (1, 0, 2))
        sel = jnp.take_along_axis(y_tok, top_idx[:, :, None], axis=1)
        out = (weights[:, :, None] * sel).sum(axis=1)
        return out.reshape(B, S, D)
    edge_index = jnp.stack([src, dst])
    x = x + _L0_gnn_ref(_layernorm(x, axis=-1), src, dst, L0_gnn_Wq, L0_gnn_bq, L0_gnn_Wk, L0_gnn_bk, L0_gnn_Wv, L0_gnn_bv, L0_gnn_Wp, L0_gnn_bp, L0_gnn_ln_g, L0_gnn_ln_b, L0_gnn_W1, L0_gnn_b1, L0_gnn_W2, L0_gnn_b2)
    x = x + _L0_ffn_ref(_layernorm(x, axis=-1)[None], L0_ffn_Wg, L0_ffn_bg, L0_ffn_W1, L0_ffn_b1, L0_ffn_W2, L0_ffn_b2)[0]
    x = x + _L1_gnn_ref(_layernorm(x, axis=-1), edge_index, L1_gnn_W1, L1_gnn_a_src1, L1_gnn_a_dst1, L1_gnn_b1, L1_gnn_W2, L1_gnn_a_src2, L1_gnn_a_dst2, L1_gnn_b2, L1_gnn_W3, L1_gnn_a_src3, L1_gnn_a_dst3, L1_gnn_b3, L1_gnn_M1, L1_gnn_mb1, L1_gnn_M2, L1_gnn_mb2, L1_gnn_M3, L1_gnn_mb3)
    x = x + _L1_ffn_ref(_layernorm(x, axis=-1)[None], L1_ffn_Wr, L1_ffn_br, L1_ffn_ln_g, L1_ffn_ln_b, L1_ffn_W1, L1_ffn_b1, L1_ffn_W2, L1_ffn_b2)[0]
    return x

_drawn_inputs = setup_inputs


def setup_inputs(seed=0):
    import zlib

    import numpy as np

    out = dict(_drawn_inputs(seed))
    spreads = {'L0_gnn_bq': (0.0, 0.8),
     'L0_gnn_bk': (0.0, 2.0),
     'L0_gnn_bv': (0.0, 0.1),
     'L0_gnn_bp': (0.0, 0.1),
     'L0_gnn_ln_g': (1.0, 0.6),
     'L0_gnn_ln_b': (0.0, 0.483),
     'L0_gnn_b1': (0.0, 0.1),
     'L0_gnn_b2': (0.0, 0.1),
     'L0_ffn_bg': (0.0, 0.1),
     'L0_ffn_b1': (0.0, 0.325),
     'L0_ffn_b2': (0.0, 0.1),
     'L1_gnn_b1': (0.0, 0.298),
     'L1_gnn_b2': (0.0, 0.1),
     'L1_gnn_b3': (0.0, 0.1),
     'L1_gnn_mb1': (0.0, 0.1),
     'L1_gnn_mb2': (0.0, 0.1),
     'L1_gnn_mb3': (0.0, 0.1),
     'L1_ffn_br': (0.0, 0.1),
     'L1_ffn_ln_g': (1.0, 0.2),
     'L1_ffn_ln_b': (0.0, 0.302),
     'L1_ffn_b1': (0.0, 0.315),
     'L1_ffn_b2': (0.0, 0.1)}
    factors = {'L0_gnn_Wq': 8.0,
     'L0_gnn_Wk': 8.0,
     'L1_gnn_a_dst1': 25.817,
     'L1_gnn_a_src2': 8.0,
     'L1_gnn_a_dst2': 53.006,
     'L1_gnn_a_src3': 22.986,
     'L1_gnn_a_dst3': 61.594}
    for name, (base, spread) in spreads.items():
        noise = np.random.default_rng([zlib.crc32(name.encode()), seed]).standard_normal(out[name].shape)
        drawn = base * np.exp(spread * noise) if base else spread * noise
        out[name] = jnp.asarray(drawn.astype(out[name].dtype))
    for name, factor in factors.items():
        out[name] = (out[name] * factor).astype(out[name].dtype)
    return out
```

```python
from contextlib import ExitStack

import numpy as np

import concourse.bass as bass
from concourse import mybir

F32, BF16, I32, U32 = mybir.dt.float32, mybir.dt.bfloat16, mybir.dt.int32, mybir.dt.uint32
ALU = mybir.AluOpType
ACT = mybir.ActivationFunctionType
AX = mybir.AxisListType

P = 128
N, C, EDGES = 3125, 256, 53125
TILES = -(-N // P)
LAST = N - (TILES - 1) * P
PAIRS = -(-EDGES // (2 * P))
ITEMS = PAIRS + TILES - 1
SUBS = 2 * ITEMS
SUBP = -(-SUBS // P) * P
BLK = SUBP // P
GB = PAIRS // 2
NOWHERE = 4000
BIG = 1.0e30
HEADS0, HD0 = 8, 32
HID = 1024
EXPERTS = 8
SLOTS_X = (2 * N + EXPERTS * (P - 1)) // P
TABW = 516
ACCW = 524


class Chain:

    def __init__(self, eng, sem):
        self.eng, self.sem, self.base, self.local, self.per, self.start, self.turns = eng, sem, 0, 0, None, 0, 0

    def loop(self, turns, per):
        self.start, self.per, self.turns = self.base + self.local, per, turns
        return self

    def at(self, t):
        self.base, self.local = self.start + t * self.per, 0

    def over(self):
        self.base, self.local = self.start + self.turns * self.per, 0

    def mark(self, ins):
        self.local += 1
        assert self.per is None or self.local <= self.per or isinstance(self.base, int), "chain"
        ins.then_inc(self.sem, 1)

    def wait(self):
        self.eng.wait_ge(self.sem, self.base + self.local)

    def __call__(self, ins):
        self.mark(ins)
        self.wait()

    def full(self):
        assert self.local == self.per, (self.local, self.per)


def apart(ph, eng):
    eng.sem_inc(ph.passes, 1)


def ready(t, slots=2):
    return t + slots + 1


def free(t):
    return t + 1


def sweep(eng, n, step):
    with eng.Fori(0, n // 2) as i:
        step(2 * i, 0)
        step(2 * i + 1, 1)
    if n % 2:
        step(n - 1, 0)


def staggered(eng, n, steps):
    depth = len(steps) - 1
    steps = [s if s else (lambda t, slot: None) for s in steps]
    for i in range(-depth, 0):
        for j, step in enumerate(steps):
            if i + depth - j >= 0:
                step(i + depth - j, (i + depth - j) % 2)
    m = n - depth

    def turn(i, parity):
        for j, step in enumerate(steps):
            step(i + (depth - j), (parity + depth - j) % 2)

    with eng.Fori(0, m // 2) as i:
        turn(2 * i, 0)
        turn(2 * i + 1, 1)
    if m % 2:
        turn(m - 1, 0)
    for i in range(m, n):
        for j, step in enumerate(steps):
            if i + depth - j < n:
                step(i + depth - j, (i + depth - j) % 2)


def ringed(eng, n, ring, steps):
    assert n % ring == 0
    depth = len(steps) - 1
    steps = [s if s else (lambda t, r, i: None) for s in steps]

    def turn(base, i, r, limit):
        for j, step in enumerate(steps):
            d = r + depth - j
            if d >= 0 and d < limit:
                step(base + d, d % ring, i + d // ring)

    for r in range(-depth, 0):
        turn(0, 0, r, n)
    with eng.Fori(0, n // ring - 1) as i:
        for r in range(ring):
            turn(i * ring, i, r, n)
    for r in range(ring):
        turn(n - ring, n // ring - 1, r, ring)


class Kit:

    def __init__(self, nc, ctx, ins, out):
        self.nc, self.ctx, self.ins, self.out = nc, ctx, ins, out
        sb, dram = self.sb, self.dram
        self.ps = [ctx.enter_context(nc.psum_tensor(f"ps{i}", [P, 512], F32)) for i in range(8)]
        self.ident = sb("ident", [P, P], F32)
        self.ones = sb("ones", [P, P], F32)
        self.before = sb("before", [P, P], F32)
        self.iota_row = sb("iota_row", [P, 256], F32)
        self.iota_p = sb("iota_p", [P, 1], F32)
        self.x = sb("x", [P, TILES, C], F32)
        self.h = sb("h", [P, TILES, TABW], F32)
        self.acc = sb("acc", [P, TILES, ACCW], F32)
        self.item_tile = sb("item_tile", [1, ITEMS + 8], I32)
        self.src_of = sb("src_of", [P, SUBP], I32)
        self.dst_in = sb("dst_in", [P, SUBP], F32)
        self.src_hi = sb("src_hi", [P, SUBP], F32)
        self.is_last = sb("is_last", [P, SUBP], F32)
        self.dst_rows = dram("dst_rows", [SUBP, P], BF16)
        self.src_rows = dram("src_rows", [SUBP, P], BF16)
        self.key_rows = dram("key_rows", [SUBP + 1, P], F32)
        self.off_rows = dram("off_rows", [SUBP, P], F32)
        self.kv_table = dram("kv_table", [TILES * P, 512], F32)
        self.h_table = dram("h_table", [TILES * P, TABW], F32)
        self.h_table3 = dram("h_table3", [TILES * P, 257], F32)
        self.routed_in = dram("routed_in", [SLOTS_X * P, C], F32)
        self.routed_out = dram("routed_out", [SLOTS_X * P, C], F32)

    def sb(self, name, shape, dt):
        return self.ctx.enter_context(self.nc.sbuf_tensor(name, shape, dt))

    def dram(self, name, shape, dt):
        return self.nc.dram_tensor(name, shape, dt, kind="Internal").ap()


class Phase:

    def __init__(self, k, name):
        self.k, self.name, self.ctx, self.sems = k, name, ExitStack(), []
        self.passes = self.sem("passes")

    def __enter__(self):
        return self

    def __exit__(self, *a):
        self.ctx.__exit__(*a)
        self.k.nc.clear_and_free_semaphores(self.sems)
        self.k.nc.all_engine_barrier()

    def sem(self, name):
        self.sems.append(self.k.nc.alloc_semaphore(name=f"{self.name}_{name}"))
        return self.sems[-1]

    def sb(self, name, shape, dt=F32):
        return self.ctx.enter_context(self.k.nc.sbuf_tensor(f"{self.name}_{name}", shape, dt))

    def block(self):
        return self.ctx.enter_context(self.k.nc.Block())


def wide(row):
    return row.rearrange("(a c) -> a c", a=1).to_broadcast([P, row.shape[0]])



def phase_constants(k):
    nc = k.nc
    with Phase(k, "const") as ph:
        cleared, loaded, base, made = ph.sem("cleared"), ph.sem("loaded"), ph.sem("base"), ph.sem("made")
        block = ph.block()

        @block.gpsimd
        def _(pool):
            nc.gpsimd.memset(k.x[:, TILES - 1, :], 0.0).then_inc(cleared, 1)
            nc.gpsimd.iota(k.iota_row[:], pattern=[[1, 256]], base=0, channel_multiplier=0,
                           allow_small_or_imprecise_dtypes=True).then_inc(base, 1)
            nc.gpsimd.iota(k.iota_p[:], pattern=[[0, 1]], base=0, channel_multiplier=1,
                           allow_small_or_imprecise_dtypes=True).then_inc(base, 1)

        @block.vector
        def _(dve):
            nc.vector.memset(k.ones[:], 1.0)
            nc.vector.memset(k.item_tile[:], 0)
            dve.wait_ge(base, 2)
            nc.vector.tensor_scalar(k.ident[:], k.iota_row[:, 0:P], k.iota_p[:, 0:1], None, ALU.is_equal)
            nc.vector.tensor_scalar(k.before[:], k.iota_row[:, 0:P], k.iota_p[:, 0:1], None, ALU.is_gt)

        @block.sync
        def _(sp):
            full = (TILES - 1) * P
            sp.dma_start(k.x[:, 0:TILES - 1, :], k.ins["x"][0:full, :].rearrange("(t p) c -> p t c", p=P)).then_inc(loaded, 16)
            sp.wait_ge(cleared, 1)
            sp.dma_start(k.x[0:LAST, TILES - 1, :], k.ins["x"][full:N, :]).then_inc(loaded, 16)
            sp.wait_ge(loaded, 32)


def phase_items(k):
    nc = k.nc
    tail = EDGES - (PAIRS - 1) * 2 * P
    with Phase(k, "items") as ph:
        dst_i, src_i = ph.sb("dst_i", [P, 2, 256], I32), ph.sb("src_i", [P, 2, 256], I32)
        dst, src = ph.sb("dst", [P, 2, 256]), ph.sb("src", [P, 2, 256])
        lim = ph.sb("lim", [P, TILES - 1])
        passed = ph.sb("passed", [P, 2, TILES - 1])
        turn = ph.sb("turn", [P, 1])
        iota_k = ph.sb("iota_k", [P, ITEMS])
        stepped = ph.sb("stepped", [P, ITEMS])
        tile_of, pair_of = ph.sb("tile_of", [P, ITEMS]), ph.sb("pair_of", [P, ITEMS])
        sel = ph.sb("sel", [P, 2, ITEMS])
        src_f = ph.sb("src_f", [P, SUBP])
        dst_f = ph.sb("dst_f", [P, SUBP])
        hi_i = ph.sb("hi_i", [P, SUBP], I32)
        keys, offs = ph.sb("keys", [P, 2, 256]), ph.sb("offs", [P, 2, 256])
        nrow = ph.sb("nrow", [P, 2])
        lo_i = ph.sb("lo_i", [P, 2, 256], I32)
        lo_b, off_b = ph.sb("lo_b", [P, 2, 256], BF16), ph.sb("off_b", [P, 2, 256], BF16)
        padf, padb = ph.sb("padf", [P, P]), ph.sb("padb", [P, P], BF16)
        filled, loaded, iotas = ph.sem("filled"), ph.sem("loaded"), ph.sem("iotas")
        fed, made, link, stored, rows_out = ph.sem("fed"), ph.sem("made"), ph.sem("link"), ph.sem("stored"), ph.sem("rows_out")
        block = ph.block()
        kb = [(0, P), (P, ITEMS - P)]

        @block.gpsimd
        def _(pool):
            nc.gpsimd.memset(dst_i[:], NOWHERE).then_inc(filled, 1)
            nc.gpsimd.memset(src_i[:], 0).then_inc(filled, 1)
            nc.gpsimd.iota(iota_k[:], pattern=[[1, ITEMS]], base=0, channel_multiplier=0,
                           allow_small_or_imprecise_dtypes=True).then_inc(iotas, 1)
            nc.gpsimd.iota(lim[:], pattern=[[P, TILES - 1]], base=P, channel_multiplier=0,
                           allow_small_or_imprecise_dtypes=True).then_inc(iotas, 1)

        @block.sync
        def _(sp):
            sp.wait_ge(filled, 2)
            for tile, vec in ((dst_i, k.ins["dst"]), (src_i, k.ins["src"])):
                sp.dma_start(tile[0:GB, 0, :], vec[0:GB * 256].rearrange("(g e) -> g e", e=256)).then_inc(loaded, 16)
                sp.dma_start(tile[0:GB - 1, 1, :],
                             vec[GB * 256:(PAIRS - 1) * 256].rearrange("(g e) -> g e", e=256)).then_inc(loaded, 16)
                sp.dma_start(tile[GB - 1:GB, 1, 0:tail],
                             vec[(PAIRS - 1) * 256:EDGES].rearrange("(g e) -> g e", g=1)).then_inc(loaded, 16)
            sp.wait_ge(rows_out, 1)
            for tab, pad in ((k.dst_rows, padb), (k.src_rows, padb), (k.off_rows, padf)):
                sp.dma_start(tab[SUBS:SUBP, :], pad[0:SUBP - SUBS, :]).then_inc(stored, 16)
            sp.dma_start(k.key_rows[SUBS:SUBP + 1, :], padf[0:SUBP + 1 - SUBS, :]).then_inc(stored, 16)
            sp.wait_ge(rows_out, 2)
            for b, (k0, m) in enumerate(kb):
                for tab, tile in ((k.dst_rows, off_b), (k.src_rows, lo_b), (k.off_rows, offs), (k.key_rows, keys)):
                    sp.dma_start(tab[2 * k0:2 * (k0 + m), :].rearrange("(g s) e -> g (s e)", s=2), tile[0:m, b, :]).then_inc(stored, 16)
            sp.wait_ge(stored, 16 * 12)

        @block.tensor
        def _(pe):
            pe.wait_ge(fed, 1)
            for b in range(2):
                mm = nc.tensor.matmul(k.ps[0][0:TILES - 1, 0:1], passed[0:GB, b, :], k.ones[0:GB, 0:1],
                                      start=(b == 0), stop=(b == 1))
            mm.then_inc(made, 1)
            pe.wait_ge(fed, 2)
            nc.tensor.matmul(k.ps[1][:, 0:ITEMS], k.ones[0:TILES - 1, :], stepped[0:TILES - 1, :], start=True, stop=True)
            for b, (k0, m) in enumerate(kb):
                mm = nc.tensor.matmul(k.ps[2 + b][0:m, 0:1], stepped[0:TILES - 1, k0:k0 + m], k.ones[0:TILES - 1, 0:1],
                                      start=True, stop=True)
            mm.then_inc(made, 1)
            pe.wait_ge(fed, 3)
            for a, arr in enumerate((dst, src)):
                for s in range(2):
                    for b in range(2):
                        mm = nc.tensor.matmul(k.ps[4 + 2 * a + s][:, 0:ITEMS], arr[0:GB, b, s * P:(s + 1) * P],
                                              sel[0:GB, b, :], start=(b == 0), stop=(b == 1))
            mm.then_inc(made, 1)
            pe.wait_ge(fed, 4)
            for a, arr in enumerate((dst, src)):
                for q, (k0, m) in enumerate(kb):
                    for b in range(2):
                        mm = nc.tensor.matmul(k.ps[[0, 1][a]][0:m, q * 256:q * 256 + 256], sel[0:GB, b, k0:k0 + m],
                                              arr[0:GB, b, :], start=(b == 0), stop=(b == 1))
            mm.then_inc(made, 1)

        @block.vector
        def _(dve):
            v, c = nc.vector, Chain(dve, link)
            v.memset(padf[:], float(NOWHERE))
            c.mark(v.memset(src_f[:], 0.0))
            c.mark(v.memset(dst_f[:], float(NOWHERE)))
            c(v.memset(padb[:], float(NOWHERE)))
            v.memset(sel[:], 0.0).then_inc(rows_out, 1)
            dve.wait_ge(loaded, 96)
            dve.wait_ge(iotas, 2)
            c.mark(v.tensor_copy(dst[:], dst_i[:]))
            c(v.tensor_copy(src[:], src_i[:]))
            for b in range(2):
                last = v.tensor_scalar(passed[:, b, :], lim[:], dst[:, b, 255:256], None, ALU.is_gt)
                c.mark(last)
            c.wait()
            dve.sem_inc(fed, 1)
            dve.wait_ge(made, 1)
            c(v.tensor_scalar(turn[0:TILES - 1, :], k.ps[0][0:TILES - 1, 0:1], k.iota_p[0:TILES - 1, 0:1], None, ALU.add))
            v.tensor_scalar(stepped[0:TILES - 1, :], iota_k[0:TILES - 1, :], turn[0:TILES - 1, 0:1], None,
                            ALU.is_gt).then_inc(fed, 1)
            dve.wait_ge(made, 2)
            c(v.tensor_copy(tile_of[:], k.ps[1][:, 0:ITEMS]))
            c.mark(v.tensor_copy(k.item_tile[0:1, 0:ITEMS], tile_of[0:1, :]))
            c(v.tensor_tensor(pair_of[:], iota_k[:], tile_of[:], ALU.subtract))
            for b in range(2):
                c(v.tensor_scalar(sel[:, b, :], pair_of[:], float(-GB * b), k.iota_p[:, 0:1], ALU.add, ALU.is_equal))
                if b == 0:
                    for q, (k0, m) in enumerate(kb):
                        c(v.tensor_scalar(nrow[0:m, q:q + 1], k.ps[2 + q][0:m, 0:1], float(P), None, ALU.mult))
            dve.sem_inc(fed, 1)
            dve.wait_ge(made, 3)
            for s in range(2):
                c.mark(v.tensor_copy(dst_f[:, s:SUBS:2], k.ps[4 + s][:, 0:ITEMS]))
                c(v.tensor_copy(src_f[:, s:SUBS:2], k.ps[6 + s][:, 0:ITEMS]))
            dve.sem_inc(fed, 1)
            c(v.tensor_copy(k.src_of[:], src_f[:]))
            c(v.tensor_scalar(hi_i[:], k.src_of[:], 7, None, ALU.arith_shift_right))
            c(v.tensor_copy(k.src_hi[:], hi_i[:]))
            v.tensor_copy(k.dst_in[:, SUBS:SUBP], dst_f[:, SUBS:SUBP])
            for s in range(2):
                c(v.scalar_tensor_tensor(k.dst_in[:, s:SUBS:2], tile_of[:], float(-P), dst_f[:, s:SUBS:2], ALU.mult, ALU.add))
            dve.wait_ge(made, 4)
            for q, (k0, m) in enumerate(kb):
                c.mark(v.tensor_copy(keys[0:m, q, :], k.ps[0][0:m, q * 256:q * 256 + 256]))
                c(v.tensor_scalar(offs[0:m, q, :], k.ps[0][0:m, q * 256:q * 256 + 256], nrow[0:m, q:q + 1], None, ALU.subtract))
                c.mark(v.tensor_copy(off_b[0:m, q, :], offs[0:m, q, :]))
                c(v.tensor_copy(lo_i[0:m, q, :], k.ps[1][0:m, q * 256:q * 256 + 256]))
                c(v.tensor_scalar(lo_i[0:m, q, :], lo_i[0:m, q, :], 127, None, ALU.bitwise_and))
                c(v.tensor_copy(lo_b[0:m, q, :], lo_i[0:m, q, :]))
            dve.sem_inc(rows_out, 1)



def phase_norm(k, name, src, eps, rstd, shift):
    nc = k.nc
    group = 5
    with Phase(k, name) as ph:
        stats, mv = ph.sb("stats", [P, group, 6]), ph.sb("mv", [P, group, 2])
        both = ph.sb("both", [P, TILES, 2])
        link, var_ready, root_ready = ph.sem("link"), ph.sem("var_ready"), ph.sem("root_ready")
        block = ph.block()

        @block.vector
        def _(dve):
            v, c = nc.vector, Chain(dve, link)
            turns = TILES // group
            c.loop(turns, 3 * group - group + 1)
            with dve.Fori(0, turns) as g:
                c.at(g)
                for j in range(group):
                    c.mark(v.bn_stats(stats[:, j:j + 1, :], src[:, bass.ds(g * group + j, 1), 0:C]))
                c.wait()
                apart(ph, dve)
                for j in range(group):
                    c.mark(v.bn_aggr(mv[:, j, :], stats[:, j, :]))
                c.wait()
                c(v.tensor_copy(both[:, bass.ds(g * group, group), :], mv[:]))
                c.full()
            c.over()
            v.tensor_scalar(rstd[:], both[:, :, 1], eps, None, ALU.add).then_inc(var_ready, 1)
            dve.wait_ge(root_ready, 1)
            c(v.reciprocal(rstd[:], shift[:]))
            v.scalar_tensor_tensor(shift[:], both[:, :, 0], -1.0, rstd[:], ALU.mult, ALU.mult)

        @block.scalar
        def _(act):
            act.wait_ge(var_ready, 1)
            nc.scalar.activation(shift[:], rstd[:], ACT.Sqrt).then_inc(root_ready, 1)


def phase_dense(k, name, kb, outs, stage, per_stage, evac, per_evac, loads=(), sb=(), stores=(), exps=None):
    nc = k.nc
    with Phase(k, name) as ph:
        ph.buf = {n: ph.sb(n, shape, dt) for n, shape, dt in sb}
        staged_tile = ph.sb("staged_tile", [P, 2, kb * P])
        turned_tile = ph.sb("turned_tile", [P, 2, kb * P])
        loaded = ph.sem("loaded")
        staged, turned, copied, made, taken = (ph.sem(s) for s in ("staged", "turned", "copied", "made", "taken"))
        link_s, link_e, stored = ph.sem("link_s"), ph.sem("link_e"), ph.sem("stored")
        ph.capped, ph.exped = ph.sem("capped"), ph.sem("exped")
        pst = [k.ps[0], k.ps[1]]
        pso = [[k.ps[2 + s * len(outs) + j] for j in range(len(outs))] for s in range(2)]
        block = ph.block()
        nload = 0

        @block.sync
        def _(sp):
            for dst, src in loads:
                sp.dma_start(ph.buf[dst][:] if isinstance(dst, str) else dst, src).then_inc(loaded, 16)
            for last, dst, src in stores:
                sp.wait_ge(taken, ready(last))
                sp.dma_start(dst, src).then_inc(stored, 16)
            if loads:
                sp.wait_ge(loaded, 16 * len(loads))
            if stores:
                sp.wait_ge(stored, 16 * len(stores))

        @block.vector
        def _(dve):
            dve.sem_inc(staged, 2)
            dve.sem_inc(taken, 2)
            cs = Chain(dve, link_s).loop(TILES, per_stage)
            ce = Chain(dve, link_e).loop(TILES, per_evac)
            if loads:
                dve.wait_ge(loaded, 16 * len(loads))

            def stage_step(t, slot):
                dve.wait_ge(turned, free(t))
                cs.at(t)
                stage(ph, t, slot, staged_tile[:, slot, :], cs).then_inc(staged, 1)
                cs.full()

            def evac_step(t, slot):
                dve.wait_ge(made, ready(t))
                ce.at(t)
                evac(ph, t, slot, pso[slot], ce).then_inc(taken, 1)
                ce.full()

            staggered(dve, TILES, [stage_step, None, evac_step])

        @block.scalar
        def _(act):
            act.sem_inc(copied, 2)

            def copy_step(t, slot):
                act.wait_ge(turned, ready(t))
                act.wait_ge(made, free(t))
                nc.scalar.copy(turned_tile[:, slot, :], pst[slot][:, 0:kb * P]).then_inc(copied, 1)

            def exp_step(t, slot):
                act.wait_ge(ph.capped, t + 1)
                act.activation(ph.buf[exps][:, slot, :], ph.buf[exps][:, slot, :], ACT.Exp).then_inc(ph.exped, 1)

            staggered(act, TILES, [exp_step, copy_step] if exps else [copy_step])

        @block.tensor
        def _(pe):
            pe.sem_inc(turned, 2)
            pe.sem_inc(made, 2)
            if loads:
                pe.wait_ge(loaded, 16 * len(loads))

            def turn_step(t, slot):
                pe.wait_ge(staged, ready(t))
                pe.wait_ge(copied, free(t))
                for b in range(kb):
                    mm = nc.tensor.transpose(pst[slot][:, b * P:(b + 1) * P], staged_tile[:, slot, b * P:(b + 1) * P],
                                             k.ident[:])
                mm.then_inc(turned, 1)

            def product_step(t, slot):
                pe.wait_ge(copied, ready(t))
                pe.wait_ge(taken, free(t))
                for j, (w, width) in enumerate(outs):
                    wt = ph.buf[w] if isinstance(w, str) else w
                    for b in range(kb):
                        mm = nc.tensor.matmul(pso[slot][j][:, 0:width], turned_tile[:, slot, b * P:(b + 1) * P],
                                              wt[:, b, 0:width], start=(b == 0), stop=(b == kb - 1))
                mm.then_inc(made, 1)

            staggered(pe, TILES, [turn_step, product_step])


def weights(w):
    return w.rearrange("(b p) n -> p b n", p=P)


def stage_normed(k, src, rstd, shift):
    def stage(ph, t, slot, dst, c):
        return k.nc.vector.tensor_scalar(dst, src[:, bass.ds(t, 1), 0:C].rearrange("p a c -> p (a c)"),
                                         rstd[:, bass.ds(t, 1)], shift[:, bass.ds(t, 1)], ALU.mult, ALU.add)
    return stage


def row(buf, t, a, b):
    return buf[:, bass.ds(t, 1), a:b].rearrange("p a c -> p (a c)")


def tile_stores(table, src, width):
    out = []
    for g in range(0, TILES, 5):
        out.append((g + 4, table[g * P:(g + 5) * P, 0:width].rearrange("(t p) c -> p t c", p=P), src[:, g:g + 5, 0:width]))
    return out

def phase_qkv(k, rstd, shift):
    nc, a = k.nc, k.ins

    def evac(ph, t, slot, ps, c):
        c(nc.vector.tensor_tensor(row(k.h, t, 0, C), ps[0][:, 0:C], ph.buf["bq"][:], ALU.add))
        nc.vector.tensor_scalar(row(k.h, t, 0, C), row(k.h, t, 0, C), float(HD0) ** -0.5, None, ALU.mult)
        return nc.vector.tensor_tensor(row(k.acc, t, 0, 2 * C), ps[1][:, 0:2 * C], ph.buf["bkv"][:], ALU.add)

    phase_dense(
        k, "qkv", 2, [("wq", C), ("wkv", 2 * C)], stage_normed(k, k.x, rstd, shift), 0, evac, 1,
        sb=[("wq", [P, 2, C], F32), ("wkv", [P, 2, 2 * C], F32), ("bq", [P, C], F32), ("bkv", [P, 2 * C], F32)],
        loads=[("wq", weights(a["L0_gnn_Wq"])), ("wkv", weights(a["L0_gnn_Wkv"])),
               ("bq", wide(a["L0_gnn_bq"])), ("bkv", wide(a["L0_gnn_bkv"]))],
        stores=tile_stores(k.kv_table, k.acc, 2 * C))


def load_batches(sp, used, credits, tables, row_in):
    def load(b, slot):
        for table, tile in tables:
            sp.dma_start(tile[:, slot, :], item_rows(table, 4 * b, 4)).then_inc(row_in[slot], 16)

    load(0, 0)
    load(1, 1)
    with sp.Fori(0, ITEMS // 8 - 1) as i:
        for slot in range(2):
            sp.wait_ge(used, i * 8 + (4 * slot + 4 + credits))
            load(2 * i + (2 + slot), slot)


def phase_attention_edges(k):
    nc = k.nc
    RING = 8
    W = C + HEADS0
    with Phase(k, "edges0") as ph:
        rows = ph.sb("rows", [P, RING, 2, 2 * C])
        index = ph.sb("index", [P, RING, 2], I32)
        dst_row = ph.sb("dst_row", [P, 2, 4 * 256], BF16)
        minus_p, one_col = ph.sb("minus_p", [P, 1]), ph.sb("one_col", [P, 1])
        hot_t = ph.sb("hot_t", [P, 2, 256])
        hot = ph.sb("hot", [P, 2, 2, P])
        prod = ph.sb("prod", [P, 2 * C])
        score = ph.sb("score", [P, 2, 2 * HEADS0])
        out_rows = ph.sb("out_rows", [P, 2, 2, W])
        cleared, indexed = ph.sem("cleared"), ph.sem("indexed")
        gathered = [ph.sem(f"gathered{r}") for r in range(RING)]
        row_in = [ph.sem(f"row_in{s}") for s in range(2)]
        hot_t_made, q_made, clipped, exped, weighted, summed, added = (
            ph.sem(s) for s in ("hot_t_made", "q_made", "clipped", "exped", "weighted", "summed", "added"))
        link_a, link_v = ph.sem("link_a"), ph.sem("link_v")
        psq, pso = [k.ps[0], k.ps[1]], [k.ps[2], k.ps[3]]
        block = ph.block()

        @block.sync
        def _(sp):
            load_batches(sp, hot_t_made, 2, [(k.dst_rows, dst_row)], row_in)

        @block.gpsimd
        def _(pool):
            with pool.Fori(0, ITEMS // RING) as i:
                for r in range(RING):
                    pool.wait_ge(indexed, i * RING + r + 1)
                    apart(ph, pool)
                    for s in range(2):
                        nc.gpsimd.indirect_dma_start(rows[:, r, s, :], None, k.kv_table,
                                                     bass.IndirectOffsetOnAxis(ap=index[:, r, s:s + 1], axis=0)
                                                     ).then_inc(gathered[r], 16)

        @block.scalar
        def _(act):
            act.sem_inc(hot_t_made, 2)
            act.sem_inc(exped, 2)

            def one_hot_t(t, r, i):
                slot = r % 2
                act.wait_ge(row_in[r // 4], (i + 1) * 16)
                act.wait_ge(q_made, free(t))
                act.activation(hot_t[:, slot, :], dst_row[:, r // 4, r % 4 * 256:(r % 4 + 1) * 256], ACT.Abs, bias=minus_p[:, 0:1]).then_inc(link_a, 1)
                act.wait_ge(link_a, t + 1)
                act.activation(hot_t[:, slot, :], hot_t[:, slot, :], ACT.Relu, bias=one_col[:, 0:1], scale=-1.0
                               ).then_inc(hot_t_made, 1)

            def exps(t, r, i):
                slot = r % 2
                act.wait_ge(clipped, ready(t))
                act.wait_ge(summed, free(t))
                act.activation(out_rows[:, slot, :, C:W], score[:, slot, :].rearrange("p (s h) -> p s h", s=2),
                               ACT.Exp).then_inc(exped, 1)

            act.wait_ge(cleared, 3)
            ringed(act, ITEMS, RING, [one_hot_t, None, exps])

        @block.tensor
        def _(pe):
            pe.sem_inc(q_made, 2)
            pe.sem_inc(summed, 2)

            def q_of_edges(t, slot):
                n = pe.value_load(k.item_tile[0:1, bass.ds(t, 1)], min_val=0, max_val=TILES - 1)
                pe.wait_ge(hot_t_made, ready(t))
                pe.wait_ge(clipped, free(t))
                for s in range(2):
                    mm = nc.tensor.matmul(psq[slot][:, s * C:(s + 1) * C], hot_t[:, slot, s * P:(s + 1) * P],
                                          row(k.h, n, 0, C), start=True, stop=True)
                mm.then_inc(q_made, 1)

            def sums(t, slot):
                pe.wait_ge(weighted, ready(t))
                pe.wait_ge(exped, ready(t))
                pe.wait_ge(added, free(t))
                for s in range(2):
                    mm = nc.tensor.matmul(pso[slot][:, 0:W], hot[:, slot, s, :], out_rows[:, slot, s, :],
                                          start=(s == 0), stop=(s == 1))
                mm.then_inc(summed, 1)

            staggered(pe, ITEMS, [q_of_edges, None, sums])

        @block.vector
        def _(dve):
            v, c = nc.vector, Chain(dve, link_v).loop(ITEMS, 2)
            v.memset(k.acc[:, :, 0:W], 0.0).then_inc(cleared, 1)
            v.memset(one_col[:], 1.0).then_inc(cleared, 1)
            v.tensor_scalar(minus_p[:], k.iota_p[:], -1.0, None, ALU.mult).then_inc(cleared, 1)
            for s in (clipped, weighted, added):
                dve.sem_inc(s, 2)
            dve.wait_ge(cleared, 3)

            def stage_index(t, r):
                v.tensor_copy(index[:, r, :], k.src_of[:, bass.ds(2 * t, 2)]).then_inc(indexed, 1)

            def scores(t, r, i):
                slot = r % 2
                c.at(t)
                dve.wait_ge(gathered[r], (i + 1) * 32)
                dve.wait_ge(q_made, ready(t))
                c(v.tensor_tensor(prod[:], psq[slot][:, 0:2 * C], rows[:, r, :, 0:C], ALU.mult))
                dve.wait_ge(exped, free(t))
                c(v.tensor_reduce(score[:, slot, :], prod[:].rearrange("p (g d) -> p g d", d=HD0), AX.X, ALU.add))
                c.full()
                v.tensor_scalar(score[:, slot, :], score[:, slot, :], 10.0, -10.0, ALU.min, ALU.max).then_inc(clipped, 1)

            def weigh(t, r, i):
                slot = r % 2
                dve.wait_ge(summed, free(t))
                for s in range(2):
                    v.tensor_scalar(hot[:, slot, s, :], k.iota_row[:, 0:P], k.dst_in[:, bass.ds(2 * t + s, 1)], None,
                                    ALU.is_equal)
                dve.wait_ge(exped, ready(t))
                for s in range(2):
                    e = out_rows[:, slot, s, C:W].rearrange("p (h o) -> p h o", o=1).to_broadcast([P, HEADS0, HD0])
                    last = v.tensor_tensor(out_rows[:, slot, s, 0:C].rearrange("p (h d) -> p h d", d=HD0),
                                           rows[:, r, s, C:2 * C].rearrange("p (h d) -> p h d", d=HD0), e, ALU.mult)
                last.then_inc(weighted, 1)

            def add(t, r, i):
                n = dve.value_load(k.item_tile[0:1, bass.ds(t, 1)], min_val=0, max_val=TILES - 1)
                dve.wait_ge(weighted, ready(t))
                stage_index(t + RING, r)
                dve.wait_ge(summed, ready(t))
                dve.wait_ge(added, t + 2)
                v.tensor_tensor(row(k.acc, n, 0, W), row(k.acc, n, 0, W), pso[r % 2][:, 0:W], ALU.add
                                ).then_inc(added, 1)

            for r in range(RING):
                stage_index(r, r)
            ringed(dve, ITEMS, RING, [scores, weigh, add])


def item_rows(table, t, n):
    return table[bass.ds(2 * t, 2 * n), :].rearrange("s e -> (s e)").rearrange("(a c) -> a c", a=1).to_broadcast([P, n * 256])


def phase_attention_out(k, rstd, shift):
    nc, a = k.nc, k.ins

    def stage(ph, t, slot, dst, c):
        v, den = nc.vector, ph.buf["den"]
        c(v.tensor_scalar(den[:, slot, :], row(k.acc, t, C, C + HEADS0), 1e-30, None, ALU.max))
        c(v.reciprocal(den[:, slot, :], den[:, slot, :]))
        return v.tensor_tensor(dst.rearrange("p (h d) -> p h d", d=HD0),
                               row(k.acc, t, 0, C).rearrange("p (h d) -> p h d", d=HD0),
                               den[:, slot, :].rearrange("p (h o) -> p h o", o=1).to_broadcast([P, HEADS0, HD0]), ALU.mult)

    def evac(ph, t, slot, ps, c):
        v, feat = nc.vector, ph.buf["feat"]
        c(v.tensor_scalar(feat[:, slot, :], row(k.x, t, 0, C), rstd[:, bass.ds(t, 1)], shift[:, bass.ds(t, 1)],
                          ALU.mult, ALU.add))
        c(v.tensor_tensor(feat[:, slot, :], feat[:, slot, :], ph.buf["bp"][:], ALU.add))
        return v.tensor_tensor(row(k.h, t, 0, C), ps[0][:, 0:C], feat[:, slot, :], ALU.add)

    phase_dense(k, "proj", 2, [("wp", C)], stage, 2, evac, 2,
                sb=[("wp", [P, 2, C], F32), ("bp", [P, C], F32), ("den", [P, 2, HEADS0], F32), ("feat", [P, 2, C], F32)],
                loads=[("wp", weights(a["L0_gnn_Wp"])), ("bp", wide(a["L0_gnn_bp"]))])



class Ffn:

    def __init__(self, ph, sets):
        self.w1, self.w2 = ph.sb("w1", [P, sets, 2, HID]), ph.sb("w2", [P, sets, HID // P, C])
        self.b1, self.b2 = ph.sb("b1", [P, sets, HID // P]), ph.sb("b2", [P, sets, C])
        self.g, self.b = ph.sb("g", [P, sets, 2]), ph.sb("b", [P, sets, 2])
        self.rows, self.turned = ph.sb("rows", [P, 2, C]), ph.sb("turned", [P, 2, 2, P])
        self.hidden = ph.sb("hidden", [P, 2, HID // P, P])
        self.rows_ready, self.turns, self.copies = ph.sem("rows_ready"), ph.sem("turns"), ph.sem("copies")
        self.ups, self.gelus, self.downs, self.taken = (ph.sem(s) for s in ("ups", "gelus", "downs", "taken"))
        self.rows_in, self.up_in, self.down_in = ([ph.sem(f"{n}{s}") for s in range(2)] for n in ("rows_in", "up_in", "down_in"))
        self.weights_in = ph.sem("weights_in")


def ffn_tensor(k, f, pe, n, wait_rows, wait_up, wait_down, multi):
    nc = k.nc
    pst, psh = [k.ps[0], k.ps[1]], [[k.ps[2], k.ps[3]], [k.ps[4], k.ps[5]]]
    pso = [k.ps[6], k.ps[7]]
    for s in (f.turns, f.ups, f.downs):
        pe.sem_inc(s, 2)

    def turn(t, slot):
        wait_rows(pe, t, slot)
        pe.wait_ge(f.copies, free(t))
        for b in range(2):
            mm = nc.tensor.transpose(pst[slot][:, b * P:(b + 1) * P], f.rows[:, slot, b:C:2], k.ident[:])
        mm.then_inc(f.turns, 1)

    def up(t, slot):
        wait_up(pe, t, slot)
        pe.wait_ge(f.copies, ready(t))
        pe.wait_ge(f.gelus, free(t))
        w = slot if multi else 0
        for j in range(HID // P):
            for b in range(2):
                mm = nc.tensor.matmul(psh[slot][j // 4][:, (j % 4) * P:(j % 4 + 1) * P], f.w1[:, w, b, j:HID:HID // P],
                                      f.turned[:, slot, b, :], start=(b == 0), stop=(b == 1))
        mm.then_inc(f.ups, 1)

    def down(t, slot):
        wait_down(pe, t, slot)
        pe.wait_ge(f.gelus, ready(t))
        pe.wait_ge(f.taken, free(t))
        w = slot if multi else 0
        for j in range(HID // P):
            mm = nc.tensor.matmul(pso[slot][:, 0:C], f.hidden[:, slot, j, :], f.w2[:, w, j, :],
                                  start=(j == 0), stop=(j == HID // P - 1))
        mm.then_inc(f.downs, 1)

    staggered(pe, n, [turn, up, down])


def ffn_scalar(k, f, act, n, wait_up, multi, affine):
    nc = k.nc
    act.sem_inc(f.copies, 2)
    act.sem_inc(f.gelus, 2)

    def copy(t, slot):
        w = slot if multi else 0
        wait_up(act, t, slot)
        act.wait_ge(f.turns, ready(t))
        act.wait_ge(f.ups, free(t))
        ps = k.ps[slot]
        if affine:
            for b in range(2):
                last = act.activation(f.turned[:, slot, b, :], ps[:, b * P:(b + 1) * P], ACT.Identity,
                                      bias=f.b[:, w, b:b + 1], scale=f.g[:, w, b:b + 1])
        else:
            last = act.copy(f.turned[:, slot, :, :], ps[:, 0:2 * P].rearrange("p (b n) -> p b n", b=2))
        last.then_inc(f.copies, 1)

    def gelu(t, slot):
        w = slot if multi else 0
        act.wait_ge(f.ups, ready(t))
        act.wait_ge(f.downs, free(t))
        for j in range(HID // P):
            last = act.activation(f.hidden[:, slot, j, :], k.ps[2 + 2 * slot + j // 4][:, (j % 4) * P:(j % 4 + 1) * P],
                                  ACT.Gelu, bias=f.b1[:, w, j:j + 1])
        last.then_inc(f.gelus, 1)

    staggered(act, n, [copy, gelu])


def phase_node_ffn(k, rstd, shift):
    nc, a = k.nc, k.ins
    with Phase(k, "ffn0") as ph:
        f = Ffn(ph, 1)
        part = ph.sb("part", [P, 2, C])
        link = ph.sem("link")
        block = ph.block()
        loads = [(f.w1[:, 0], a["L0_gnn_W1"].rearrange("(p b) n -> p b n", b=2)),
                 (f.w2[:, 0], a["L0_gnn_W2"].rearrange("(p j) n -> p j n", p=P)),
                 (f.b1[:, 0, :], a["L0_gnn_b1"].rearrange("(p j) -> p j", p=P)), (f.b2[:, 0, :], wide(a["L0_gnn_b2"])),
                 (f.g[:, 0, :], a["L0_gnn_ln_g"].rearrange("(p b) -> p b", b=2)),
                 (f.b[:, 0, :], a["L0_gnn_ln_b"].rearrange("(p b) -> p b", b=2))]

        @block.sync
        def _(sp):
            for dst, src in loads:
                sp.dma_start(dst, src).then_inc(f.weights_in, 16)
            sp.wait_ge(f.weights_in, 16 * len(loads))

        @block.tensor
        def _(pe):
            pe.wait_ge(f.weights_in, 16 * len(loads))
            ffn_tensor(k, f, pe, TILES, lambda e, t, s: e.wait_ge(f.rows_ready, ready(t)),
                       lambda e, t, s: None, lambda e, t, s: None, False)

        @block.scalar
        def _(act):
            act.wait_ge(f.weights_in, 16 * len(loads))
            ffn_scalar(k, f, act, TILES, lambda e, t, s: None, False, True)

        @block.vector
        def _(dve):
            v = nc.vector
            dve.sem_inc(f.rows_ready, 2)
            dve.sem_inc(f.taken, 2)
            dve.wait_ge(f.weights_in, 16 * len(loads))
            c = Chain(dve, link).loop(TILES, 2)

            def stage(t, slot):
                dve.wait_ge(f.turns, free(t))
                v.tensor_scalar(f.rows[:, slot, :], row(k.h, t, 0, C), rstd[:, bass.ds(t, 1)], shift[:, bass.ds(t, 1)],
                                ALU.mult, ALU.add).then_inc(f.rows_ready, 1)

            def take(t, slot):
                c.at(t)
                c(v.tensor_tensor(part[:, slot, :], row(k.h, t, 0, C), f.b2[:, 0, :], ALU.add))
                dve.wait_ge(f.downs, ready(t))
                c(v.tensor_tensor(part[:, slot, :], part[:, slot, :], k.ps[6 + slot][:, 0:C], ALU.add))
                v.tensor_tensor(row(k.x, t, 0, C), row(k.x, t, 0, C), part[:, slot, :], ALU.add).then_inc(f.taken, 1)

            staggered(dve, TILES, [stage, lambda t, slot: None, take])



class Route:

    def __init__(self, k, ctx, name):
        def sb(n, shape, dt):
            return ctx.enter_context(k.nc.sbuf_tensor(f"{name}_{n}", shape, dt))
        self.top = sb("top", [P, TILES, 2], F32)
        self.which = sb("which", [P, TILES, 2], F32)
        self.share = sb("share", [P, TILES, 2], F32)
        self.place = sb("place", [P, TILES, 2], I32)
        self.expert = sb("expert", [P, 64], I32)


def phase_gate(k, name, r, wg, bg, rstd, shift):
    nc = k.nc

    def stage(ph, t, slot, dst, c):
        for d in (row(k.h, t, 0, C), dst):
            last = nc.vector.tensor_scalar(d, row(k.x, t, 0, C), rstd[:, bass.ds(t, 1)], shift[:, bass.ds(t, 1)],
                                           ALU.mult, ALU.add)
        return last

    def evac(ph, t, slot, ps, c):
        v, lg, mx, ix = nc.vector, ph.buf["lg"], ph.buf["mx"], ph.buf["ix"]
        c(v.tensor_tensor(lg[:, slot, :], ps[0][:, 0:EXPERTS], ph.buf["bg"][:], ALU.add))
        apart(ph, c.eng)
        c(v.max(mx[:, slot, :], lg[:, slot, :]))
        v.tensor_copy(row(r.top, t, 0, 2), mx[:, slot, 0:2])
        c(v.max_index(ix[:, slot, :], mx[:, slot, :], lg[:, slot, :]))
        return v.tensor_copy(row(r.which, t, 0, 2), ix[:, slot, 0:2])

    phase_dense(k, name, 2, [("wg", EXPERTS)], stage, 0, evac, 3,
                sb=[("wg", [P, 2, EXPERTS], F32), ("bg", [P, EXPERTS], F32), ("lg", [P, 2, EXPERTS], F32),
                    ("mx", [P, 2, EXPERTS], F32), ("ix", [P, 2, EXPERTS], U32)],
                loads=[("wg", weights(wg)), ("bg", wide(bg))])


def phase_route(k, name, r, first):
    nc = k.nc
    TE = TILES * EXPERTS
    with Phase(k, name) as ph:
        hot = ph.sb("hot", [P, 2, TILES, EXPERTS])
        both, incl, pos, tmp = (ph.sb(n, [P, TILES, EXPERTS]) for n in ("both", "incl", "pos", "tmp"))
        zero = ph.sb("zero", [P, 2048])
        real = ph.sb("real", [P, TILES])
        e2, r1 = ph.sb("e2", [P, TILES]), ph.sb("r1", [P, TILES])
        count, tiles_f, ends = (ph.sb(n, [P, EXPERTS]) for n in ("count", "tiles_f", "ends"))
        count_i = ph.sb("count_i", [P, EXPERTS], I32)
        placef = ph.sb("placef", [P, TILES, 2])
        of_tile = ph.sb("of_tile", [P, 2, 64])
        link, diff, exped, masked, counted, placed = (ph.sem(s) for s in ("link", "diff", "exped", "masked", "counted", "placed"))
        zeroed, zero_in, scattered = ph.sem("zeroed"), ph.sem("zero_in"), ph.sem("scattered")
        block = ph.block()

        @block.scalar
        def _(act):
            act.wait_ge(diff, 1)
            act.activation(e2[:], r1[:], ACT.Exp).then_inc(exped, 1)

        @block.tensor
        def _(pe):
            pe.wait_ge(masked, 1)
            nc.tensor.matmul(k.ps[0][:, 0:TE], k.before[:], both[:].rearrange("p t e -> p (t e)"), start=True, stop=True)
            nc.tensor.matmul(k.ps[1][:, 0:TE], k.ones[:], both[:].rearrange("p t e -> p (t e)"),
                             start=True, stop=True).then_inc(counted, 1)

        @block.vector
        def _(dve):
            v, c = nc.vector, Chain(dve, link)
            v.memset(zero[:], 0.0).then_inc(zeroed, 1)
            v.tensor_tensor(r1[:], r.top[:, :, 1], r.top[:, :, 0], ALU.subtract).then_inc(diff, 1)
            c(v.memset(real[:], 1.0))
            c(v.tensor_scalar(real[:, TILES - 1:TILES], k.iota_p[:], float(LAST), None, ALU.is_lt))
            for j in range(2):
                c(v.tensor_tensor(hot[:, j], k.iota_row[:, 0:EXPERTS].rearrange("p (a e) -> p a e", a=1).to_broadcast([P, TILES, EXPERTS]),
                                  r.which[:, :, j:j + 1].to_broadcast([P, TILES, EXPERTS]), ALU.is_equal))
            c(v.tensor_tensor(both[:], hot[:, 0], hot[:, 1], ALU.add))
            c(v.tensor_tensor(both[:], both[:], real[:].rearrange("p (t a) -> p t a", a=1).to_broadcast([P, TILES, EXPERTS]), ALU.mult))
            dve.sem_inc(masked, 1)
            dve.wait_ge(exped, 1)
            c(v.tensor_scalar(r1[:], e2[:], 1.0, None, ALU.add))
            c(v.reciprocal(r1[:], r1[:]))
            v.tensor_copy(r.share[:, :, 0], r1[:])
            v.tensor_tensor(r.share[:, :, 1], r1[:], e2[:], ALU.mult)
            dve.wait_ge(counted, 1)
            total = k.ps[1][:, 0:TE].rearrange("p (t e) -> p t e", e=EXPERTS)
            inner = k.ps[0][:, 0:TE].rearrange("p (t e) -> p t e", e=EXPERTS)
            dve.wait_ge(zeroed, 1)
            for e in range(EXPERTS):
                c.mark(v.tensor_tensor_scan(incl[:, :, e], total[:, :, e], zero[:, 0:TILES], 0.0, ALU.add, ALU.add))
            c.wait()
            c(v.tensor_tensor(pos[:], incl[:], total, ALU.subtract))
            c(v.tensor_tensor(pos[:], pos[:], inner, ALU.add))
            c(v.tensor_scalar(count[:], incl[:, TILES - 1, :], float(P - 1), None, ALU.add))
            c(v.tensor_copy(count_i[:], count[:]))
            c(v.tensor_scalar(count_i[:], count_i[:], 7, None, ALU.arith_shift_right))
            c(v.tensor_copy(tiles_f[:], count_i[:]))
            c(v.tensor_tensor_scan(ends[:], tiles_f[:], zero[:, 0:EXPERTS], 0.0, ALU.add, ALU.add))
            c(v.tensor_tensor(count[:], ends[:], tiles_f[:], ALU.subtract))
            c(v.tensor_scalar(count[:], count[:], float(P), None, ALU.mult))
            c(v.tensor_tensor(pos[:], pos[:], count[:].rearrange("p (a e) -> p a e", a=1).to_broadcast([P, TILES, EXPERTS]), ALU.add))
            for j in range(2):
                c(v.tensor_tensor(tmp[:], pos[:], hot[:, j], ALU.mult))
                c(v.tensor_reduce(placef[:, :, j], tmp[:], AX.X, ALU.add))
            c(v.tensor_copy(r.place[:], placef[:]))
            dve.sem_inc(placed, 1)
            c(v.tensor_scalar(of_tile[:, 0, :], k.iota_row[:, 0:64], ends[:, 0:1], None, ALU.is_ge))
            for e in range(1, EXPERTS - 1):
                c(v.scalar_tensor_tensor(of_tile[:, e % 2, :], k.iota_row[:, 0:64], ends[:, e:e + 1], of_tile[:, (e - 1) % 2, :],
                                         ALU.is_ge, ALU.add))
            v.tensor_copy(r.expert[:], of_tile[:, (EXPERTS - 2) % 2, :])

        @block.sync
        def _(sp):
            if first:
                sp.wait_ge(zeroed, 1)
                per = 2048 // C
                for j in range(SLOTS_X // per):
                    sp.dma_start(k.routed_in[j * P * per:(j + 1) * P * per, :].rearrange("(p r) c -> p (r c)", p=P),
                                 zero[:]).then_inc(zero_in, 16)
                sp.wait_ge(zero_in, 16 * (SLOTS_X // per))

        @block.gpsimd
        def _(pool):
            pool.wait_ge(placed, 1)
            if first:
                pool.wait_ge(zero_in, 16 * (SLOTS_X * C // 2048))
            for t in range(TILES):
                m = P if t < TILES - 1 else LAST
                for j in range(2):
                    nc.gpsimd.indirect_dma_start(k.routed_in, bass.IndirectOffsetOnAxis(ap=r.place[0:m, t, j:j + 1], axis=0),
                                                 k.h[0:m, t, 0:C], None).then_inc(scattered, 16)
            pool.wait_ge(scattered, 16 * 2 * TILES)


def phase_experts(k, name, r, prefix, norm):
    nc, a = k.nc, k.ins
    w = {n: a[f"{prefix}_{n}"] for n in ("W1", "b1", "W2", "b2")}
    if norm:
        w |= {n: a[f"{prefix}_{n}"] for n in ("ln_g", "ln_b")}
    with Phase(k, name) as ph:
        f = Ffn(ph, 2)
        result = ph.sb("result", [P, 2, C])
        stored, drained = ph.sem("stored"), ph.sem("drained")
        block = ph.block()
        up_dmas = 4 if norm else 2

        def rows_there(e, t, slot):
            e.wait_ge(f.rows_in[slot], (t // 2 + 1) * 16)

        def up_there(e, t, slot):
            e.wait_ge(f.up_in[slot], (t // 2 + 1) * (16 * up_dmas))

        def down_there(e, t, slot):
            e.wait_ge(f.down_in[slot], (t // 2 + 1) * 32)

        @block.sync
        def _(sp):
            def expert(t):
                return sp.value_load(r.expert[0:1, bass.ds(t, 1)], min_val=0, max_val=EXPERTS - 1)

            def load_rows(t, slot):
                sp.wait_ge(f.turns, free(t))
                sp.dma_start(f.rows[:, slot, :], k.routed_in[bass.ds(t * P, P), :]).then_inc(f.rows_in[slot], 16)

            def load_up(t, slot):
                n, s = expert(t), f.up_in[slot]
                sp.wait_ge(f.gelus, free(t))
                sp.dma_start(f.w1[:, slot], w["W1"][bass.ds(n, 1)].rearrange("a (p b) n -> p (a b) n", b=2)).then_inc(s, 16)
                sp.dma_start(f.b1[:, slot, :], w["b1"][bass.ds(n, 1)].rearrange("a (p j) -> p (a j)", p=P)).then_inc(s, 16)
                if norm:
                    for tile, n_ in ((f.g, "ln_g"), (f.b, "ln_b")):
                        sp.dma_start(tile[:, slot, :], w[n_][bass.ds(n, 1)].rearrange("a (p b) -> p (a b)", b=2)).then_inc(s, 16)

            def load_down(t, slot):
                n, s = expert(t), f.down_in[slot]
                sp.wait_ge(f.taken, free(t))
                sp.dma_start(f.w2[:, slot], w["W2"][bass.ds(n, 1)].rearrange("a (p j) n -> p (a j) n", p=P)).then_inc(s, 16)
                sp.dma_start(f.b2[:, slot, :], w["b2"][bass.ds(n, 1)].to_broadcast([P, C])).then_inc(s, 16)

            staggered(sp, SLOTS_X, [load_rows, load_up, load_down])

        @block.tensor
        def _(pe):
            ffn_tensor(k, f, pe, SLOTS_X, rows_there, up_there, down_there, True)

        @block.scalar
        def _(act):
            ffn_scalar(k, f, act, SLOTS_X, up_there, True, norm)

        @block.vector
        def _(dve):
            dve.sem_inc(f.taken, 2)

            def take(t, slot):
                down_there(dve, t, slot)
                dve.wait_ge(f.downs, ready(t))
                dve.wait_ge(drained, free(t))
                nc.vector.tensor_tensor(result[:, slot, :], k.ps[6 + slot][:, 0:C], f.b2[:, slot, :], ALU.add).then_inc(f.taken, 1)
            sweep(dve, SLOTS_X, take)

        @block.gpsimd
        def _(pool):
            pool.sem_inc(drained, 2)

            def store(t, slot):
                pool.wait_ge(f.taken, ready(t))
                pool.dma_start(k.routed_out[bass.ds(t * P, P), :], result[:, slot, :]).then_inc(stored, 16)
                pool.wait_ge(stored, (t + 1) * 16)
                pool.sem_inc(drained, 1)
            sweep(pool, SLOTS_X, store)


def phase_combine(k, name, r):
    nc = k.nc
    RING = 8
    with Phase(k, name) as ph:
        got = ph.sb("got", [P, RING, C])
        gathered = [ph.sem(f"gathered{i}") for i in range(RING)]
        added = ph.sem("added")
        block = ph.block()
        steps = [(t, j) for t in range(TILES) for j in range(2)]

        @block.gpsimd
        def _(pool):
            for i, (t, j) in enumerate(steps):
                m = P if t < TILES - 1 else LAST
                if i >= RING:
                    pool.wait_ge(added, i - RING + 1)
                nc.gpsimd.indirect_dma_start(got[0:m, i % RING, :], None, k.routed_out,
                                             bass.IndirectOffsetOnAxis(ap=r.place[0:m, t, j:j + 1], axis=0)
                                             ).then_inc(gathered[i % RING], 16)

        @block.vector
        def _(dve):
            for i, (t, j) in enumerate(steps):
                m = P if t < TILES - 1 else LAST
                dve.wait_ge(gathered[i % RING], 16 * (i // RING + 1))
                if i:
                    dve.wait_ge(added, i)
                nc.vector.scalar_tensor_tensor(k.x[0:m, t, :], got[0:m, i % RING, :], r.share[0:m, t, j:j + 1], k.x[0:m, t, :],
                                               ALU.mult, ALU.add).then_inc(added, 1)


def routed_layer(k, name, prefix, wg, bg, norm, first, rstd, shift):
    with ExitStack() as ctx:
        r = Route(k, ctx, name)
        phase_norm(k, name + "_norm", k.x, 1e-5, rstd, shift)
        phase_gate(k, name + "_gate", r, wg, bg, rstd, shift)
        phase_route(k, name + "_route", r, first)
        phase_experts(k, name + "_experts", r, prefix, norm)
        phase_combine(k, name + "_combine", r)



class Spans:

    def __init__(self, k, ctx):
        def sb(n, shape):
            return ctx.enter_context(k.nc.sbuf_tensor(f"span_{n}", shape, BF16))
        self.prev = sb("prev", [P, BLK, P])
        self.next = sb("next", [P, BLK, P])
        self.head = sb("head", [P, BLK, P])
        self.tail = sb("tail", [P, BLK, P])
        self.in_item = sb("in_item", [P, BLK, P])
        self.carry = sb("carry", [4, SUBP + 1])
        self.down = sb("down", [4, SUBP])
        self.up = sb("up", [4, SUBP])


def phase_spans(k, s):
    nc = k.nc
    with Phase(k, "spans") as ph:
        key, off = ph.sb("key", [P, BLK, P]), ph.sb("off", [P, BLK, P])
        first_next = ph.sb("first_next", [P, BLK])
        first, last_ = ph.sb("first", [4, SUBP + 1]), ph.sb("last", [4, SUBP + 1])
        same, low = ph.sb("same", [P, BLK, P]), ph.sb("low", [P, BLK, P])
        loaded, link, flagged, turned = ph.sem("loaded"), ph.sem("link"), ph.sem("flagged"), ph.sem("turned")
        block = ph.block()

        @block.sync
        def _(sp):
            with nc.allow_non_contiguous_dma(reason="one key of each edge tile"):
                sp.dma_start(key[:], k.key_rows[0:SUBP, :].rearrange("(b p) e -> p b e", p=P)).then_inc(loaded, 16)
                sp.dma_start(off[:], k.off_rows.rearrange("(b p) e -> p b e", p=P)).then_inc(loaded, 16)
                for b in range(BLK):
                    sp.dma_start(first_next[:, b:b + 1], k.key_rows[b * P + 1:(b + 1) * P + 1, 0:1]).then_inc(loaded, 16)
                for tile, col in ((first, 0), (last_, P - 1)):
                    for h in range(4):
                        sp.dma_start(tile[h:h + 1, :], k.key_rows[:, col:col + 1].rearrange("r o -> o r")).then_inc(loaded, 16)
            sp.wait_ge(loaded, 16 * (2 + BLK + 8))

        @block.vector
        def _(dve):
            v, c = nc.vector, Chain(dve, link)
            dve.wait_ge(loaded, 16 * (2 + BLK + 8))

            def penalty(dst, flag):
                c(v.tensor_scalar(dst, flag, 1.0, BIG, ALU.subtract, ALU.mult))

            c(v.memset(same[:, :, 0:1], 0.0))
            c(v.tensor_tensor(same[:, :, 1:P], key[:, :, 1:P], key[:, :, 0:P - 1], ALU.is_equal))
            penalty(s.prev[:], same[:])
            c(v.tensor_tensor(same[:, :, 0:P - 1], key[:, :, 1:P], key[:, :, 0:P - 1], ALU.is_equal))
            c(v.memset(same[:, :, P - 1:P], 0.0))
            penalty(s.next[:], same[:])
            c(v.tensor_tensor(same[:, :, P - 1], key[:, :, P - 1], first_next[:], ALU.is_equal))
            c(v.tensor_scalar(same[:], same[:], -1.0, 1.0, ALU.mult, ALU.add))
            c(v.tensor_scalar(low[:], off[:], 0.0, None, ALU.is_ge))
            c(v.tensor_scalar(off[:], off[:], float(P), None, ALU.is_lt))
            c(v.tensor_tensor(low[:], low[:], off[:], ALU.mult))
            penalty(s.in_item[:], low[:])
            c(v.tensor_tensor(same[:], same[:], low[:], ALU.mult))
            dve.sem_inc(flagged, 1)
            for b in range(BLK):
                c(v.tensor_scalar(off[:, b, :], key[:, b, :], key[:, b, 0:1], None, ALU.is_equal))
                c(v.tensor_scalar(low[:, b, :], key[:, b, :], key[:, b, P - 1:P], None, ALU.is_equal))
            penalty(s.head[:], off[:])
            penalty(s.tail[:], low[:])
            c(v.tensor_tensor(s.carry[:, 1:SUBP + 1], first[:, 1:SUBP + 1], last_[:, 0:SUBP], ALU.is_equal))
            c(v.memset(s.carry[:, 0:1], 0.0))
            c(v.memset(s.carry[:, SUBP:SUBP + 1], 0.0))
            penalty(s.carry[:], s.carry[:])
            c(v.tensor_tensor(first[:], first[:], last_[:], ALU.is_equal))
            penalty(first[:], first[:])
            c(v.tensor_tensor(s.down[:], s.carry[:, 0:SUBP], first[:, 0:SUBP], ALU.add))
            c(v.tensor_tensor(s.up[:], s.carry[:, 1:SUBP + 1], first[:, 0:SUBP], ALU.add))
            dve.wait_ge(turned, 1)
            v.tensor_copy(k.is_last[:], k.ps[0][:, 0:SUBP])

        @block.tensor
        def _(pe):
            pe.wait_ge(flagged, 1)
            for b in range(BLK):
                mm = nc.tensor.transpose(k.ps[0][:, b * P:(b + 1) * P], same[:, b, :], k.ident[:])
            mm.then_inc(turned, 1)


class Gat:

    def __init__(self, buf, n, heads, width, table):
        self.n, self.H, self.D, self.table = n, heads, width, table
        self.W = heads * (width + 1)
        self.of_node = buf["of_node"][:, 0:2 * heads, :]
        self.of_src = buf["of_src"][:, 0:heads, :]
        self.of_dst = buf["shared"][:, 0:2 * heads * SUBP].rearrange("p (h e) -> p h e", e=SUBP)
        self.rows = buf["shared"][:, 0:8 * self.W].rearrange("p (r s w) -> p r s w", s=2, w=self.W)
        self.last_max = buf["last_max"][:, :, 0:heads + 1]
        self.own = buf["own"][:, 0:heads, :]
        self.inv = buf["inv"][:, 0:heads, :]

    @staticmethod
    def buffers(k, ctx, heads):
        shapes = {"of_node": [P, 2 * heads, TILES], "of_src": [P, heads, SUBP], "shared": [P, max(2 * heads * SUBP, 8 * ACCW)],
                  "last_max": [P, SUBS, heads + 1], "own": [P, heads, TILES], "inv": [P, heads, TILES]}
        return {n: ctx.enter_context(k.nc.sbuf_tensor(f"gat_{n}", s, F32)) for n, s in shapes.items()}


def phase_gat_dense(k, g, kb, w, a_src, a_dst, stage, per_stage, sb, loads):
    nc = k.nc
    H, D = g.H, g.D
    with ExitStack() as ctx:
        wt = ctx.enter_context(nc.sbuf_tensor(f"gat{g.n}_w", [P, kb, H * D], F32))
        wa = ctx.enter_context(nc.sbuf_tensor(f"gat{g.n}_wa", [P, kb, 2 * H], F32))
        with Phase(k, f"gat{g.n}_wa") as ph:
            av = ph.sb("av", [P, 2, H * D])
            prod = ph.sb("prod", [P, H * D])
            loaded, link = ph.sem("loaded"), ph.sem("link")
            block = ph.block()

            @block.sync
            def _(sp):
                sp.dma_start(wt[:], weights(w)).then_inc(loaded, 16)
                for i, vec in enumerate((a_src, a_dst)):
                    sp.dma_start(av[:, i, :], wide(vec.rearrange("h d -> (h d)"))).then_inc(loaded, 16)
                sp.wait_ge(loaded, 48)

            @block.vector
            def _(dve):
                v, c = nc.vector, Chain(dve, link)
                dve.wait_ge(loaded, 48)
                for b in range(kb):
                    for i in range(2):
                        c(v.tensor_tensor(prod[:], wt[:, b, :], av[:, i, :], ALU.mult))
                        c(v.tensor_reduce(wa[:, b, i * H:(i + 1) * H], prod[:].rearrange("p (h d) -> p h d", d=D), AX.X, ALU.add))

        def evac(ph, t, slot, ps, c):
            v = nc.vector
            apart(ph, c.eng)
            node = k.h[:, bass.ds(t, 1), 0:g.W].rearrange("p a (h d) -> p (a h) d", d=D + 1)
            v.tensor_copy(node[:, :, 0:D], ps[0][:, 0:H * D].rearrange("p (h d) -> p h d", d=D))
            v.tensor_copy(node[:, :, D], k.ones[:, 0:H])
            return v.tensor_copy(g.of_node[:, :, bass.ds(t, 1)].rearrange("p h a -> p (h a)"), ps[1][:, 0:2 * H])

        phase_dense(k, f"gat{g.n}", kb, [(wt, H * D), (wa, 2 * H)], stage, per_stage, evac, 0, sb=sb, loads=loads,
                    exps="neg" if per_stage else None,
                    stores=tile_stores(g.table, k.h, g.W))


def phase_gat_scores(k, g):
    nc, H = k.nc, g.H
    RING = 8
    HT = H * TILES
    with Phase(k, f"gat{g.n}_scores") as ph:
        rows = ph.sb("rows", [P, 2, 2, 4 * 256], BF16)
        hot = ph.sb("hot", [P, 4, 2, 256], BF16)
        parts = ph.sb("parts", [P, 3, 2 * HT], BF16)
        rest = ph.sb("rest", [P, 2 * HT])
        tile_hot = ph.sb("tile_hot", [P, 2, TILES])
        picked = ph.sb("picked", [P, 2, H, TILES])
        row_in = [ph.sem(f"row_in{s}") for s in range(2)]
        hots, made, taken, dst_taken, cut, link = (ph.sem(s) for s in ("hots", "made", "taken", "dst_taken", "cut", "link"))
        block = ph.block()
        bank, dst_bank = k.ps[0:4], k.ps[4:8]

        @block.sync
        def _(sp):
            load_batches(sp, hots, 4, [(k.src_rows, rows[:, 0]), (k.dst_rows, rows[:, 1])], row_in)

        @block.tensor
        def _(pe):
            pe.sem_inc(made, 4)
            pe.wait_ge(cut, 1)

            def products(t, r, i):
                slot = r % 4
                n = pe.value_load(k.item_tile[0:1, bass.ds(t, 1)], min_val=0, max_val=TILES - 1)
                pe.wait_ge(hots, ready(t, 4))
                pe.wait_ge(taken, free(t))
                pe.wait_ge(dst_taken, free(t))
                for s in range(2):
                    for p in range(3):
                        nc.tensor.matmul(bank[slot][:, s * HT:(s + 1) * HT], hot[:, slot, 0, s * P:(s + 1) * P],
                                         parts[:, p, 0:HT], start=(p == 0), stop=(p == 2))
                for s in range(2):
                    for p in range(3):
                        mm = nc.tensor.matmul(dst_bank[slot][:, s * 2 * H:(s + 1) * 2 * H],
                                              hot[:, slot, 1, s * P:(s + 1) * P],
                                              parts[:, p, :].rearrange("p (h t) -> p h t", t=TILES)[:, :, bass.ds(n, 1)]
                                              .rearrange("p h a -> p (h a)"), start=(p == 0), stop=(p == 2))
                mm.then_inc(made, 1)
            ringed(pe, ITEMS, RING, [products])

        @block.scalar
        def _(act):
            act.sem_inc(dst_taken, 4)

            def take(t, r, i):
                act.wait_ge(made, ready(t, 4))
                act.copy(g.of_dst[:, :, bass.ds(2 * t, 2)],
                         dst_bank[r % 4][:, 0:4 * H].rearrange("p (s h) -> p h s", s=2)).then_inc(dst_taken, 1)
            ringed(act, ITEMS, RING, [take])

        @block.vector
        def _(dve):
            v, c = nc.vector, Chain(dve, link)
            dve.sem_inc(hots, 4)
            dve.sem_inc(taken, 4)
            v.memset(g.of_src[:, :, SUBS:SUBP], 0.0)
            v.memset(g.of_dst[:, :, SUBS:SUBP], 0.0)
            flat = g.of_node.rearrange("p h t -> p (h t)")
            c(v.tensor_copy(parts[:, 0, :], flat))
            c(v.tensor_tensor(rest[:], flat, parts[:, 0, :], ALU.subtract))
            c(v.tensor_copy(parts[:, 1, :], rest[:]))
            c(v.tensor_tensor(rest[:], rest[:], parts[:, 1, :], ALU.subtract))
            v.tensor_copy(parts[:, 2, :], rest[:]).then_inc(cut, 1)
            c.loop(ITEMS, 2)

            def one_hots(t, r, i):
                dve.wait_ge(row_in[r // 4], (i + 1) * 32)
                dve.wait_ge(made, free(t))
                v.tensor_scalar(hot[:, r % 4, :, :], rows[:, :, r // 4, r % 4 * 256:(r % 4 + 1) * 256], k.iota_p[:, 0:1], None,
                                ALU.is_equal).then_inc(hots, 1)

            def pick(t, r, i):
                c.at(t)
                dve.wait_ge(taken, t + 4)
                c(v.tensor_tensor(tile_hot[:], k.iota_row[:, 0:TILES].rearrange("p (a n) -> p a n", a=1).to_broadcast([P, 2, TILES]),
                                  k.src_hi[:, bass.ds(2 * t, 2)].rearrange("p (s a) -> p s a", a=1).to_broadcast([P, 2, TILES]),
                                  ALU.is_equal))
                dve.wait_ge(made, ready(t, 4))
                c(v.tensor_tensor(picked[:], bank[r % 4][:, 0:2 * HT].rearrange("p (s h n) -> p s h n", s=2, h=H),
                                  tile_hot[:].rearrange("p s (a n) -> p s a n", a=1).to_broadcast([P, 2, H, TILES]), ALU.mult))
                v.tensor_reduce(g.of_src[:, :, bass.ds(2 * t, 2)].rearrange("p h s -> p s h"), picked[:], AX.X, ALU.add
                                ).then_inc(taken, 1)
                c.full()

            ringed(dve, ITEMS, RING, [one_hots, None, pick])


def phase_gat_softmax(k, g, s):
    nc, H = k.nc, g.H
    with Phase(k, f"gat{g.n}_softmax") as ph:
        run, back = ph.sb("run", [P, H, BLK, P]), ph.sb("back", [P, H, BLK, P])
        ends, into = ph.sb("ends", [4, SUBP]), ph.sb("into", [4, SUBP])
        cin = ph.sb("cin", [P, BLK, H])
        turned, masked, scanned, ends_in, carried, cins, passed, back_out, taken, shifted, exped, link = (
            ph.sem(n) for n in ("turned", "masked", "scanned", "ends_in", "carried", "cins", "passed", "back_out", "taken",
                                "shifted", "exped", "link"))
        z = back[:].rearrange("p h b e -> p h (b e)")
        block = ph.block()

        @block.tensor
        def _(pe):
            for h in range(H):
                for b in range(BLK):
                    mm = nc.tensor.transpose(k.ps[h][:, b * P:(b + 1) * P], g.of_src[:, h, b * P:(b + 1) * P], k.ident[:])
                mm.then_inc(turned, 1)
            for way, (data, col) in enumerate(((run, P - 1), (back, 0))):
                pe.wait_ge(scanned, way + 1)
                for b in range(BLK):
                    mm = nc.tensor.transpose(k.ps[4][0:H, b * P:(b + 1) * P], data[:, :, b, col], k.ident[:])
                mm.then_inc(ends_in, 1)
                pe.wait_ge(carried, way + 1)
                for b in range(BLK):
                    mm = nc.tensor.transpose(k.ps[5][:, b * H:(b + 1) * H], into[0:H, b * P:(b + 1) * P], k.ident[0:H, 0:H])
                mm.then_inc(cins, 1)
            pe.wait_ge(passed, 1)
            for h in range(H):
                for b in range(BLK):
                    mm = nc.tensor.transpose(k.ps[h][:, b * P:(b + 1) * P], back[:, h, b, :], k.ident[:])
                mm.then_inc(back_out, 1)

        @block.scalar
        def _(act):
            act.wait_ge(shifted, 1)
            act.activation(g.of_src[:], z, ACT.Exp).then_inc(exped, 1)

        @block.vector
        def _(dve):
            v, c = nc.vector, Chain(dve, link)

            def flat(a):
                return a.rearrange("p b e -> p (b e)")

            for h in range(H):
                dve.wait_ge(turned, h + 1)
                c(v.tensor_tensor(flat(back[:, h]), k.ps[h][:, 0:SUBP], flat(s.in_item[:]), ALU.add))
                c.mark(v.tensor_tensor_scan(flat(run[:, h]), flat(s.prev[:]), flat(back[:, h]), -BIG, ALU.add, ALU.max))
            c.wait()
            dve.sem_inc(scanned, 1)
            dve.wait_ge(ends_in, 1)
            c(v.tensor_tensor_scan(ends[0:H, :], s.down[0:H, :], k.ps[4][0:H, 0:SUBP], -BIG, ALU.add, ALU.max))
            c.mark(v.memset(into[0:H, 0:1], -BIG))
            c(v.tensor_tensor(into[0:H, 1:SUBP], ends[0:H, 0:SUBP - 1], s.carry[0:H, 1:SUBP], ALU.add))
            dve.sem_inc(carried, 1)
            dve.wait_ge(cins, 1)
            c(v.tensor_copy(cin[:], k.ps[5][:, 0:BLK * H].rearrange("p (b h) -> p b h", h=H)))
            for h in range(H):
                for b in range(BLK):
                    c.mark(v.scalar_tensor_tensor(run[:, h, b, :], s.head[:, b, :], cin[:, b, h:h + 1], run[:, h, b, :],
                                                  ALU.add, ALU.max))
            c.wait()
            for h in range(H):
                c.mark(v.tensor_tensor_scan(flat(back[:, h])[:, ::-1], flat(s.next[:])[:, ::-1], flat(run[:, h])[:, ::-1], -BIG,
                                            ALU.add, ALU.max))
            c.wait()
            dve.sem_inc(scanned, 1)
            dve.wait_ge(ends_in, 2)
            c(v.tensor_tensor_scan(ends[0:H, ::-1], s.up[0:H, ::-1], k.ps[4][0:H, 0:SUBP][:, ::-1], -BIG, ALU.add, ALU.max))
            c.mark(v.memset(into[0:H, SUBP - 1:SUBP], -BIG))
            c(v.tensor_tensor(into[0:H, 0:SUBP - 1], ends[0:H, 1:SUBP], s.carry[0:H, 1:SUBP], ALU.add))
            dve.sem_inc(carried, 1)
            dve.wait_ge(cins, 2)
            c(v.tensor_copy(cin[:], k.ps[5][:, 0:BLK * H].rearrange("p (b h) -> p b h", h=H)))
            for h in range(H):
                for b in range(BLK):
                    c.mark(v.scalar_tensor_tensor(back[:, h, b, :], s.tail[:, b, :], cin[:, b, h:h + 1], back[:, h, b, :],
                                                  ALU.add, ALU.max))
            c.wait()
            dve.sem_inc(passed, 1)
            top, al_s, al_d = run[:].rearrange("p h b e -> p h (b e)"), g.of_dst[:, 0:H, :], g.of_dst[:, H:2 * H, :]
            for h in range(H):
                dve.wait_ge(back_out, h + 1)
                c(v.tensor_tensor(top[:, h, :], k.ps[h][:, 0:SUBP], al_s[:, h, :], ALU.max))
                c(v.tensor_tensor(g.last_max[:, :, h], top[:, h, 0:SUBS], k.is_last[:, 0:SUBS], ALU.mult))
            c(v.tensor_copy(g.last_max[:, :, H], k.is_last[:, 0:SUBS]))
            c(v.tensor_tensor(top, top, al_d, ALU.add))
            c(v.scalar_tensor_tensor(top, top, 0.2, top, ALU.mult, ALU.max))
            c(v.tensor_tensor(z, g.of_src[:], al_d, ALU.add))
            c(v.scalar_tensor_tensor(z, z, 0.2, z, ALU.mult, ALU.max))
            c(v.tensor_tensor(z, z, top, ALU.subtract))
            v.tensor_scalar(z, z, 0.0, None, ALU.min).then_inc(shifted, 1)


def phase_gat_edges(k, g):
    nc, H, D = k.nc, g.H, g.D
    RING = 4
    by_act = H * 3 // 4
    lo_heads = max(1, H // 2)
    A = lo_heads * (D + 1)
    B = g.W - A + H + 1
    with Phase(k, f"gat{g.n}_edges") as ph:
        rows = g.rows
        index = ph.sb("index", [P, RING, 2], I32)
        hot = ph.sb("hot", [P, RING, 2, H + 1, P])
        cleared, indexed = ph.sem("cleared"), ph.sem("indexed")
        gathered = [ph.sem(f"gathered{r}") for r in range(RING)]
        bare, weighed, scaled, summed, added = (ph.sem(n) for n in ("bare", "weighed", "scaled", "summed", "added"))
        psa, psb = k.ps[0:RING], k.ps[RING:2 * RING]
        block = ph.block()

        @block.gpsimd
        def _(pool):
            with pool.Fori(0, ITEMS // RING) as i:
                for r in range(RING):
                    pool.wait_ge(indexed, i * RING + r + 1)
                    apart(ph, pool)
                    for s in range(2):
                        nc.gpsimd.indirect_dma_start(rows[:, r, s, :], None, g.table,
                                                     bass.IndirectOffsetOnAxis(ap=index[:, r, s:s + 1], axis=0)
                                                     ).then_inc(gathered[r], 16)

        @block.scalar
        def _(act):
            act.sem_inc(scaled, RING)

            def scale(t, slot, i):
                act.wait_ge(bare, ready(t, RING))
                act.wait_ge(summed, free(t))
                for s in range(2):
                    for h in range(H - by_act, H):
                        last = act.mul(hot[:, slot, s, h, :], hot[:, slot, s, H, :],
                                       g.of_src[:, h, bass.ds(2 * t + s, 1)])
                last.then_inc(scaled, 1)
            if by_act:
                ringed(act, ITEMS, RING, [scale])

        @block.tensor
        def _(pe):
            pe.sem_inc(summed, RING)

            def sums(t, slot, i):
                pe.wait_ge(gathered[slot], (i + 1) * 32)
                pe.wait_ge(weighed, ready(t, RING))
                if by_act:
                    pe.wait_ge(scaled, ready(t, RING))
                pe.wait_ge(added, free(t))
                for h in range(H):
                    out = psa[slot][:, h * (D + 1):(h + 1) * (D + 1)] if h < lo_heads else \
                        psb[slot][:, (h - lo_heads) * (D + 1):(h - lo_heads + 1) * (D + 1)]
                    for s in range(2):
                        nc.tensor.matmul(out, hot[:, slot, s, h, :], rows[:, slot, s, h * (D + 1):(h + 1) * (D + 1)],
                                         start=(s == 0), stop=(s == 1))
                for s in range(2):
                    mm = nc.tensor.matmul(psb[slot][:, B - H - 1:B], hot[:, slot, s, H, :],
                                          g.last_max[:, bass.ds(2 * t + s, 1), :].rearrange("p a h -> p (a h)"),
                                          start=(s == 0), stop=(s == 1))
                mm.then_inc(summed, 1)

            ringed(pe, ITEMS, RING, [sums])

        @block.vector
        def _(dve):
            v = nc.vector
            v.memset(k.acc[:, :, 0:g.W + H + 1], 0.0).then_inc(cleared, 1)
            for n in (bare, weighed, added):
                dve.sem_inc(n, RING)
            dve.wait_ge(cleared, 1)

            def stage_index(t, r):
                v.tensor_copy(index[:, r, :], k.src_of[:, bass.ds(2 * t, 2)]).then_inc(indexed, 1)

            def one_hots(t, slot, i):
                dve.wait_ge(summed, free(t))
                dve.wait_ge(scaled, free(t)) if by_act else None
                for s in range(2):
                    last = v.tensor_scalar(hot[:, slot, s, H, :], k.iota_row[:, 0:P], k.dst_in[:, bass.ds(2 * t + s, 1)],
                                           None, ALU.is_equal)
                last.then_inc(bare, 1)
                for s in range(2):
                    for h in range(H - by_act):
                        last = v.tensor_scalar(hot[:, slot, s, h, :], k.iota_row[:, 0:P], k.dst_in[:, bass.ds(2 * t + s, 1)],
                                               g.of_src[:, h, bass.ds(2 * t + s, 1)], ALU.is_equal, ALU.mult)
                last.then_inc(weighed, 1)

            def add(t, slot, i):
                n = dve.value_load(k.item_tile[0:1, bass.ds(t, 1)], min_val=0, max_val=TILES - 1)
                dve.wait_ge(summed, ready(t, RING))
                stage_index(t + RING, slot)
                dve.wait_ge(added, t + RING)
                v.tensor_tensor(row(k.acc, n, 0, A), row(k.acc, n, 0, A), psa[slot][:, 0:A], ALU.add)
                v.tensor_tensor(row(k.acc, n, A, A + B), row(k.acc, n, A, A + B), psb[slot][:, 0:B], ALU.add
                                ).then_inc(added, 1)

            for r in range(RING):
                stage_index(r, r)
            ringed(dve, ITEMS, RING, [one_hots, None, add])


def phase_gat_nodes(k, g):
    nc, H, D = k.nc, g.H, g.D
    with Phase(k, f"gat{g.n}_nodes") as ph:
        alone = ph.sb("alone", [P, 1, TILES])
        top, e = (ph.sb(n, [P, 4, TILES])[:, 0:H, :] for n in ("top", "e"))
        link, shifted, exped = ph.sem("link"), ph.sem("shifted"), ph.sem("exped")
        block = ph.block()

        @block.scalar
        def _(act):
            act.wait_ge(shifted, 1)
            act.activation(g.own[:], e, ACT.Exp).then_inc(exped, 1)

        @block.vector
        def _(dve):
            v, c = nc.vector, Chain(dve, link)
            acc = k.acc[:].rearrange("p t w -> p w t")
            al_s, al_d = g.of_node[:, 0:H, :], g.of_node[:, H:2 * H, :]
            c(v.tensor_scalar(alone[:], acc[:, g.W + H:g.W + H + 1, :], -1.0, 1.0, ALU.mult, ALU.add))
            c(v.tensor_tensor(top, al_s, alone[:].to_broadcast([P, H, TILES]), ALU.mult))
            c(v.tensor_tensor(top, top, acc[:, g.W:g.W + H, :], ALU.add))
            c(v.tensor_tensor(top, top, al_s, ALU.max))
            c(v.tensor_tensor(top, top, al_d, ALU.add))
            c(v.scalar_tensor_tensor(top, top, 0.2, top, ALU.mult, ALU.max))
            c(v.tensor_tensor(e, al_s, al_d, ALU.add))
            c(v.scalar_tensor_tensor(e, e, 0.2, e, ALU.mult, ALU.max))
            c(v.tensor_tensor(e, e, top, ALU.subtract))
            v.tensor_scalar(e, e, 0.0, None, ALU.min).then_inc(shifted, 1)
            dve.wait_ge(exped, 1)
            c(v.tensor_tensor(top, g.own[:], acc[:, D:g.W:D + 1, :], ALU.add))
            c(v.tensor_scalar(top, top, 1e-16, None, ALU.add))
            v.reciprocal(g.inv[:], top)


def stage_attended(k, g, elu):
    nc, H, D = k.nc, g.H, g.D

    def stage(ph, t, slot, dst, c):
        v, part = nc.vector, ph.buf["part"]
        out = part[:, slot, :] if elu else dst
        for h in range(H):
            a, b = h * (D + 1), h * (D + 1) + D
            c.mark(v.scalar_tensor_tensor(part[:, slot, h * D:(h + 1) * D], row(k.h, t, a, b), g.own[:, h, bass.ds(t, 1)],
                                          row(k.acc, t, a, b), ALU.mult, ALU.add))
        c.wait()
        for h in range(H):
            last = v.scalar_tensor_tensor(out[:, h * D:(h + 1) * D], part[:, slot, h * D:(h + 1) * D], g.inv[:, h, bass.ds(t, 1)],
                                          ph.buf["bias"][:, h * D:(h + 1) * D], ALU.mult, ALU.add)
            if elu:
                c.mark(last)
        if not elu:
            return last
        c.wait()
        neg = ph.buf["neg"]
        v.tensor_scalar(neg[:, slot, :], out, 0.0, None, ALU.min).then_inc(ph.capped, 1)
        c(v.tensor_scalar(out, out, 0.0, -1.0, ALU.max, ALU.add))
        c.eng.wait_ge(ph.exped, t + 1)
        return v.tensor_tensor(dst, out, neg[:, slot, :], ALU.add)
    return stage


def phase_mlp(k, g):
    nc, a = k.nc, k.ins
    HIDDEN2 = a["L1_gnn_M2"].shape[1]

    def relu_to_h(width):
        def evac(ph, t, slot, ps, c):
            tmp = ph.buf["tmp"]
            c(nc.vector.tensor_tensor(tmp[:, slot, :], ps[0][:, 0:width], ph.buf["mb"][:], ALU.add))
            return nc.vector.tensor_scalar(row(k.h, t, 0, width), tmp[:, slot, :], 0.0, None, ALU.max)
        return evac

    def stage_h(width):
        def stage(ph, t, slot, dst, c):
            return nc.vector.tensor_copy(dst, row(k.h, t, 0, width))
        return stage

    def add_to_x(ph, t, slot, ps, c):
        tmp = ph.buf["tmp"]
        c(nc.vector.tensor_tensor(tmp[:, slot, :], ps[0][:, 0:C], ph.buf["mb"][:], ALU.add))
        return nc.vector.tensor_tensor(row(k.x, t, 0, C), row(k.x, t, 0, C), tmp[:, slot, :], ALU.add)

    def bufs(kb, width):
        return [("w", [P, kb, width], F32), ("mb", [P, width], F32), ("tmp", [P, 2, width], F32)]

    phase_dense(k, "mlp1", 2, [("w", 2 * P)], stage_attended(k, g, False), 1, relu_to_h(2 * P), 1,
                sb=bufs(2, 2 * P) + [("part", [P, 2, C], F32), ("bias", [P, C], F32)],
                loads=[("w", weights(a["L1_gnn_M1"])), ("mb", wide(a["L1_gnn_mb1"])), ("bias", wide(a["L1_gnn_b3"]))])
    phase_dense(k, "mlp2", 2, [("w", HIDDEN2)], stage_h(2 * P), 0, relu_to_h(HIDDEN2), 1, sb=bufs(2, HIDDEN2),
                loads=[("w", weights(a["L1_gnn_M2"])), ("mb", wide(a["L1_gnn_mb2"]))])
    phase_dense(k, "mlp3", 1, [("w", C)], stage_h(HIDDEN2), 0, add_to_x, 1, sb=bufs(1, C),
                loads=[("w", weights(a["L1_gnn_M3"])), ("mb", wide(a["L1_gnn_mb3"]))])


def attention_layers(k, rstd, shift):
    a = k.ins
    heads, width = a["L1_gnn_a_src1"].shape
    with ExitStack() as ctx:
        s = Spans(k, ctx)
        buf = Gat.buffers(k, ctx, heads)
        phase_spans(k, s)
        phase_norm(k, "norm2", k.x, 1e-5, rstd, shift)
        stage, per, sb, loads, kb = stage_normed(k, k.x, rstd, shift), 0, [], [], C // P
        for n, H, D, table in ((1, heads, width, k.h_table), (2, heads, width, k.h_table), (3, 1, C, k.h_table3)):
            g = Gat(buf, n, H, D, table)
            phase_gat_dense(k, g, kb, a[f"L1_gnn_W{n}"], a[f"L1_gnn_a_src{n}"], a[f"L1_gnn_a_dst{n}"], stage, per, sb, loads)
            phase_gat_scores(k, g)
            phase_gat_softmax(k, g, s)
            phase_gat_edges(k, g)
            phase_gat_nodes(k, g)
            stage, per, kb = stage_attended(k, g, True), 2 * H + 1, H * D // P
            sb = [("part", [P, 2, H * D], F32), ("neg", [P, 2, H * D], F32), ("bias", [P, H * D], F32)]
            loads = [("bias", wide(a[f"L1_gnn_b{n}"]))]
        phase_mlp(k, g)


def phase_output(k):
    nc = k.nc
    with Phase(k, "output") as ph:
        stored = ph.sem("stored")
        block = ph.block()

        @block.sync
        def _(sp):
            full = (TILES - 1) * P
            sp.dma_start(k.out[0:full, :].rearrange("(t p) c -> p t c", p=P), k.x[:, 0:TILES - 1, :]).then_inc(stored, 16)
            sp.dma_start(k.out[full:N, :], k.x[0:LAST, TILES - 1, :]).then_inc(stored, 16)
            sp.wait_ge(stored, 32)


def run_phases(k, stop=None):
    phase_constants(k)
    phase_items(k)
    rstd, shift = k.sb("rstd", [P, TILES], F32), k.sb("shift", [P, TILES], F32)
    phase_norm(k, "norm0", k.x, 1e-5, rstd, shift)
    if stop != "skip0":
        phase_qkv(k, rstd, shift)
        phase_attention_edges(k)
        phase_attention_out(k, rstd, shift)
        phase_norm(k, "norm1", k.h, 1e-5, rstd, shift)
        phase_node_ffn(k, rstd, shift)
        routed_layer(k, "moe0", "L0_ffn", k.ins["L0_ffn_Wg"], k.ins["L0_ffn_bg"], False, True, rstd, shift)
    attention_layers(k, rstd, shift)
    if stop != "skip0":
        routed_layer(k, "moe1", "L1_ffn", k.ins["L1_ffn_Wr"], k.ins["L1_ffn_br"], True, False, rstd, shift)
        phase_output(k)


_OUT_SHAPE = (N, C)


def program(nc, ins, out, stop=None):
    with ExitStack() as ctx:
        k = Kit(nc, ctx, ins, out)
        run_phases(k, stop)


def host_arrays(inputs):
    import numpy as _np
    a = {n: _np.ascontiguousarray(v) for n, v in inputs.items()}
    for n in ("Wq", "Wk", "Wv", "Wp", "W1", "W2"):
        a["L0_gnn_" + n] = _np.ascontiguousarray(a["L0_gnn_" + n].T)
    a["L0_gnn_Wkv"] = _np.concatenate([a.pop("L0_gnn_Wk"), a.pop("L0_gnn_Wv")], axis=1)
    a["L0_gnn_bkv"] = _np.concatenate([a.pop("L0_gnn_bk"), a.pop("L0_gnn_bv")])
    return a


def declare(nc, arrays):
    return {n: nc.dram_tensor(f"in_{n}", v.shape, mybir.dt.from_np(v.dtype), kind="ExternalInput").ap()
            for n, v in arrays.items()}


def kernel(**inputs):
    import concourse.bacc as _bacc
    from concourse.bass_utils import run_bass_kernel_spmd as _run

    nc = _bacc.Bacc("TRN2", target_bir_lowering=False, num_devices=1)
    arrays = host_arrays(inputs)
    ins = declare(nc, arrays)
    out = nc.dram_tensor("out_x", _OUT_SHAPE, F32, kind="ExternalOutput").ap()
    program(nc, ins, out)
    r = _run(nc, [{f"in_{n}": v for n, v in arrays.items()}], core_ids=[0])
    return r.results[0]["out_x"]
```

```python
from contextlib import ExitStack

import numpy as np

import concourse.bass as bass
from concourse import mybir

F32, BF16, I32, U32 = mybir.dt.float32, mybir.dt.bfloat16, mybir.dt.int32, mybir.dt.uint32
ALU = mybir.AluOpType
ACT = mybir.ActivationFunctionType
AX = mybir.AxisListType

P = 128
N, C, EDGES = 3125, 256, 53125
TILES = -(-N // P)
LAST = N - (TILES - 1) * P
PAIRS = -(-EDGES // (2 * P))
ITEMS = PAIRS + TILES - 1
SUBS = 2 * ITEMS
SUBP = -(-SUBS // P) * P
BLK = SUBP // P
GB = PAIRS // 2
NOWHERE = 4000
BIG = 1.0e30
HEADS0, HD0 = 8, 32
HID = 1024
EXPERTS = 8
SLOTS_X = (2 * N + EXPERTS * (P - 1)) // P
TABW = 516
ACCW = 524


class Chain:

    def __init__(self, eng, sem):
        self.eng, self.sem, self.base, self.local, self.per, self.start, self.turns = eng, sem, 0, 0, None, 0, 0

    def loop(self, turns, per):
        self.start, self.per, self.turns = self.base + self.local, per, turns
        return self

    def at(self, t):
        self.base, self.local = self.start + t * self.per, 0

    def over(self):
        self.base, self.local = self.start + self.turns * self.per, 0

    def mark(self, ins):
        self.local += 1
        assert self.per is None or self.local <= self.per or isinstance(self.base, int), "chain"
        ins.then_inc(self.sem, 1)

    def wait(self):
        self.eng.wait_ge(self.sem, self.base + self.local)

    def __call__(self, ins):
        self.mark(ins)
        self.wait()

    def full(self):
        assert self.local == self.per, (self.local, self.per)


def apart(ph, eng):
    eng.sem_inc(ph.passes, 1)


def ready(t, slots=2):
    return t + slots + 1


def free(t):
    return t + 1


def sweep(eng, n, step):
    with eng.Fori(0, n // 2) as i:
        step(2 * i, 0)
        step(2 * i + 1, 1)
    if n % 2:
        step(n - 1, 0)


def staggered(eng, n, steps):
    depth = len(steps) - 1
    steps = [s if s else (lambda t, slot: None) for s in steps]
    for i in range(-depth, 0):
        for j, step in enumerate(steps):
            if i + depth - j >= 0:
                step(i + depth - j, (i + depth - j) % 2)
    m = n - depth

    def turn(i, parity):
        for j, step in enumerate(steps):
            step(i + (depth - j), (parity + depth - j) % 2)

    with eng.Fori(0, m // 2) as i:
        turn(2 * i, 0)
        turn(2 * i + 1, 1)
    if m % 2:
        turn(m - 1, 0)
    for i in range(m, n):
        for j, step in enumerate(steps):
            if i + depth - j < n:
                step(i + depth - j, (i + depth - j) % 2)


def ringed(eng, n, ring, steps):
    assert n % ring == 0
    depth = len(steps) - 1
    steps = [s if s else (lambda t, r, i: None) for s in steps]

    def turn(base, i, r, limit):
        for j, step in enumerate(steps):
            d = r + depth - j
            if d >= 0 and d < limit:
                step(base + d, d % ring, i + d // ring)

    for r in range(-depth, 0):
        turn(0, 0, r, n)
    with eng.Fori(0, n // ring - 1) as i:
        for r in range(ring):
            turn(i * ring, i, r, n)
    for r in range(ring):
        turn(n - ring, n // ring - 1, r, ring)


class Kit:

    def __init__(self, nc, ctx, ins, out):
        self.nc, self.ctx, self.ins, self.out = nc, ctx, ins, out
        sb, dram = self.sb, self.dram
        self.ps = [ctx.enter_context(nc.psum_tensor(f"ps{i}", [P, 512], F32)) for i in range(8)]
        self.ident = sb("ident", [P, P], F32)
        self.ones = sb("ones", [P, P], F32)
        self.before = sb("before", [P, P], F32)
        self.iota_row = sb("iota_row", [P, 256], F32)
        self.iota_p = sb("iota_p", [P, 1], F32)
        self.x = sb("x", [P, TILES, C], F32)
        self.h = sb("h", [P, TILES, TABW], F32)
        self.acc = sb("acc", [P, TILES, ACCW], F32)
        self.item_tile = sb("item_tile", [1, ITEMS + 8], I32)
        self.src_of = sb("src_of", [P, SUBP], I32)
        self.dst_in = sb("dst_in", [P, SUBP], F32)
        self.src_hi = sb("src_hi", [P, SUBP], F32)
        self.is_last = sb("is_last", [P, SUBP], F32)
        self.dst_rows = dram("dst_rows", [SUBP, P], BF16)
        self.src_rows = dram("src_rows", [SUBP, P], BF16)
        self.key_rows = dram("key_rows", [SUBP + 1, P], F32)
        self.off_rows = dram("off_rows", [SUBP, P], F32)
        self.kv_table = dram("kv_table", [TILES * P, 512], F32)
        self.h_table = dram("h_table", [TILES * P, TABW], F32)
        self.h_table3 = dram("h_table3", [TILES * P, 257], F32)
        self.routed_in = dram("routed_in", [SLOTS_X * P, C], F32)
        self.routed_out = dram("routed_out", [SLOTS_X * P, C], F32)

    def sb(self, name, shape, dt):
        return self.ctx.enter_context(self.nc.sbuf_tensor(name, shape, dt))

    def dram(self, name, shape, dt):
        return self.nc.dram_tensor(name, shape, dt, kind="Internal").ap()


class Phase:

    def __init__(self, k, name):
        self.k, self.name, self.ctx, self.sems = k, name, ExitStack(), []
        self.passes = self.sem("passes")

    def __enter__(self):
        return self

    def __exit__(self, *a):
        self.ctx.__exit__(*a)
        self.k.nc.clear_and_free_semaphores(self.sems)
        self.k.nc.all_engine_barrier()

    def sem(self, name):
        self.sems.append(self.k.nc.alloc_semaphore(name=f"{self.name}_{name}"))
        return self.sems[-1]

    def sb(self, name, shape, dt=F32):
        return self.ctx.enter_context(self.k.nc.sbuf_tensor(f"{self.name}_{name}", shape, dt))

    def block(self):
        return self.ctx.enter_context(self.k.nc.Block())


def wide(row):
    return row.rearrange("(a c) -> a c", a=1).to_broadcast([P, row.shape[0]])



def phase_constants(k):
    nc = k.nc
    with Phase(k, "const") as ph:
        cleared, loaded, base, made = ph.sem("cleared"), ph.sem("loaded"), ph.sem("base"), ph.sem("made")
        block = ph.block()

        @block.gpsimd
        def _(pool):
            nc.gpsimd.memset(k.x[:, TILES - 1, :], 0.0).then_inc(cleared, 1)
            nc.gpsimd.iota(k.iota_row[:], pattern=[[1, 256]], base=0, channel_multiplier=0,
                           allow_small_or_imprecise_dtypes=True).then_inc(base, 1)
            nc.gpsimd.iota(k.iota_p[:], pattern=[[0, 1]], base=0, channel_multiplier=1,
                           allow_small_or_imprecise_dtypes=True).then_inc(base, 1)

        @block.vector
        def _(dve):
            nc.vector.memset(k.ones[:], 1.0)
            nc.vector.memset(k.item_tile[:], 0)
            dve.wait_ge(base, 2)
            nc.vector.tensor_scalar(k.ident[:], k.iota_row[:, 0:P], k.iota_p[:, 0:1], None, ALU.is_equal)
            nc.vector.tensor_scalar(k.before[:], k.iota_row[:, 0:P], k.iota_p[:, 0:1], None, ALU.is_gt)

        @block.sync
        def _(sp):
            full = (TILES - 1) * P
            sp.dma_start(k.x[:, 0:TILES - 1, :], k.ins["x"][0:full, :].rearrange("(t p) c -> p t c", p=P)).then_inc(loaded, 16)
            sp.wait_ge(cleared, 1)
            sp.dma_start(k.x[0:LAST, TILES - 1, :], k.ins["x"][full:N, :]).then_inc(loaded, 16)
            sp.wait_ge(loaded, 32)


def phase_items(k):
    nc = k.nc
    tail = EDGES - (PAIRS - 1) * 2 * P
    with Phase(k, "items") as ph:
        dst_i, src_i = ph.sb("dst_i", [P, 2, 256], I32), ph.sb("src_i", [P, 2, 256], I32)
        dst, src = ph.sb("dst", [P, 2, 256]), ph.sb("src", [P, 2, 256])
        lim = ph.sb("lim", [P, TILES - 1])
        passed = ph.sb("passed", [P, 2, TILES - 1])
        turn = ph.sb("turn", [P, 1])
        iota_k = ph.sb("iota_k", [P, ITEMS])
        stepped = ph.sb("stepped", [P, ITEMS])
        tile_of, pair_of = ph.sb("tile_of", [P, ITEMS]), ph.sb("pair_of", [P, ITEMS])
        sel = ph.sb("sel", [P, 2, ITEMS])
        src_f = ph.sb("src_f", [P, SUBP])
        dst_f = ph.sb("dst_f", [P, SUBP])
        hi_i = ph.sb("hi_i", [P, SUBP], I32)
        keys, offs = ph.sb("keys", [P, 2, 256]), ph.sb("offs", [P, 2, 256])
        nrow = ph.sb("nrow", [P, 2])
        lo_i = ph.sb("lo_i", [P, 2, 256], I32)
        lo_b, off_b = ph.sb("lo_b", [P, 2, 256], BF16), ph.sb("off_b", [P, 2, 256], BF16)
        padf, padb = ph.sb("padf", [P, P]), ph.sb("padb", [P, P], BF16)
        filled, loaded, iotas = ph.sem("filled"), ph.sem("loaded"), ph.sem("iotas")
        fed, made, link, stored, rows_out = ph.sem("fed"), ph.sem("made"), ph.sem("link"), ph.sem("stored"), ph.sem("rows_out")
        block = ph.block()
        kb = [(0, P), (P, ITEMS - P)]

        @block.gpsimd
        def _(pool):
            nc.gpsimd.memset(dst_i[:], NOWHERE).then_inc(filled, 1)
            nc.gpsimd.memset(src_i[:], 0).then_inc(filled, 1)
            nc.gpsimd.iota(iota_k[:], pattern=[[1, ITEMS]], base=0, channel_multiplier=0,
                           allow_small_or_imprecise_dtypes=True).then_inc(iotas, 1)
            nc.gpsimd.iota(lim[:], pattern=[[P, TILES - 1]], base=P, channel_multiplier=0,
                           allow_small_or_imprecise_dtypes=True).then_inc(iotas, 1)

        @block.sync
        def _(sp):
            sp.wait_ge(filled, 2)
            for tile, vec in ((dst_i, k.ins["dst"]), (src_i, k.ins["src"])):
                sp.dma_start(tile[0:GB, 0, :], vec[0:GB * 256].rearrange("(g e) -> g e", e=256)).then_inc(loaded, 16)
                sp.dma_start(tile[0:GB - 1, 1, :],
                             vec[GB * 256:(PAIRS - 1) * 256].rearrange("(g e) -> g e", e=256)).then_inc(loaded, 16)
                sp.dma_start(tile[GB - 1:GB, 1, 0:tail],
                             vec[(PAIRS - 1) * 256:EDGES].rearrange("(g e) -> g e", g=1)).then_inc(loaded, 16)
            sp.wait_ge(rows_out, 1)
            for tab, pad in ((k.dst_rows, padb), (k.src_rows, padb), (k.off_rows, padf)):
                sp.dma_start(tab[SUBS:SUBP, :], pad[0:SUBP - SUBS, :]).then_inc(stored, 16)
            sp.dma_start(k.key_rows[SUBS:SUBP + 1, :], padf[0:SUBP + 1 - SUBS, :]).then_inc(stored, 16)
            sp.wait_ge(rows_out, 2)
            for b, (k0, m) in enumerate(kb):
                for tab, tile in ((k.dst_rows, off_b), (k.src_rows, lo_b), (k.off_rows, offs), (k.key_rows, keys)):
                    sp.dma_start(tab[2 * k0:2 * (k0 + m), :].rearrange("(g s) e -> g (s e)", s=2), tile[0:m, b, :]).then_inc(stored, 16)
            sp.wait_ge(stored, 16 * 12)

        @block.tensor
        def _(pe):
            pe.wait_ge(fed, 1)
            for b in range(2):
                mm = nc.tensor.matmul(k.ps[0][0:TILES - 1, 0:1], passed[0:GB, b, :], k.ones[0:GB, 0:1],
                                      start=(b == 0), stop=(b == 1))
            mm.then_inc(made, 1)
            pe.wait_ge(fed, 2)
            nc.tensor.matmul(k.ps[1][:, 0:ITEMS], k.ones[0:TILES - 1, :], stepped[0:TILES - 1, :], start=True, stop=True)
            for b, (k0, m) in enumerate(kb):
                mm = nc.tensor.matmul(k.ps[2 + b][0:m, 0:1], stepped[0:TILES - 1, k0:k0 + m], k.ones[0:TILES - 1, 0:1],
                                      start=True, stop=True)
            mm.then_inc(made, 1)
            pe.wait_ge(fed, 3)
            for a, arr in enumerate((dst, src)):
                for s in range(2):
                    for b in range(2):
                        mm = nc.tensor.matmul(k.ps[4 + 2 * a + s][:, 0:ITEMS], arr[0:GB, b, s * P:(s + 1) * P],
                                              sel[0:GB, b, :], start=(b == 0), stop=(b == 1))
            mm.then_inc(made, 1)
            pe.wait_ge(fed, 4)
            for a, arr in enumerate((dst, src)):
                for q, (k0, m) in enumerate(kb):
                    for b in range(2):
                        mm = nc.tensor.matmul(k.ps[[0, 1][a]][0:m, q * 256:q * 256 + 256], sel[0:GB, b, k0:k0 + m],
                                              arr[0:GB, b, :], start=(b == 0), stop=(b == 1))
            mm.then_inc(made, 1)

        @block.vector
        def _(dve):
            v, c = nc.vector, Chain(dve, link)
            v.memset(padf[:], float(NOWHERE))
            c.mark(v.memset(src_f[:], 0.0))
            c.mark(v.memset(dst_f[:], float(NOWHERE)))
            c(v.memset(padb[:], float(NOWHERE)))
            v.memset(sel[:], 0.0).then_inc(rows_out, 1)
            dve.wait_ge(loaded, 96)
            dve.wait_ge(iotas, 2)
            c.mark(v.tensor_copy(dst[:], dst_i[:]))
            c(v.tensor_copy(src[:], src_i[:]))
            for b in range(2):
                last = v.tensor_scalar(passed[:, b, :], lim[:], dst[:, b, 255:256], None, ALU.is_gt)
                c.mark(last)
            c.wait()
            dve.sem_inc(fed, 1)
            dve.wait_ge(made, 1)
            c(v.tensor_scalar(turn[0:TILES - 1, :], k.ps[0][0:TILES - 1, 0:1], k.iota_p[0:TILES - 1, 0:1], None, ALU.add))
            v.tensor_scalar(stepped[0:TILES - 1, :], iota_k[0:TILES - 1, :], turn[0:TILES - 1, 0:1], None,
                            ALU.is_gt).then_inc(fed, 1)
            dve.wait_ge(made, 2)
            c(v.tensor_copy(tile_of[:], k.ps[1][:, 0:ITEMS]))
            c.mark(v.tensor_copy(k.item_tile[0:1, 0:ITEMS], tile_of[0:1, :]))
            c(v.tensor_tensor(pair_of[:], iota_k[:], tile_of[:], ALU.subtract))
            for b in range(2):
                c(v.tensor_scalar(sel[:, b, :], pair_of[:], float(-GB * b), k.iota_p[:, 0:1], ALU.add, ALU.is_equal))
                if b == 0:
                    for q, (k0, m) in enumerate(kb):
                        c(v.tensor_scalar(nrow[0:m, q:q + 1], k.ps[2 + q][0:m, 0:1], float(P), None, ALU.mult))
            dve.sem_inc(fed, 1)
            dve.wait_ge(made, 3)
            for s in range(2):
                c.mark(v.tensor_copy(dst_f[:, s:SUBS:2], k.ps[4 + s][:, 0:ITEMS]))
                c(v.tensor_copy(src_f[:, s:SUBS:2], k.ps[6 + s][:, 0:ITEMS]))
            dve.sem_inc(fed, 1)
            c(v.tensor_copy(k.src_of[:], src_f[:]))
            c(v.tensor_scalar(hi_i[:], k.src_of[:], 7, None, ALU.arith_shift_right))
            c(v.tensor_copy(k.src_hi[:], hi_i[:]))
            v.tensor_copy(k.dst_in[:, SUBS:SUBP], dst_f[:, SUBS:SUBP])
            for s in range(2):
                c(v.scalar_tensor_tensor(k.dst_in[:, s:SUBS:2], tile_of[:], float(-P), dst_f[:, s:SUBS:2], ALU.mult, ALU.add))
            dve.wait_ge(made, 4)
            for q, (k0, m) in enumerate(kb):
                c.mark(v.tensor_copy(keys[0:m, q, :], k.ps[0][0:m, q * 256:q * 256 + 256]))
                c(v.tensor_scalar(offs[0:m, q, :], k.ps[0][0:m, q * 256:q * 256 + 256], nrow[0:m, q:q + 1], None, ALU.subtract))
                c.mark(v.tensor_copy(off_b[0:m, q, :], offs[0:m, q, :]))
                c(v.tensor_copy(lo_i[0:m, q, :], k.ps[1][0:m, q * 256:q * 256 + 256]))
                c(v.tensor_scalar(lo_i[0:m, q, :], lo_i[0:m, q, :], 127, None, ALU.bitwise_and))
                c(v.tensor_copy(lo_b[0:m, q, :], lo_i[0:m, q, :]))
            dve.sem_inc(rows_out, 1)



def phase_norm(k, name, src, eps, rstd, shift):
    nc = k.nc
    group = 5
    with Phase(k, name) as ph:
        stats, mv = ph.sb("stats", [P, group, 6]), ph.sb("mv", [P, group, 2])
        both = ph.sb("both", [P, TILES, 2])
        link, var_ready, root_ready = ph.sem("link"), ph.sem("var_ready"), ph.sem("root_ready")
        block = ph.block()

        @block.vector
        def _(dve):
            v, c = nc.vector, Chain(dve, link)
            turns = TILES // group
            c.loop(turns, 3 * group - group + 1)
            with dve.Fori(0, turns) as g:
                c.at(g)
                for j in range(group):
                    c.mark(v.bn_stats(stats[:, j:j + 1, :], src[:, bass.ds(g * group + j, 1), 0:C]))
                c.wait()
                apart(ph, dve)
                for j in range(group):
                    c.mark(v.bn_aggr(mv[:, j, :], stats[:, j, :]))
                c.wait()
                c(v.tensor_copy(both[:, bass.ds(g * group, group), :], mv[:]))
                c.full()
            c.over()
            v.tensor_scalar(rstd[:], both[:, :, 1], eps, None, ALU.add).then_inc(var_ready, 1)
            dve.wait_ge(root_ready, 1)
            c(v.reciprocal(rstd[:], shift[:]))
            v.scalar_tensor_tensor(shift[:], both[:, :, 0], -1.0, rstd[:], ALU.mult, ALU.mult)

        @block.scalar
        def _(act):
            act.wait_ge(var_ready, 1)
            nc.scalar.activation(shift[:], rstd[:], ACT.Sqrt).then_inc(root_ready, 1)


def phase_dense(k, name, kb, outs, stage, per_stage, evac, per_evac, loads=(), sb=(), stores=(), exps=None):
    nc = k.nc
    with Phase(k, name) as ph:
        ph.buf = {n: ph.sb(n, shape, dt) for n, shape, dt in sb}
        staged_tile = ph.sb("staged_tile", [P, 2, kb * P])
        turned_tile = ph.sb("turned_tile", [P, 2, kb * P])
        loaded = ph.sem("loaded")
        staged, turned, copied, made, taken = (ph.sem(s) for s in ("staged", "turned", "copied", "made", "taken"))
        link_s, link_e, stored = ph.sem("link_s"), ph.sem("link_e"), ph.sem("stored")
        ph.capped, ph.exped = ph.sem("capped"), ph.sem("exped")
        pst = [k.ps[0], k.ps[1]]
        pso = [[k.ps[2 + s * len(outs) + j] for j in range(len(outs))] for s in range(2)]
        block = ph.block()
        nload = 0

        @block.sync
        def _(sp):
            for dst, src in loads:
                sp.dma_start(ph.buf[dst][:] if isinstance(dst, str) else dst, src).then_inc(loaded, 16)
            for last, dst, src in stores:
                sp.wait_ge(taken, ready(last))
                sp.dma_start(dst, src).then_inc(stored, 16)
            if loads:
                sp.wait_ge(loaded, 16 * len(loads))
            if stores:
                sp.wait_ge(stored, 16 * len(stores))

        @block.vector
        def _(dve):
            dve.sem_inc(staged, 2)
            dve.sem_inc(taken, 2)
            cs = Chain(dve, link_s).loop(TILES, per_stage)
            ce = Chain(dve, link_e).loop(TILES, per_evac)
            if loads:
                dve.wait_ge(loaded, 16 * len(loads))

            def stage_step(t, slot):
                dve.wait_ge(turned, free(t))
                cs.at(t)
                stage(ph, t, slot, staged_tile[:, slot, :], cs).then_inc(staged, 1)
                cs.full()

            def evac_step(t, slot):
                dve.wait_ge(made, ready(t))
                ce.at(t)
                evac(ph, t, slot, pso[slot], ce).then_inc(taken, 1)
                ce.full()

            staggered(dve, TILES, [stage_step, None, evac_step])

        @block.scalar
        def _(act):
            act.sem_inc(copied, 2)

            def copy_step(t, slot):
                act.wait_ge(turned, ready(t))
                act.wait_ge(made, free(t))
                nc.scalar.copy(turned_tile[:, slot, :], pst[slot][:, 0:kb * P]).then_inc(copied, 1)

            def exp_step(t, slot):
                act.wait_ge(ph.capped, t + 1)
                act.activation(ph.buf[exps][:, slot, :], ph.buf[exps][:, slot, :], ACT.Exp).then_inc(ph.exped, 1)

            staggered(act, TILES, [exp_step, copy_step] if exps else [copy_step])

        @block.tensor
        def _(pe):
            pe.sem_inc(turned, 2)
            pe.sem_inc(made, 2)
            if loads:
                pe.wait_ge(loaded, 16 * len(loads))

            def turn_step(t, slot):
                pe.wait_ge(staged, ready(t))
                pe.wait_ge(copied, free(t))
                for b in range(kb):
                    mm = nc.tensor.transpose(pst[slot][:, b * P:(b + 1) * P], staged_tile[:, slot, b * P:(b + 1) * P],
                                             k.ident[:])
                mm.then_inc(turned, 1)

            def product_step(t, slot):
                pe.wait_ge(copied, ready(t))
                pe.wait_ge(taken, free(t))
                for j, (w, width) in enumerate(outs):
                    wt = ph.buf[w] if isinstance(w, str) else w
                    for b in range(kb):
                        mm = nc.tensor.matmul(pso[slot][j][:, 0:width], turned_tile[:, slot, b * P:(b + 1) * P],
                                              wt[:, b, 0:width], start=(b == 0), stop=(b == kb - 1))
                mm.then_inc(made, 1)

            staggered(pe, TILES, [turn_step, product_step])


def weights(w):
    return w.rearrange("(b p) n -> p b n", p=P)


def stage_normed(k, src, rstd, shift):
    def stage(ph, t, slot, dst, c):
        return k.nc.vector.tensor_scalar(dst, src[:, bass.ds(t, 1), 0:C].rearrange("p a c -> p (a c)"),
                                         rstd[:, bass.ds(t, 1)], shift[:, bass.ds(t, 1)], ALU.mult, ALU.add)
    return stage


def row(buf, t, a, b):
    return buf[:, bass.ds(t, 1), a:b].rearrange("p a c -> p (a c)")


def tile_stores(table, src, width):
    out = []
    for g in range(0, TILES, 5):
        out.append((g + 4, table[g * P:(g + 5) * P, 0:width].rearrange("(t p) c -> p t c", p=P), src[:, g:g + 5, 0:width]))
    return out

def phase_qkv(k, rstd, shift):
    nc, a = k.nc, k.ins

    def evac(ph, t, slot, ps, c):
        c(nc.vector.tensor_tensor(row(k.h, t, 0, C), ps[0][:, 0:C], ph.buf["bq"][:], ALU.add))
        nc.vector.tensor_scalar(row(k.h, t, 0, C), row(k.h, t, 0, C), float(HD0) ** -0.5, None, ALU.mult)
        return nc.vector.tensor_tensor(row(k.acc, t, 0, 2 * C), ps[1][:, 0:2 * C], ph.buf["bkv"][:], ALU.add)

    phase_dense(
        k, "qkv", 2, [("wq", C), ("wkv", 2 * C)], stage_normed(k, k.x, rstd, shift), 0, evac, 1,
        sb=[("wq", [P, 2, C], F32), ("wkv", [P, 2, 2 * C], F32), ("bq", [P, C], F32), ("bkv", [P, 2 * C], F32)],
        loads=[("wq", weights(a["L0_gnn_Wq"])), ("wkv", weights(a["L0_gnn_Wkv"])),
               ("bq", wide(a["L0_gnn_bq"])), ("bkv", wide(a["L0_gnn_bkv"]))],
        stores=tile_stores(k.kv_table, k.acc, 2 * C))


def load_batches(sp, used, credits, tables, row_in):
    def load(b, slot):
        for table, tile in tables:
            sp.dma_start(tile[:, slot, :], item_rows(table, 4 * b, 4)).then_inc(row_in[slot], 16)

    load(0, 0)
    load(1, 1)
    with sp.Fori(0, ITEMS // 8 - 1) as i:
        for slot in range(2):
            sp.wait_ge(used, i * 8 + (4 * slot + 4 + credits))
            load(2 * i + (2 + slot), slot)


def phase_attention_edges(k):
    nc = k.nc
    RING = 8
    S = 4
    W = C + HEADS0
    with Phase(k, "edges0") as ph:
        rows = ph.sb("rows", [P, RING, 2, 2 * C])
        index = ph.sb("index", [P, RING, 2], I32)
        dst_row = ph.sb("dst_row", [P, 2, 4 * 256], BF16)
        minus_p, one_col = ph.sb("minus_p", [P, 1]), ph.sb("one_col", [P, 1])
        hot_t = ph.sb("hot_t", [P, S, 256])
        hot = ph.sb("hot", [P, S, 2 * P])
        prod = ph.sb("prod", [P, 2, 2 * C])
        score = ph.sb("score", [P, S, 2 * HEADS0])
        out_rows = ph.sb("out_rows", [P, S, 2, W])
        cleared, consts, indexed = ph.sem("cleared"), ph.sem("consts"), ph.sem("indexed")
        gathered = [ph.sem(f"gathered{r}") for r in range(RING)]
        row_in = [ph.sem(f"row_in{s}") for s in range(2)]
        hot_t_made, q_made, multiplied, reduced, clipped, exped, hot_made, weighted, summed, added = (
            ph.sem(s) for s in ("hot_t_made", "q_made", "multiplied", "reduced", "clipped", "exped", "hot_made",
                                "weighted", "summed", "added"))
        link_a, link_h = ph.sem("link_a"), ph.sem("link_h")
        psq, pso = k.ps[0:S], k.ps[S:2 * S]
        block = ph.block()

        @block.sync
        def _(sp):
            load_batches(sp, hot_t_made, S, [(k.dst_rows, dst_row)], row_in)

        @block.gpsimd
        def _(pool):
            def gather(t, r, i):
                pool.wait_ge(indexed, t + 1)
                apart(ph, pool)
                for s in range(2):
                    nc.gpsimd.indirect_dma_start(rows[:, r, s, :], None, k.kv_table,
                                                 bass.IndirectOffsetOnAxis(ap=index[:, r, s:s + 1], axis=0)
                                                 ).then_inc(gathered[r], 16)
                if isinstance(t, int) and t == 1:
                    nc.gpsimd.memset(k.acc[:, :, 0:W], 0.0).then_inc(cleared, 1)
            for r in range(RING):
                gather(r, r, 0)
            with pool.Fori(1, ITEMS // RING) as i:
                for r in range(RING):
                    gather(i * RING + r, r, i)

        @block.scalar
        def _(act):
            act.sem_inc(hot_t_made, S)
            act.sem_inc(exped, S)
            act.sem_inc(hot_made, S)

            def one_hot_t(t, r, i):
                act.wait_ge(row_in[r // 4], (i + 1) * 16)
                act.wait_ge(q_made, free(t))
                act.activation(hot_t[:, r % S, :], dst_row[:, r // 4, r % 4 * 256:(r % 4 + 1) * 256], ACT.Abs,
                               bias=minus_p[:, 0:1]).then_inc(link_a, 1)
                act.wait_ge(link_a, t + 1)
                act.activation(hot_t[:, r % S, :], hot_t[:, r % S, :], ACT.Relu, bias=one_col[:, 0:1], scale=-1.0
                               ).then_inc(hot_t_made, 1)

            def exps(t, r, i):
                act.wait_ge(clipped, ready(t, S))
                act.wait_ge(summed, free(t))
                act.activation(out_rows[:, r % S, :, C:W], score[:, r % S, :].rearrange("p (s h) -> p s h", s=2),
                               ACT.Exp).then_inc(exped, 1)

            def one_hot(t, r, i):
                for s in range(2):
                    last = act.activation(hot[:, r % S, s * P:(s + 1) * P], k.iota_row[:, 0:P], ACT.Abs,
                                          bias=k.dst_in[:, bass.ds(2 * t + s, 1)], scale=-1.0)
                last.then_inc(link_h, 1)
                act.wait_ge(link_h, t + 1)
                act.activation(hot[:, r % S, :], hot[:, r % S, :], ACT.Relu, bias=one_col[:, 0:1], scale=-1.0
                               ).then_inc(hot_made, 1)

            def exps_and_one_hot(t, r, i):
                exps(t, r, i)
                one_hot(t, r, i)

            act.wait_ge(consts, 2)
            ringed(act, ITEMS, RING, [one_hot_t, None, None, None, exps_and_one_hot])

        @block.tensor
        def _(pe):
            pe.sem_inc(q_made, S)
            pe.sem_inc(summed, S)

            def q_of_edges(t, r, i):
                n = pe.value_load(k.item_tile[0:1, bass.ds(t, 1)], min_val=0, max_val=TILES - 1)
                pe.wait_ge(hot_t_made, ready(t, S))
                pe.wait_ge(multiplied, free(t))
                for s in range(2):
                    mm = nc.tensor.matmul(psq[r % S][:, s * C:(s + 1) * C], hot_t[:, r % S, s * P:(s + 1) * P],
                                          row(k.h, n, 0, C), start=True, stop=True)
                mm.then_inc(q_made, 1)

            def sums(t, r, i):
                pe.wait_ge(weighted, ready(t, S))
                pe.wait_ge(exped, ready(t, S))
                pe.wait_ge(hot_made, ready(t, S))
                pe.wait_ge(added, free(t))
                for s in range(2):
                    mm = nc.tensor.matmul(pso[r % S][:, 0:W], hot[:, r % S, s * P:(s + 1) * P], out_rows[:, r % S, s, :],
                                          start=(s == 0), stop=(s == 1))
                mm.then_inc(summed, 1)

            ringed(pe, ITEMS, RING, [q_of_edges, None, None, None, None, sums])

        @block.vector
        def _(dve):
            v = nc.vector
            v.memset(one_col[:], 1.0).then_inc(consts, 1)
            v.tensor_scalar(minus_p[:], k.iota_p[:], -1.0, None, ALU.mult).then_inc(consts, 1)
            for s in (multiplied, reduced, clipped, weighted, added):
                dve.sem_inc(s, S)

            def stage_index(t, r):
                v.tensor_copy(index[:, r, :], k.src_of[:, bass.ds(2 * t, 2)]).then_inc(indexed, 1)

            def multiply(t, r, i):
                dve.wait_ge(gathered[r], (i + 1) * 32)
                dve.wait_ge(q_made, ready(t, S))
                dve.wait_ge(reduced, t + S - 1)
                v.tensor_tensor(prod[:, r % 2, :], psq[r % S][:, 0:2 * C], rows[:, r, :, 0:C], ALU.mult).then_inc(multiplied, 1)

            def reduce(t, r, i):
                dve.wait_ge(multiplied, ready(t, S))
                dve.wait_ge(exped, free(t))
                v.tensor_reduce(score[:, r % S, :], prod[:, r % 2, :].rearrange("p (g d) -> p g d", d=HD0), AX.X, ALU.add
                                ).then_inc(reduced, 1)

            def clip(t, r, i):
                dve.wait_ge(reduced, ready(t, S))
                v.tensor_scalar(score[:, r % S, :], score[:, r % S, :], 10.0, -10.0, ALU.min, ALU.max).then_inc(clipped, 1)

            def weigh(t, r, i):
                dve.wait_ge(summed, free(t))
                dve.wait_ge(exped, ready(t, S))
                e = out_rows[:, r % S, :, C:W].rearrange("p s (h o) -> p s h o", o=1).to_broadcast([P, 2, HEADS0, HD0])
                v.tensor_tensor(out_rows[:, r % S, :, 0:C].rearrange("p s (h d) -> p s h d", d=HD0),
                                rows[:, r, :, C:2 * C].rearrange("p s (h d) -> p s h d", d=HD0), e, ALU.mult
                                ).then_inc(weighted, 1)

            def add(t, r, i):
                n = dve.value_load(k.item_tile[0:1, bass.ds(t, 1)], min_val=0, max_val=TILES - 1)
                dve.wait_ge(weighted, ready(t, S))
                stage_index(t + RING, r)
                dve.wait_ge(summed, ready(t, S))
                dve.wait_ge(cleared, 1)
                dve.wait_ge(added, t + S)
                v.tensor_tensor(row(k.acc, n, 0, W), row(k.acc, n, 0, W), pso[r % S][:, 0:W], ALU.add
                                ).then_inc(added, 1)

            for r in range(RING):
                stage_index(r, r)
            ringed(dve, ITEMS, RING, [multiply, reduce, clip, weigh, add])


def item_rows(table, t, n):
    return table[bass.ds(2 * t, 2 * n), :].rearrange("s e -> (s e)").rearrange("(a c) -> a c", a=1).to_broadcast([P, n * 256])


def phase_attention_out(k, rstd, shift):
    nc, a = k.nc, k.ins

    def stage(ph, t, slot, dst, c):
        v, den = nc.vector, ph.buf["den"]
        c(v.tensor_scalar(den[:, slot, :], row(k.acc, t, C, C + HEADS0), 1e-30, None, ALU.max))
        c(v.reciprocal(den[:, slot, :], den[:, slot, :]))
        return v.tensor_tensor(dst.rearrange("p (h d) -> p h d", d=HD0),
                               row(k.acc, t, 0, C).rearrange("p (h d) -> p h d", d=HD0),
                               den[:, slot, :].rearrange("p (h o) -> p h o", o=1).to_broadcast([P, HEADS0, HD0]), ALU.mult)

    def evac(ph, t, slot, ps, c):
        v, feat = nc.vector, ph.buf["feat"]
        c(v.tensor_scalar(feat[:, slot, :], row(k.x, t, 0, C), rstd[:, bass.ds(t, 1)], shift[:, bass.ds(t, 1)],
                          ALU.mult, ALU.add))
        c(v.tensor_tensor(feat[:, slot, :], feat[:, slot, :], ph.buf["bp"][:], ALU.add))
        return v.tensor_tensor(row(k.h, t, 0, C), ps[0][:, 0:C], feat[:, slot, :], ALU.add)

    phase_dense(k, "proj", 2, [("wp", C)], stage, 2, evac, 2,
                sb=[("wp", [P, 2, C], F32), ("bp", [P, C], F32), ("den", [P, 2, HEADS0], F32), ("feat", [P, 2, C], F32)],
                loads=[("wp", weights(a["L0_gnn_Wp"])), ("bp", wide(a["L0_gnn_bp"]))])



class Ffn:

    def __init__(self, ph, sets):
        self.w1, self.w2 = ph.sb("w1", [P, sets, 2, HID]), ph.sb("w2", [P, sets, HID // P, C])
        self.b1, self.b2 = ph.sb("b1", [P, sets, HID // P]), ph.sb("b2", [P, sets, C])
        self.g, self.b = ph.sb("g", [P, sets, 2]), ph.sb("b", [P, sets, 2])
        self.rows, self.turned = ph.sb("rows", [P, 2, C]), ph.sb("turned", [P, 2, 2, P])
        self.hidden = ph.sb("hidden", [P, 2, HID // P, P])
        self.rows_ready, self.turns, self.copies = ph.sem("rows_ready"), ph.sem("turns"), ph.sem("copies")
        self.ups, self.gelus, self.downs, self.taken = (ph.sem(s) for s in ("ups", "gelus", "downs", "taken"))
        self.rows_in, self.up_in, self.down_in = ([ph.sem(f"{n}{s}") for s in range(2)] for n in ("rows_in", "up_in", "down_in"))
        self.weights_in = ph.sem("weights_in")


def ffn_tensor(k, f, pe, n, wait_rows, wait_up, wait_down, multi):
    nc = k.nc
    pst, psh = [k.ps[0], k.ps[1]], [[k.ps[2], k.ps[3]], [k.ps[4], k.ps[5]]]
    pso = [k.ps[6], k.ps[7]]
    for s in (f.turns, f.ups, f.downs):
        pe.sem_inc(s, 2)

    def turn(t, slot):
        wait_rows(pe, t, slot)
        pe.wait_ge(f.copies, free(t))
        for b in range(2):
            mm = nc.tensor.transpose(pst[slot][:, b * P:(b + 1) * P], f.rows[:, slot, b:C:2], k.ident[:])
        mm.then_inc(f.turns, 1)

    def up(t, slot):
        wait_up(pe, t, slot)
        pe.wait_ge(f.copies, ready(t))
        pe.wait_ge(f.gelus, free(t))
        w = slot if multi else 0
        for j in range(HID // P):
            for b in range(2):
                mm = nc.tensor.matmul(psh[slot][j // 4][:, (j % 4) * P:(j % 4 + 1) * P], f.w1[:, w, b, j:HID:HID // P],
                                      f.turned[:, slot, b, :], start=(b == 0), stop=(b == 1))
        mm.then_inc(f.ups, 1)

    def down(t, slot):
        wait_down(pe, t, slot)
        pe.wait_ge(f.gelus, ready(t))
        pe.wait_ge(f.taken, free(t))
        w = slot if multi else 0
        for j in range(HID // P):
            mm = nc.tensor.matmul(pso[slot][:, 0:C], f.hidden[:, slot, j, :], f.w2[:, w, j, :],
                                  start=(j == 0), stop=(j == HID // P - 1))
        mm.then_inc(f.downs, 1)

    staggered(pe, n, [turn, up, down])


def turned_copy(k, f, dve, wait_up, multi, affine):
    v = k.nc.vector
    dve.sem_inc(f.copies, 2)

    def copy(t, slot):
        w = slot if multi else 0
        wait_up(dve, t, slot)
        dve.wait_ge(f.turns, ready(t))
        dve.wait_ge(f.ups, free(t))
        ps = k.ps[slot]
        if affine:
            for b in range(2):
                last = v.tensor_scalar(f.turned[:, slot, b, :], ps[:, b * P:(b + 1) * P], f.g[:, w, b:b + 1],
                                       f.b[:, w, b:b + 1], ALU.mult, ALU.add)
        else:
            last = v.tensor_copy(f.turned[:, slot, :, :], ps[:, 0:2 * P].rearrange("p (b n) -> p b n", b=2))
        last.then_inc(f.copies, 1)
    return copy


def ffn_scalar(k, f, act, n, wait_up, multi):
    act.sem_inc(f.gelus, 2)

    def gelu(t, slot):
        w = slot if multi else 0
        wait_up(act, t, slot)
        act.wait_ge(f.ups, ready(t))
        act.wait_ge(f.downs, free(t))
        for j in range(HID // P):
            last = act.activation(f.hidden[:, slot, j, :], k.ps[2 + 2 * slot + j // 4][:, (j % 4) * P:(j % 4 + 1) * P],
                                  ACT.Gelu, bias=f.b1[:, w, j:j + 1])
        last.then_inc(f.gelus, 1)

    sweep(act, n, gelu)


def phase_node_ffn(k, rstd, shift):
    nc, a = k.nc, k.ins
    with Phase(k, "ffn0") as ph:
        f = Ffn(ph, 1)
        part = ph.sb("part", [P, 2, C])
        link = ph.sem("link")
        block = ph.block()
        loads = [(f.w1[:, 0], a["L0_gnn_W1"].rearrange("(p b) n -> p b n", b=2)),
                 (f.w2[:, 0], a["L0_gnn_W2"].rearrange("(p j) n -> p j n", p=P)),
                 (f.b1[:, 0, :], a["L0_gnn_b1"].rearrange("(p j) -> p j", p=P)), (f.b2[:, 0, :], wide(a["L0_gnn_b2"])),
                 (f.g[:, 0, :], a["L0_gnn_ln_g"].rearrange("(p b) -> p b", b=2)),
                 (f.b[:, 0, :], a["L0_gnn_ln_b"].rearrange("(p b) -> p b", b=2))]

        @block.sync
        def _(sp):
            for dst, src in loads:
                sp.dma_start(dst, src).then_inc(f.weights_in, 16)
            sp.wait_ge(f.weights_in, 16 * len(loads))

        @block.tensor
        def _(pe):
            pe.wait_ge(f.weights_in, 16 * len(loads))
            ffn_tensor(k, f, pe, TILES, lambda e, t, s: e.wait_ge(f.rows_ready, ready(t)),
                       lambda e, t, s: None, lambda e, t, s: None, False)

        @block.scalar
        def _(act):
            act.wait_ge(f.weights_in, 16 * len(loads))
            ffn_scalar(k, f, act, TILES, lambda e, t, s: None, False)

        @block.vector
        def _(dve):
            v = nc.vector
            dve.sem_inc(f.rows_ready, 2)
            dve.sem_inc(f.taken, 2)
            dve.wait_ge(f.weights_in, 16 * len(loads))
            c = Chain(dve, link).loop(TILES, 2)

            def stage(t, slot):
                dve.wait_ge(f.turns, free(t))
                v.tensor_scalar(f.rows[:, slot, :], row(k.h, t, 0, C), rstd[:, bass.ds(t, 1)], shift[:, bass.ds(t, 1)],
                                ALU.mult, ALU.add).then_inc(f.rows_ready, 1)

            def take(t, slot):
                c.at(t)
                c(v.tensor_tensor(part[:, slot, :], row(k.h, t, 0, C), f.b2[:, 0, :], ALU.add))
                dve.wait_ge(f.downs, ready(t))
                c(v.tensor_tensor(part[:, slot, :], part[:, slot, :], k.ps[6 + slot][:, 0:C], ALU.add))
                v.tensor_tensor(row(k.x, t, 0, C), row(k.x, t, 0, C), part[:, slot, :], ALU.add).then_inc(f.taken, 1)

            staggered(dve, TILES, [stage, turned_copy(k, f, dve, lambda e, t, s: None, False, True), None, take])



class Route:

    def __init__(self, k, ctx, name):
        def sb(n, shape, dt):
            return ctx.enter_context(k.nc.sbuf_tensor(f"{name}_{n}", shape, dt))
        self.logits = sb("logits", [P, TILES, EXPERTS], F32)
        self.share = sb("share", [P, TILES, 2], F32)
        self.place = sb("place", [P, TILES, 2], I32)
        self.expert = sb("expert", [P, 64], I32)


def phase_gate(k, name, r, wg, bg, rstd, shift):
    nc = k.nc

    def stage(ph, t, slot, dst, c):
        for d in (row(k.h, t, 0, C), dst):
            last = nc.vector.tensor_scalar(d, row(k.x, t, 0, C), rstd[:, bass.ds(t, 1)], shift[:, bass.ds(t, 1)],
                                           ALU.mult, ALU.add)
        return last

    def evac(ph, t, slot, ps, c):
        return nc.vector.tensor_tensor(row(r.logits, t, 0, EXPERTS), ps[0][:, 0:EXPERTS], ph.buf["bg"][:], ALU.add)

    phase_dense(k, name, 2, [("wg", EXPERTS)], stage, 0, evac, 0,
                sb=[("wg", [P, 2, EXPERTS], F32), ("bg", [P, EXPERTS], F32)],
                loads=[("wg", weights(wg)), ("bg", wide(bg))])


def phase_route(k, name, r, first):
    nc = k.nc
    TE = TILES * EXPERTS
    with Phase(k, name) as ph:
        hot = ph.sb("hot", [P, 2, TILES, EXPERTS])
        mx = ph.sb("mx", [P, TILES, EXPERTS])
        ix = ph.sb("ix", [P, TILES, EXPERTS], U32)
        which = ph.sb("which", [P, TILES, 2])
        both, incl, pos, tmp = (ph.sb(n, [P, TILES, EXPERTS]) for n in ("both", "incl", "pos", "tmp"))
        zero = ph.sb("zero", [P, 2048])
        real = ph.sb("real", [P, TILES])
        e2, r1 = ph.sb("e2", [P, TILES]), ph.sb("r1", [P, TILES])
        count, tiles_f, ends = (ph.sb(n, [P, EXPERTS]) for n in ("count", "tiles_f", "ends"))
        count_i = ph.sb("count_i", [P, EXPERTS], I32)
        placef = ph.sb("placef", [P, TILES, 2])
        of_tile = ph.sb("of_tile", [P, 2, 64])
        link, diff, exped, masked, counted, placed = (ph.sem(s) for s in ("link", "diff", "exped", "masked", "counted", "placed"))
        zeroed, zero_in, scattered = ph.sem("zeroed"), ph.sem("zero_in"), ph.sem("scattered")
        block = ph.block()

        @block.scalar
        def _(act):
            act.wait_ge(diff, 1)
            act.activation(e2[:], r1[:], ACT.Exp).then_inc(exped, 1)

        @block.tensor
        def _(pe):
            pe.wait_ge(masked, 1)
            nc.tensor.matmul(k.ps[0][:, 0:TE], k.before[:], both[:].rearrange("p t e -> p (t e)"), start=True, stop=True)
            nc.tensor.matmul(k.ps[1][:, 0:TE], k.ones[:], both[:].rearrange("p t e -> p (t e)"),
                             start=True, stop=True).then_inc(counted, 1)

        @block.vector
        def _(dve):
            v, c = nc.vector, Chain(dve, link)
            v.memset(zero[:], 0.0).then_inc(zeroed, 1)
            for t in range(TILES):
                c.mark(v.max(mx[:, t, :], r.logits[:, t, :]))
            c.wait()
            for t in range(TILES):
                c.mark(v.max_index(ix[:, t, :], mx[:, t, :], r.logits[:, t, :]))
            c.wait()
            c(v.tensor_copy(which[:], ix[:, :, 0:2]))
            v.tensor_tensor(r1[:], mx[:, :, 1], mx[:, :, 0], ALU.subtract).then_inc(diff, 1)
            c(v.memset(real[:], 1.0))
            c(v.tensor_scalar(real[:, TILES - 1:TILES], k.iota_p[:], float(LAST), None, ALU.is_lt))
            for j in range(2):
                c(v.tensor_tensor(hot[:, j], k.iota_row[:, 0:EXPERTS].rearrange("p (a e) -> p a e", a=1).to_broadcast([P, TILES, EXPERTS]),
                                  which[:, :, j:j + 1].to_broadcast([P, TILES, EXPERTS]), ALU.is_equal))
            c(v.tensor_tensor(both[:], hot[:, 0], hot[:, 1], ALU.add))
            c(v.tensor_tensor(both[:], both[:], real[:].rearrange("p (t a) -> p t a", a=1).to_broadcast([P, TILES, EXPERTS]), ALU.mult))
            dve.sem_inc(masked, 1)
            dve.wait_ge(exped, 1)
            c(v.tensor_scalar(r1[:], e2[:], 1.0, None, ALU.add))
            c(v.reciprocal(r1[:], r1[:]))
            v.tensor_copy(r.share[:, :, 0], r1[:])
            v.tensor_tensor(r.share[:, :, 1], r1[:], e2[:], ALU.mult)
            dve.wait_ge(counted, 1)
            total = k.ps[1][:, 0:TE].rearrange("p (t e) -> p t e", e=EXPERTS)
            inner = k.ps[0][:, 0:TE].rearrange("p (t e) -> p t e", e=EXPERTS)
            dve.wait_ge(zeroed, 1)
            for e in range(EXPERTS):
                c.mark(v.tensor_tensor_scan(incl[:, :, e], total[:, :, e], zero[:, 0:TILES], 0.0, ALU.add, ALU.add))
            c.wait()
            c(v.tensor_tensor(pos[:], incl[:], total, ALU.subtract))
            c(v.tensor_tensor(pos[:], pos[:], inner, ALU.add))
            c(v.tensor_scalar(count[:], incl[:, TILES - 1, :], float(P - 1), None, ALU.add))
            c(v.tensor_copy(count_i[:], count[:]))
            c(v.tensor_scalar(count_i[:], count_i[:], 7, None, ALU.arith_shift_right))
            c(v.tensor_copy(tiles_f[:], count_i[:]))
            c(v.tensor_tensor_scan(ends[:], tiles_f[:], zero[:, 0:EXPERTS], 0.0, ALU.add, ALU.add))
            c(v.tensor_tensor(count[:], ends[:], tiles_f[:], ALU.subtract))
            c(v.tensor_scalar(count[:], count[:], float(P), None, ALU.mult))
            c(v.tensor_tensor(pos[:], pos[:], count[:].rearrange("p (a e) -> p a e", a=1).to_broadcast([P, TILES, EXPERTS]), ALU.add))
            for j in range(2):
                c(v.tensor_tensor(tmp[:], pos[:], hot[:, j], ALU.mult))
                c(v.tensor_reduce(placef[:, :, j], tmp[:], AX.X, ALU.add))
            c(v.tensor_copy(r.place[:], placef[:]))
            dve.sem_inc(placed, 1)
            c(v.tensor_scalar(of_tile[:, 0, :], k.iota_row[:, 0:64], ends[:, 0:1], None, ALU.is_ge))
            for e in range(1, EXPERTS - 1):
                c(v.scalar_tensor_tensor(of_tile[:, e % 2, :], k.iota_row[:, 0:64], ends[:, e:e + 1], of_tile[:, (e - 1) % 2, :],
                                         ALU.is_ge, ALU.add))
            v.tensor_copy(r.expert[:], of_tile[:, (EXPERTS - 2) % 2, :])

        @block.sync
        def _(sp):
            if first:
                sp.wait_ge(zeroed, 1)
                per = 2048 // C
                for j in range(SLOTS_X // per):
                    sp.dma_start(k.routed_in[j * P * per:(j + 1) * P * per, :].rearrange("(p r) c -> p (r c)", p=P),
                                 zero[:]).then_inc(zero_in, 16)
                sp.wait_ge(zero_in, 16 * (SLOTS_X // per))

        @block.gpsimd
        def _(pool):
            pool.wait_ge(placed, 1)
            if first:
                pool.wait_ge(zero_in, 16 * (SLOTS_X * C // 2048))
            for t in range(TILES):
                m = P if t < TILES - 1 else LAST
                for j in range(2):
                    nc.gpsimd.indirect_dma_start(k.routed_in, bass.IndirectOffsetOnAxis(ap=r.place[0:m, t, j:j + 1], axis=0),
                                                 k.h[0:m, t, 0:C], None).then_inc(scattered, 16)
            pool.wait_ge(scattered, 16 * 2 * TILES)


def phase_experts(k, name, r, prefix, norm):
    nc, a = k.nc, k.ins
    w = {n: a[f"{prefix}_{n}"] for n in ("W1", "b1", "W2", "b2")}
    if norm:
        w |= {n: a[f"{prefix}_{n}"] for n in ("ln_g", "ln_b")}
    with Phase(k, name) as ph:
        f = Ffn(ph, 2)
        result = ph.sb("result", [P, 2, C])
        stored, drained = ph.sem("stored"), ph.sem("drained")
        block = ph.block()
        up_dmas = 4 if norm else 2

        def rows_there(e, t, slot):
            e.wait_ge(f.rows_in[slot], (t // 2 + 1) * 16)

        def up_there(e, t, slot):
            e.wait_ge(f.up_in[slot], (t // 2 + 1) * (16 * up_dmas))

        def down_there(e, t, slot):
            e.wait_ge(f.down_in[slot], (t // 2 + 1) * 32)

        @block.sync
        def _(sp):
            def expert(t):
                return sp.value_load(r.expert[0:1, bass.ds(t, 1)], min_val=0, max_val=EXPERTS - 1)

            def load_rows(t, slot):
                sp.wait_ge(f.turns, free(t))
                sp.dma_start(f.rows[:, slot, :], k.routed_in[bass.ds(t * P, P), :]).then_inc(f.rows_in[slot], 16)

            def load_up(t, slot):
                n, s = expert(t), f.up_in[slot]
                sp.wait_ge(f.gelus, free(t))
                sp.dma_start(f.w1[:, slot], w["W1"][bass.ds(n, 1)].rearrange("a (p b) n -> p (a b) n", b=2)).then_inc(s, 16)
                sp.dma_start(f.b1[:, slot, :], w["b1"][bass.ds(n, 1)].rearrange("a (p j) -> p (a j)", p=P)).then_inc(s, 16)
                if norm:
                    for tile, n_ in ((f.g, "ln_g"), (f.b, "ln_b")):
                        sp.dma_start(tile[:, slot, :], w[n_][bass.ds(n, 1)].rearrange("a (p b) -> p (a b)", b=2)).then_inc(s, 16)

            def load_down(t, slot):
                n, s = expert(t), f.down_in[slot]
                sp.wait_ge(f.taken, free(t))
                sp.dma_start(f.w2[:, slot], w["W2"][bass.ds(n, 1)].rearrange("a (p j) n -> p (a j) n", p=P)).then_inc(s, 16)
                sp.dma_start(f.b2[:, slot, :], w["b2"][bass.ds(n, 1)].to_broadcast([P, C])).then_inc(s, 16)

            staggered(sp, SLOTS_X, [load_rows, load_up, load_down])

        @block.tensor
        def _(pe):
            ffn_tensor(k, f, pe, SLOTS_X, rows_there, up_there, down_there, True)

        @block.scalar
        def _(act):
            ffn_scalar(k, f, act, SLOTS_X, up_there, True)

        @block.vector
        def _(dve):
            dve.sem_inc(f.taken, 2)

            def take(t, slot):
                down_there(dve, t, slot)
                dve.wait_ge(f.downs, ready(t))
                dve.wait_ge(drained, free(t))
                nc.vector.tensor_tensor(result[:, slot, :], k.ps[6 + slot][:, 0:C], f.b2[:, slot, :], ALU.add).then_inc(f.taken, 1)
            staggered(dve, SLOTS_X, [turned_copy(k, f, dve, up_there, True, norm), None, take])

        @block.gpsimd
        def _(pool):
            pool.sem_inc(drained, 2)

            def store(t, slot):
                pool.wait_ge(f.taken, ready(t))
                pool.dma_start(k.routed_out[bass.ds(t * P, P), :], result[:, slot, :]).then_inc(stored, 16)
                pool.wait_ge(stored, (t + 1) * 16)
                pool.sem_inc(drained, 1)
            sweep(pool, SLOTS_X, store)


def phase_combine(k, name, r):
    nc = k.nc
    RING = 8
    with Phase(k, name) as ph:
        got = ph.sb("got", [P, RING, C])
        gathered = [ph.sem(f"gathered{i}") for i in range(RING)]
        added = ph.sem("added")
        block = ph.block()
        steps = [(t, j) for t in range(TILES) for j in range(2)]

        @block.gpsimd
        def _(pool):
            for i, (t, j) in enumerate(steps):
                m = P if t < TILES - 1 else LAST
                if i >= RING:
                    pool.wait_ge(added, i - RING + 1)
                nc.gpsimd.indirect_dma_start(got[0:m, i % RING, :], None, k.routed_out,
                                             bass.IndirectOffsetOnAxis(ap=r.place[0:m, t, j:j + 1], axis=0)
                                             ).then_inc(gathered[i % RING], 16)

        @block.vector
        def _(dve):
            for i, (t, j) in enumerate(steps):
                m = P if t < TILES - 1 else LAST
                dve.wait_ge(gathered[i % RING], 16 * (i // RING + 1))
                if i:
                    dve.wait_ge(added, i)
                nc.vector.scalar_tensor_tensor(k.x[0:m, t, :], got[0:m, i % RING, :], r.share[0:m, t, j:j + 1], k.x[0:m, t, :],
                                               ALU.mult, ALU.add).then_inc(added, 1)


def routed_layer(k, name, prefix, wg, bg, norm, first, rstd, shift):
    with ExitStack() as ctx:
        r = Route(k, ctx, name)
        phase_norm(k, name + "_norm", k.x, 1e-5, rstd, shift)
        phase_gate(k, name + "_gate", r, wg, bg, rstd, shift)
        phase_route(k, name + "_route", r, first)
        phase_experts(k, name + "_experts", r, prefix, norm)
        phase_combine(k, name + "_combine", r)



class Spans:

    def __init__(self, k, ctx):
        def sb(n, shape):
            return ctx.enter_context(k.nc.sbuf_tensor(f"span_{n}", shape, BF16))
        self.prev = sb("prev", [P, BLK, P])
        self.next = sb("next", [P, BLK, P])
        self.head = sb("head", [P, BLK, P])
        self.tail = sb("tail", [P, BLK, P])
        self.in_item = sb("in_item", [P, BLK, P])
        self.carry = sb("carry", [4, SUBP + 1])
        self.down = sb("down", [4, SUBP])
        self.up = sb("up", [4, SUBP])


def phase_spans(k, s):
    nc = k.nc
    with Phase(k, "spans") as ph:
        key, off = ph.sb("key", [P, BLK, P]), ph.sb("off", [P, BLK, P])
        first_next = ph.sb("first_next", [P, BLK])
        first, last_ = ph.sb("first", [4, SUBP + 1]), ph.sb("last", [4, SUBP + 1])
        same, low = ph.sb("same", [P, BLK, P]), ph.sb("low", [P, BLK, P])
        loaded, link, flagged, turned = ph.sem("loaded"), ph.sem("link"), ph.sem("flagged"), ph.sem("turned")
        block = ph.block()

        @block.sync
        def _(sp):
            with nc.allow_non_contiguous_dma(reason="one key of each edge tile"):
                sp.dma_start(key[:], k.key_rows[0:SUBP, :].rearrange("(b p) e -> p b e", p=P)).then_inc(loaded, 16)
                sp.dma_start(off[:], k.off_rows.rearrange("(b p) e -> p b e", p=P)).then_inc(loaded, 16)
                for b in range(BLK):
                    sp.dma_start(first_next[:, b:b + 1], k.key_rows[b * P + 1:(b + 1) * P + 1, 0:1]).then_inc(loaded, 16)
                for tile, col in ((first, 0), (last_, P - 1)):
                    for h in range(4):
                        sp.dma_start(tile[h:h + 1, :], k.key_rows[:, col:col + 1].rearrange("r o -> o r")).then_inc(loaded, 16)
            sp.wait_ge(loaded, 16 * (2 + BLK + 8))

        @block.vector
        def _(dve):
            v, c = nc.vector, Chain(dve, link)
            dve.wait_ge(loaded, 16 * (2 + BLK + 8))

            def penalty(dst, flag):
                c(v.tensor_scalar(dst, flag, 1.0, BIG, ALU.subtract, ALU.mult))

            c(v.memset(same[:, :, 0:1], 0.0))
            c(v.tensor_tensor(same[:, :, 1:P], key[:, :, 1:P], key[:, :, 0:P - 1], ALU.is_equal))
            penalty(s.prev[:], same[:])
            c(v.tensor_tensor(same[:, :, 0:P - 1], key[:, :, 1:P], key[:, :, 0:P - 1], ALU.is_equal))
            c(v.memset(same[:, :, P - 1:P], 0.0))
            penalty(s.next[:], same[:])
            c(v.tensor_tensor(same[:, :, P - 1], key[:, :, P - 1], first_next[:], ALU.is_equal))
            c(v.tensor_scalar(same[:], same[:], -1.0, 1.0, ALU.mult, ALU.add))
            c(v.tensor_scalar(low[:], off[:], 0.0, None, ALU.is_ge))
            c(v.tensor_scalar(off[:], off[:], float(P), None, ALU.is_lt))
            c(v.tensor_tensor(low[:], low[:], off[:], ALU.mult))
            penalty(s.in_item[:], low[:])
            c(v.tensor_tensor(same[:], same[:], low[:], ALU.mult))
            dve.sem_inc(flagged, 1)
            for b in range(BLK):
                c(v.tensor_scalar(off[:, b, :], key[:, b, :], key[:, b, 0:1], None, ALU.is_equal))
                c(v.tensor_scalar(low[:, b, :], key[:, b, :], key[:, b, P - 1:P], None, ALU.is_equal))
            penalty(s.head[:], off[:])
            penalty(s.tail[:], low[:])
            c(v.tensor_tensor(s.carry[:, 1:SUBP + 1], first[:, 1:SUBP + 1], last_[:, 0:SUBP], ALU.is_equal))
            c(v.memset(s.carry[:, 0:1], 0.0))
            c(v.memset(s.carry[:, SUBP:SUBP + 1], 0.0))
            penalty(s.carry[:], s.carry[:])
            c(v.tensor_tensor(first[:], first[:], last_[:], ALU.is_equal))
            penalty(first[:], first[:])
            c(v.tensor_tensor(s.down[:], s.carry[:, 0:SUBP], first[:, 0:SUBP], ALU.add))
            c(v.tensor_tensor(s.up[:], s.carry[:, 1:SUBP + 1], first[:, 0:SUBP], ALU.add))
            dve.wait_ge(turned, 1)
            v.tensor_copy(k.is_last[:], k.ps[0][:, 0:SUBP])

        @block.tensor
        def _(pe):
            pe.wait_ge(flagged, 1)
            for b in range(BLK):
                mm = nc.tensor.transpose(k.ps[0][:, b * P:(b + 1) * P], same[:, b, :], k.ident[:])
            mm.then_inc(turned, 1)


class Gat:

    def __init__(self, buf, n, heads, width, table):
        self.n, self.H, self.D, self.table = n, heads, width, table
        self.W = heads * (width + 1)
        self.of_node = buf["of_node"][:, 0:2 * heads, :]
        self.of_src = buf["of_src"][:, 0:heads, :]
        self.of_dst = buf["shared"][:, 0:2 * heads * SUBP].rearrange("p (h e) -> p h e", e=SUBP)
        ring = 8 if heads == 1 else 4
        self.rows = buf["shared"][:, 0:ring * 2 * self.W].rearrange("p (r s w) -> p r s w", s=2, w=self.W)
        self.last_max = buf["last_max"][:, :, 0:heads + 1]
        self.own = buf["own"][:, 0:heads, :]
        self.inv = buf["inv"][:, 0:heads, :]

    @staticmethod
    def buffers(k, ctx, heads):
        shapes = {"of_node": [P, 2 * heads, TILES], "of_src": [P, heads, SUBP], "shared": [P, max(2 * heads * SUBP, 8 * ACCW)],
                  "last_max": [P, SUBS, heads + 1], "own": [P, heads, TILES], "inv": [P, heads, TILES]}
        return {n: ctx.enter_context(k.nc.sbuf_tensor(f"gat_{n}", s, F32)) for n, s in shapes.items()}


def phase_gat_dense(k, g, kb, w, a_src, a_dst, stage, per_stage, sb, loads):
    nc = k.nc
    H, D = g.H, g.D
    with ExitStack() as ctx:
        wt = ctx.enter_context(nc.sbuf_tensor(f"gat{g.n}_w", [P, kb, H * D], F32))
        wa = ctx.enter_context(nc.sbuf_tensor(f"gat{g.n}_wa", [P, kb, 2 * H], F32))
        with Phase(k, f"gat{g.n}_wa") as ph:
            av = ph.sb("av", [P, 2, H * D])
            prod = ph.sb("prod", [P, H * D])
            loaded, link = ph.sem("loaded"), ph.sem("link")
            block = ph.block()

            @block.sync
            def _(sp):
                sp.dma_start(wt[:], weights(w)).then_inc(loaded, 16)
                for i, vec in enumerate((a_src, a_dst)):
                    sp.dma_start(av[:, i, :], wide(vec.rearrange("h d -> (h d)"))).then_inc(loaded, 16)
                sp.wait_ge(loaded, 48)

            @block.vector
            def _(dve):
                v, c = nc.vector, Chain(dve, link)
                dve.wait_ge(loaded, 48)
                for b in range(kb):
                    for i in range(2):
                        c(v.tensor_tensor(prod[:], wt[:, b, :], av[:, i, :], ALU.mult))
                        c(v.tensor_reduce(wa[:, b, i * H:(i + 1) * H], prod[:].rearrange("p (h d) -> p h d", d=D), AX.X, ALU.add))

        def evac(ph, t, slot, ps, c):
            v = nc.vector
            apart(ph, c.eng)
            node = k.h[:, bass.ds(t, 1), 0:g.W].rearrange("p a (h d) -> p (a h) d", d=D + 1)
            v.tensor_copy(node[:, :, 0:D], ps[0][:, 0:H * D].rearrange("p (h d) -> p h d", d=D))
            v.tensor_copy(node[:, :, D], k.ones[:, 0:H])
            return v.tensor_copy(g.of_node[:, :, bass.ds(t, 1)].rearrange("p h a -> p (h a)"), ps[1][:, 0:2 * H])

        phase_dense(k, f"gat{g.n}", kb, [(wt, H * D), (wa, 2 * H)], stage, per_stage, evac, 0, sb=sb, loads=loads,
                    exps="neg" if per_stage else None,
                    stores=tile_stores(g.table, k.h, g.W))


def phase_gat_scores(k, g):
    nc, H = k.nc, g.H
    RING = 8
    HT = H * TILES
    with Phase(k, f"gat{g.n}_scores") as ph:
        rows = ph.sb("rows", [P, 2, 2, 4 * 256], BF16)
        hot = ph.sb("hot", [P, 4, 2, 256], BF16)
        parts = ph.sb("parts", [P, 3, 2 * HT], BF16)
        of_item = ph.sb("of_item", [P, 4, 3, 2 * H], BF16)
        rest = ph.sb("rest", [P, 2 * HT])
        tile_hot = ph.sb("tile_hot", [P, 2, 8, TILES])
        picked = ph.sb("picked", [P, 2, 2, H, TILES])
        row_in = [ph.sem(f"row_in{s}") for s in range(2)]
        hots, chosen, made, masked, picks, dst_taken, cut, link = (
            ph.sem(s) for s in ("hots", "chosen", "made", "masked", "picks", "dst_taken", "cut", "link"))
        block = ph.block()
        bank, dst_bank = k.ps[0:4], k.ps[4:8]

        @block.sync
        def _(sp):
            load_batches(sp, hots, 4, [(k.src_rows, rows[:, 0]), (k.dst_rows, rows[:, 1])], row_in)

        @block.gpsimd
        def _(pool):
            pool.sem_inc(chosen, 4)
            pool.wait_ge(cut, 1)

            def choose(t, r, i):
                n = pool.value_load(k.item_tile[0:1, bass.ds(t, 1)], min_val=0, max_val=TILES - 1)
                pool.wait_ge(made, free(t))
                apart(ph, pool)
                nc.gpsimd.tensor_copy(of_item[:, r % 4, :, :],
                                      parts[:].rearrange("p c (h t) -> p c h t", t=TILES)[:, :, :, bass.ds(n, 1)]
                                      .rearrange("p c h a -> p c (h a)")).then_inc(chosen, 1)
            ringed(pool, ITEMS, RING, [choose])

        @block.tensor
        def _(pe):
            pe.sem_inc(made, 4)
            pe.wait_ge(cut, 1)

            def products(t, r, i):
                slot = r % 4
                pe.wait_ge(hots, ready(t, 4))
                pe.wait_ge(chosen, ready(t, 4))
                pe.wait_ge(masked, free(t))
                pe.wait_ge(dst_taken, free(t))
                for s in range(2):
                    for p in range(3):
                        nc.tensor.matmul(bank[slot][:, s * HT:(s + 1) * HT], hot[:, slot, 0, s * P:(s + 1) * P],
                                         parts[:, p, 0:HT], start=(p == 0), stop=(p == 2))
                for s in range(2):
                    for p in range(3):
                        mm = nc.tensor.matmul(dst_bank[slot][:, s * 2 * H:(s + 1) * 2 * H],
                                              hot[:, slot, 1, s * P:(s + 1) * P],
                                              of_item[:, slot, p, :], start=(p == 0), stop=(p == 2))
                mm.then_inc(made, 1)
            ringed(pe, ITEMS, RING, [products])

        @block.scalar
        def _(act):
            act.sem_inc(dst_taken, 4)

            def take(t, r, i):
                act.wait_ge(made, ready(t, 4))
                act.copy(g.of_dst[:, :, bass.ds(2 * t, 2)],
                         dst_bank[r % 4][:, 0:4 * H].rearrange("p (s h) -> p h s", s=2)).then_inc(dst_taken, 1)
            ringed(act, ITEMS, RING, [take])

        @block.vector
        def _(dve):
            v, c = nc.vector, Chain(dve, link)
            dve.sem_inc(hots, 4)
            dve.sem_inc(masked, 4)
            dve.sem_inc(picks, 2)
            v.memset(g.of_src[:, :, SUBS:SUBP], 0.0)
            v.memset(g.of_dst[:, :, SUBS:SUBP], 0.0)
            flat = g.of_node.rearrange("p h t -> p (h t)")
            c(v.tensor_copy(parts[:, 0, :], flat))
            c(v.tensor_tensor(rest[:], flat, parts[:, 0, :], ALU.subtract))
            c(v.tensor_copy(parts[:, 1, :], rest[:]))
            c(v.tensor_tensor(rest[:], rest[:], parts[:, 1, :], ALU.subtract))
            v.tensor_copy(parts[:, 2, :], rest[:]).then_inc(cut, 1)

            def one_hots(t, r, i):
                dve.wait_ge(row_in[r // 4], (i + 1) * 32)
                dve.wait_ge(made, free(t))
                if r % 4 == 0:
                    v.tensor_tensor(tile_hot[:, r // 4], k.iota_row[:, 0:TILES].rearrange("p (a n) -> p a n", a=1).to_broadcast([P, 8, TILES]),
                                    k.src_hi[:, bass.ds(2 * t, 8)].rearrange("p (s a) -> p s a", a=1).to_broadcast([P, 8, TILES]),
                                    ALU.is_equal)
                v.tensor_scalar(hot[:, r % 4, :, :], rows[:, :, r // 4, r % 4 * 256:(r % 4 + 1) * 256], k.iota_p[:, 0:1], None,
                                ALU.is_equal).then_inc(hots, 1)

            def mask(t, r, i):
                dve.wait_ge(hots, ready(t, 4))
                dve.wait_ge(made, ready(t, 4))
                dve.wait_ge(picks, free(t))
                v.tensor_tensor(picked[:, r % 2], bank[r % 4][:, 0:2 * HT].rearrange("p (s h n) -> p s h n", s=2, h=H),
                                tile_hot[:, r // 4, r % 4 * 2:r % 4 * 2 + 2].rearrange("p s (a n) -> p s a n", a=1).to_broadcast([P, 2, H, TILES]), ALU.mult
                                ).then_inc(masked, 1)

            def pick(t, r, i):
                dve.wait_ge(masked, ready(t, 4))
                v.tensor_reduce(g.of_src[:, :, bass.ds(2 * t, 2)].rearrange("p h s -> p s h"), picked[:, r % 2], AX.X, ALU.add
                                ).then_inc(picks, 1)

            ringed(dve, ITEMS, RING, [one_hots, None, mask, pick])


def phase_gat_softmax(k, g, s):
    nc, H = k.nc, g.H
    with Phase(k, f"gat{g.n}_softmax") as ph:
        run, back = ph.sb("run", [P, H, BLK, P]), ph.sb("back", [P, H, BLK, P])
        ends, into = ph.sb("ends", [4, SUBP]), ph.sb("into", [4, SUBP])
        cin = ph.sb("cin", [P, BLK, H])
        turned, masked, scanned, ends_in, carried, cins, passed, back_out, taken, shifted, exped, link = (
            ph.sem(n) for n in ("turned", "masked", "scanned", "ends_in", "carried", "cins", "passed", "back_out", "taken",
                                "shifted", "exped", "link"))
        z = back[:].rearrange("p h b e -> p h (b e)")
        block = ph.block()

        @block.tensor
        def _(pe):
            for h in range(H):
                for b in range(BLK):
                    mm = nc.tensor.transpose(k.ps[h][:, b * P:(b + 1) * P], g.of_src[:, h, b * P:(b + 1) * P], k.ident[:])
                mm.then_inc(turned, 1)
            for way, (data, col) in enumerate(((run, P - 1), (back, 0))):
                pe.wait_ge(scanned, way + 1)
                for b in range(BLK):
                    mm = nc.tensor.transpose(k.ps[4][0:H, b * P:(b + 1) * P], data[:, :, b, col], k.ident[:])
                mm.then_inc(ends_in, 1)
                pe.wait_ge(carried, way + 1)
                for b in range(BLK):
                    mm = nc.tensor.transpose(k.ps[5][:, b * H:(b + 1) * H], into[0:H, b * P:(b + 1) * P], k.ident[0:H, 0:H])
                mm.then_inc(cins, 1)
            pe.wait_ge(passed, 1)
            for h in range(H):
                for b in range(BLK):
                    mm = nc.tensor.transpose(k.ps[h][:, b * P:(b + 1) * P], back[:, h, b, :], k.ident[:])
                mm.then_inc(back_out, 1)

        @block.gpsimd
        def _(pool):
            nc.gpsimd.memset(k.acc[:, :, 0:g.W + H + 1], 0.0)

        @block.scalar
        def _(act):
            act.wait_ge(shifted, 1)
            act.activation(g.of_src[:], z, ACT.Exp).then_inc(exped, 1)

        @block.vector
        def _(dve):
            v, c = nc.vector, Chain(dve, link)

            def flat(a):
                return a.rearrange("p b e -> p (b e)")

            for h in range(H):
                dve.wait_ge(turned, h + 1)
                c(v.tensor_tensor(flat(back[:, h]), k.ps[h][:, 0:SUBP], flat(s.in_item[:]), ALU.add))
                c.mark(v.tensor_tensor_scan(flat(run[:, h]), flat(s.prev[:]), flat(back[:, h]), -BIG, ALU.add, ALU.max))
            c.wait()
            dve.sem_inc(scanned, 1)
            dve.wait_ge(ends_in, 1)
            c(v.tensor_tensor_scan(ends[0:H, :], s.down[0:H, :], k.ps[4][0:H, 0:SUBP], -BIG, ALU.add, ALU.max))
            c.mark(v.memset(into[0:H, 0:1], -BIG))
            c(v.tensor_tensor(into[0:H, 1:SUBP], ends[0:H, 0:SUBP - 1], s.carry[0:H, 1:SUBP], ALU.add))
            dve.sem_inc(carried, 1)
            dve.wait_ge(cins, 1)
            c(v.tensor_copy(cin[:], k.ps[5][:, 0:BLK * H].rearrange("p (b h) -> p b h", h=H)))
            for h in range(H):
                for b in range(BLK):
                    c.mark(v.scalar_tensor_tensor(run[:, h, b, :], s.head[:, b, :], cin[:, b, h:h + 1], run[:, h, b, :],
                                                  ALU.add, ALU.max))
            c.wait()
            for h in range(H):
                c.mark(v.tensor_tensor_scan(flat(back[:, h])[:, ::-1], flat(s.next[:])[:, ::-1], flat(run[:, h])[:, ::-1], -BIG,
                                            ALU.add, ALU.max))
            c.wait()
            dve.sem_inc(scanned, 1)
            dve.wait_ge(ends_in, 2)
            c(v.tensor_tensor_scan(ends[0:H, ::-1], s.up[0:H, ::-1], k.ps[4][0:H, 0:SUBP][:, ::-1], -BIG, ALU.add, ALU.max))
            c.mark(v.memset(into[0:H, SUBP - 1:SUBP], -BIG))
            c(v.tensor_tensor(into[0:H, 0:SUBP - 1], ends[0:H, 1:SUBP], s.carry[0:H, 1:SUBP], ALU.add))
            dve.sem_inc(carried, 1)
            dve.wait_ge(cins, 2)
            c(v.tensor_copy(cin[:], k.ps[5][:, 0:BLK * H].rearrange("p (b h) -> p b h", h=H)))
            for h in range(H):
                for b in range(BLK):
                    c.mark(v.scalar_tensor_tensor(back[:, h, b, :], s.tail[:, b, :], cin[:, b, h:h + 1], back[:, h, b, :],
                                                  ALU.add, ALU.max))
            c.wait()
            dve.sem_inc(passed, 1)
            top, al_s, al_d = run[:].rearrange("p h b e -> p h (b e)"), g.of_dst[:, 0:H, :], g.of_dst[:, H:2 * H, :]
            for h in range(H):
                dve.wait_ge(back_out, h + 1)
                c(v.tensor_tensor(top[:, h, :], k.ps[h][:, 0:SUBP], al_s[:, h, :], ALU.max))
                c(v.tensor_tensor(g.last_max[:, :, h], top[:, h, 0:SUBS], k.is_last[:, 0:SUBS], ALU.mult))
            c(v.tensor_copy(g.last_max[:, :, H], k.is_last[:, 0:SUBS]))
            c(v.tensor_tensor(top, top, al_d, ALU.add))
            c(v.scalar_tensor_tensor(top, top, 0.2, top, ALU.mult, ALU.max))
            c(v.tensor_tensor(z, g.of_src[:], al_d, ALU.add))
            c(v.scalar_tensor_tensor(z, z, 0.2, z, ALU.mult, ALU.max))
            c(v.tensor_tensor(z, z, top, ALU.subtract))
            v.tensor_scalar(z, z, 0.0, None, ALU.min).then_inc(shifted, 1)


def phase_gat_edges(k, g):
    nc, H, D = k.nc, g.H, g.D
    S = 4
    RING = 2 * S if H == 1 else S
    by_act = H * 3 // 4
    lo_heads = max(1, H // 2)
    A = lo_heads * (D + 1)
    B = g.W - A + H + 1
    with Phase(k, f"gat{g.n}_edges") as ph:
        rows = [g.rows[:, r] for r in range(RING)]
        index = ph.sb("index", [P, RING, 2], I32)
        hot = ph.sb("hot", [P, S, 2, H + 1, P])
        indexed = ph.sem("indexed")
        gathered = [ph.sem(f"gathered{r}") for r in range(RING)]
        bare, weighed, scaled, summed, added = (ph.sem(n) for n in ("bare", "weighed", "scaled", "summed", "added"))
        psa, psb = k.ps[0:S], k.ps[S:2 * S]
        block = ph.block()

        @block.gpsimd
        def _(pool):
            with pool.Fori(0, ITEMS // RING) as i:
                for r in range(RING):
                    pool.wait_ge(indexed, i * RING + r + 1)
                    apart(ph, pool)
                    for s in range(2):
                        nc.gpsimd.indirect_dma_start(rows[r][:, s, :], None, g.table,
                                                     bass.IndirectOffsetOnAxis(ap=index[:, r, s:s + 1], axis=0)
                                                     ).then_inc(gathered[r], 16)

        @block.scalar
        def _(act):
            act.sem_inc(scaled, S)

            def scale(t, r, i):
                slot = r % S
                act.wait_ge(bare, ready(t, S))
                act.wait_ge(summed, free(t))
                for s in range(2):
                    for h in range(H - by_act, H):
                        last = act.mul(hot[:, slot, s, h, :], hot[:, slot, s, H, :],
                                       g.of_src[:, h, bass.ds(2 * t + s, 1)])
                last.then_inc(scaled, 1)
            if by_act:
                ringed(act, ITEMS, RING, [scale])

        @block.tensor
        def _(pe):
            pe.sem_inc(summed, S)

            def sums(t, r, i):
                slot = r % S
                pe.wait_ge(gathered[r], (i + 1) * 32)
                pe.wait_ge(weighed, ready(t, S))
                if by_act:
                    pe.wait_ge(scaled, ready(t, S))
                pe.wait_ge(added, free(t))
                for h in range(H):
                    out = psa[slot][:, h * (D + 1):(h + 1) * (D + 1)] if h < lo_heads else \
                        psb[slot][:, (h - lo_heads) * (D + 1):(h - lo_heads + 1) * (D + 1)]
                    for s in range(2):
                        nc.tensor.matmul(out, hot[:, slot, s, h, :], rows[r][:, s, h * (D + 1):(h + 1) * (D + 1)],
                                         start=(s == 0), stop=(s == 1))
                for s in range(2):
                    mm = nc.tensor.matmul(psb[slot][:, B - H - 1:B], hot[:, slot, s, H, :],
                                          g.last_max[:, bass.ds(2 * t + s, 1), :].rearrange("p a h -> p (a h)"),
                                          start=(s == 0), stop=(s == 1))
                mm.then_inc(summed, 1)

            ringed(pe, ITEMS, RING, [sums])

        @block.vector
        def _(dve):
            v = nc.vector
            for n in (bare, weighed, added):
                dve.sem_inc(n, S)

            def stage_index(t, r):
                v.tensor_copy(index[:, r, :], k.src_of[:, bass.ds(2 * t, 2)]).then_inc(indexed, 1)

            def one_hots(t, r, i):
                slot = r % S
                dve.wait_ge(summed, free(t))
                dve.wait_ge(scaled, free(t)) if by_act else None
                for s in range(2):
                    last = v.tensor_scalar(hot[:, slot, s, H, :], k.iota_row[:, 0:P], k.dst_in[:, bass.ds(2 * t + s, 1)],
                                           None, ALU.is_equal)
                last.then_inc(bare, 1)
                for s in range(2):
                    for h in range(H - by_act):
                        last = v.tensor_scalar(hot[:, slot, s, h, :], k.iota_row[:, 0:P], k.dst_in[:, bass.ds(2 * t + s, 1)],
                                               g.of_src[:, h, bass.ds(2 * t + s, 1)], ALU.is_equal, ALU.mult)
                last.then_inc(weighed, 1)

            def add(t, r, i):
                slot = r % S
                n = dve.value_load(k.item_tile[0:1, bass.ds(t, 1)], min_val=0, max_val=TILES - 1)
                dve.wait_ge(summed, ready(t, S))
                stage_index(t + RING, r)
                dve.wait_ge(added, t + S)
                v.tensor_tensor(row(k.acc, n, 0, A), row(k.acc, n, 0, A), psa[slot][:, 0:A], ALU.add)
                v.tensor_tensor(row(k.acc, n, A, A + B), row(k.acc, n, A, A + B), psb[slot][:, 0:B], ALU.add
                                ).then_inc(added, 1)

            for r in range(RING):
                stage_index(r, r)
            ringed(dve, ITEMS, RING, [one_hots, None, add])


def phase_gat_nodes(k, g):
    nc, H, D = k.nc, g.H, g.D
    with Phase(k, f"gat{g.n}_nodes") as ph:
        alone = ph.sb("alone", [P, 1, TILES])
        top, e = (ph.sb(n, [P, 4, TILES])[:, 0:H, :] for n in ("top", "e"))
        link, shifted, exped = ph.sem("link"), ph.sem("shifted"), ph.sem("exped")
        block = ph.block()

        @block.scalar
        def _(act):
            act.wait_ge(shifted, 1)
            act.activation(g.own[:], e, ACT.Exp).then_inc(exped, 1)

        @block.vector
        def _(dve):
            v, c = nc.vector, Chain(dve, link)
            acc = k.acc[:].rearrange("p t w -> p w t")
            al_s, al_d = g.of_node[:, 0:H, :], g.of_node[:, H:2 * H, :]
            c(v.tensor_scalar(alone[:], acc[:, g.W + H:g.W + H + 1, :], -1.0, 1.0, ALU.mult, ALU.add))
            c(v.tensor_tensor(top, al_s, alone[:].to_broadcast([P, H, TILES]), ALU.mult))
            c(v.tensor_tensor(top, top, acc[:, g.W:g.W + H, :], ALU.add))
            c(v.tensor_tensor(top, top, al_s, ALU.max))
            c(v.tensor_tensor(top, top, al_d, ALU.add))
            c(v.scalar_tensor_tensor(top, top, 0.2, top, ALU.mult, ALU.max))
            c(v.tensor_tensor(e, al_s, al_d, ALU.add))
            c(v.scalar_tensor_tensor(e, e, 0.2, e, ALU.mult, ALU.max))
            c(v.tensor_tensor(e, e, top, ALU.subtract))
            v.tensor_scalar(e, e, 0.0, None, ALU.min).then_inc(shifted, 1)
            dve.wait_ge(exped, 1)
            c(v.tensor_tensor(top, g.own[:], acc[:, D:g.W:D + 1, :], ALU.add))
            c(v.tensor_scalar(top, top, 1e-16, None, ALU.add))
            v.reciprocal(g.inv[:], top)


def stage_attended(k, g, elu):
    nc, H, D = k.nc, g.H, g.D

    def stage(ph, t, slot, dst, c):
        v, part = nc.vector, ph.buf["part"]
        out = part[:, slot, :] if elu else dst
        for h in range(H):
            a, b = h * (D + 1), h * (D + 1) + D
            c.mark(v.scalar_tensor_tensor(part[:, slot, h * D:(h + 1) * D], row(k.h, t, a, b), g.own[:, h, bass.ds(t, 1)],
                                          row(k.acc, t, a, b), ALU.mult, ALU.add))
        c.wait()
        for h in range(H):
            last = v.scalar_tensor_tensor(out[:, h * D:(h + 1) * D], part[:, slot, h * D:(h + 1) * D], g.inv[:, h, bass.ds(t, 1)],
                                          ph.buf["bias"][:, h * D:(h + 1) * D], ALU.mult, ALU.add)
            if elu:
                c.mark(last)
        if not elu:
            return last
        c.wait()
        neg = ph.buf["neg"]
        v.tensor_scalar(neg[:, slot, :], out, 0.0, None, ALU.min).then_inc(ph.capped, 1)
        c(v.tensor_scalar(out, out, 0.0, -1.0, ALU.max, ALU.add))
        c.eng.wait_ge(ph.exped, t + 1)
        return v.tensor_tensor(dst, out, neg[:, slot, :], ALU.add)
    return stage


def phase_mlp(k, g):
    nc, a = k.nc, k.ins
    HIDDEN2 = a["L1_gnn_M2"].shape[1]

    def relu_to_h(width):
        def evac(ph, t, slot, ps, c):
            tmp = ph.buf["tmp"]
            c(nc.vector.tensor_tensor(tmp[:, slot, :], ps[0][:, 0:width], ph.buf["mb"][:], ALU.add))
            return nc.vector.tensor_scalar(row(k.h, t, 0, width), tmp[:, slot, :], 0.0, None, ALU.max)
        return evac

    def stage_h(width):
        def stage(ph, t, slot, dst, c):
            return nc.vector.tensor_copy(dst, row(k.h, t, 0, width))
        return stage

    def add_to_x(ph, t, slot, ps, c):
        tmp = ph.buf["tmp"]
        c(nc.vector.tensor_tensor(tmp[:, slot, :], ps[0][:, 0:C], ph.buf["mb"][:], ALU.add))
        return nc.vector.tensor_tensor(row(k.x, t, 0, C), row(k.x, t, 0, C), tmp[:, slot, :], ALU.add)

    def bufs(kb, width):
        return [("w", [P, kb, width], F32), ("mb", [P, width], F32), ("tmp", [P, 2, width], F32)]

    phase_dense(k, "mlp1", 2, [("w", 2 * P)], stage_attended(k, g, False), 1, relu_to_h(2 * P), 1,
                sb=bufs(2, 2 * P) + [("part", [P, 2, C], F32), ("bias", [P, C], F32)],
                loads=[("w", weights(a["L1_gnn_M1"])), ("mb", wide(a["L1_gnn_mb1"])), ("bias", wide(a["L1_gnn_b3"]))])
    phase_dense(k, "mlp2", 2, [("w", HIDDEN2)], stage_h(2 * P), 0, relu_to_h(HIDDEN2), 1, sb=bufs(2, HIDDEN2),
                loads=[("w", weights(a["L1_gnn_M2"])), ("mb", wide(a["L1_gnn_mb2"]))])
    phase_dense(k, "mlp3", 1, [("w", C)], stage_h(HIDDEN2), 0, add_to_x, 1, sb=bufs(1, C),
                loads=[("w", weights(a["L1_gnn_M3"])), ("mb", wide(a["L1_gnn_mb3"]))])


def attention_layers(k, rstd, shift):
    a = k.ins
    heads, width = a["L1_gnn_a_src1"].shape
    with ExitStack() as ctx:
        s = Spans(k, ctx)
        buf = Gat.buffers(k, ctx, heads)
        phase_spans(k, s)
        phase_norm(k, "norm2", k.x, 1e-5, rstd, shift)
        stage, per, sb, loads, kb = stage_normed(k, k.x, rstd, shift), 0, [], [], C // P
        for n, H, D, table in ((1, heads, width, k.h_table), (2, heads, width, k.h_table), (3, 1, C, k.h_table3)):
            g = Gat(buf, n, H, D, table)
            phase_gat_dense(k, g, kb, a[f"L1_gnn_W{n}"], a[f"L1_gnn_a_src{n}"], a[f"L1_gnn_a_dst{n}"], stage, per, sb, loads)
            phase_gat_scores(k, g)
            phase_gat_softmax(k, g, s)
            phase_gat_edges(k, g)
            phase_gat_nodes(k, g)
            stage, per, kb = stage_attended(k, g, True), 2 * H + 1, H * D // P
            sb = [("part", [P, 2, H * D], F32), ("neg", [P, 2, H * D], F32), ("bias", [P, H * D], F32)]
            loads = [("bias", wide(a[f"L1_gnn_b{n}"]))]
        phase_mlp(k, g)


def phase_output(k):
    nc = k.nc
    with Phase(k, "output") as ph:
        stored = ph.sem("stored")
        block = ph.block()

        @block.sync
        def _(sp):
            full = (TILES - 1) * P
            sp.dma_start(k.out[0:full, :].rearrange("(t p) c -> p t c", p=P), k.x[:, 0:TILES - 1, :]).then_inc(stored, 16)
            sp.dma_start(k.out[full:N, :], k.x[0:LAST, TILES - 1, :]).then_inc(stored, 16)
            sp.wait_ge(stored, 32)


def run_phases(k, stop=None):
    phase_constants(k)
    phase_items(k)
    rstd, shift = k.sb("rstd", [P, TILES], F32), k.sb("shift", [P, TILES], F32)
    phase_norm(k, "norm0", k.x, 1e-5, rstd, shift)
    if stop != "skip0":
        phase_qkv(k, rstd, shift)
        phase_attention_edges(k)
        phase_attention_out(k, rstd, shift)
        phase_norm(k, "norm1", k.h, 1e-5, rstd, shift)
        phase_node_ffn(k, rstd, shift)
        routed_layer(k, "moe0", "L0_ffn", k.ins["L0_ffn_Wg"], k.ins["L0_ffn_bg"], False, True, rstd, shift)
    attention_layers(k, rstd, shift)
    if stop != "skip0":
        routed_layer(k, "moe1", "L1_ffn", k.ins["L1_ffn_Wr"], k.ins["L1_ffn_br"], True, False, rstd, shift)
        phase_output(k)


_OUT_SHAPE = (N, C)


def program(nc, ins, out, stop=None):
    with ExitStack() as ctx:
        k = Kit(nc, ctx, ins, out)
        run_phases(k, stop)


def host_arrays(inputs):
    import numpy as _np
    a = {n: _np.ascontiguousarray(v) for n, v in inputs.items()}
    for n in ("Wq", "Wk", "Wv", "Wp", "W1", "W2"):
        a["L0_gnn_" + n] = _np.ascontiguousarray(a["L0_gnn_" + n].T)
    a["L0_gnn_Wkv"] = _np.concatenate([a.pop("L0_gnn_Wk"), a.pop("L0_gnn_Wv")], axis=1)
    a["L0_gnn_bkv"] = _np.concatenate([a.pop("L0_gnn_bk"), a.pop("L0_gnn_bv")])
    return a


def declare(nc, arrays):
    return {n: nc.dram_tensor(f"in_{n}", v.shape, mybir.dt.from_np(v.dtype), kind="ExternalInput").ap()
            for n, v in arrays.items()}


def kernel(**inputs):
    import concourse.bacc as _bacc
    from concourse.bass_utils import run_bass_kernel_spmd as _run

    nc = _bacc.Bacc("TRN2", target_bir_lowering=False, num_devices=1)
    arrays = host_arrays(inputs)
    ins = declare(nc, arrays)
    out = nc.dram_tensor("out_x", _OUT_SHAPE, F32, kind="ExternalOutput").ap()
    program(nc, ins, out)
    r = _run(nc, [{f"in_{n}": v for n, v in arrays.items()}], core_ids=[0])
    return r.results[0]["out_x"]
```

```python
from contextlib import ExitStack

import numpy as np

import concourse.bass as bass
from concourse import mybir

F32, BF16, I32, U32 = mybir.dt.float32, mybir.dt.bfloat16, mybir.dt.int32, mybir.dt.uint32
ALU = mybir.AluOpType
ACT = mybir.ActivationFunctionType
AX = mybir.AxisListType

P = 128
N, C, EDGES = 3125, 256, 53125
TILES = -(-N // P)
LAST = N - (TILES - 1) * P
PAIRS = -(-EDGES // (2 * P))
ITEMS = PAIRS + TILES - 1
SUBS = 2 * ITEMS
SUBP = -(-SUBS // P) * P
BLK = SUBP // P
GB = PAIRS // 2
NOWHERE = 4000
BIG = 1.0e30
HEADS0, HD0 = 8, 32
HID = 1024
EXPERTS = 8
SLOTS_X = (2 * N + EXPERTS * (P - 1)) // P
TABW = 516
ACCW = 524


class Chain:

    def __init__(self, eng, sem):
        self.eng, self.sem, self.base, self.local, self.per, self.start, self.turns = eng, sem, 0, 0, None, 0, 0

    def loop(self, turns, per):
        self.start, self.per, self.turns = self.base + self.local, per, turns
        return self

    def at(self, t):
        self.base, self.local = self.start + t * self.per, 0

    def over(self):
        self.base, self.local = self.start + self.turns * self.per, 0

    def mark(self, ins):
        self.local += 1
        assert self.per is None or self.local <= self.per or isinstance(self.base, int), "chain"
        ins.then_inc(self.sem, 1)

    def wait(self):
        self.eng.wait_ge(self.sem, self.base + self.local)

    def __call__(self, ins):
        self.mark(ins)
        self.wait()

    def full(self):
        assert self.local == self.per, (self.local, self.per)


def apart(ph, eng):
    eng.sem_inc(ph.passes, 1)


def ready(t, slots=2):
    return t + slots + 1


def free(t):
    return t + 1


def sweep(eng, n, step):
    with eng.Fori(0, n // 2) as i:
        step(2 * i, 0)
        step(2 * i + 1, 1)
    if n % 2:
        step(n - 1, 0)


def staggered(eng, n, steps, order=None):
    depth = len(steps) - 1
    order = [j for j in order or range(len(steps)) if steps[j]]

    def turn(base, r, limit):
        for j in order:
            d = r + depth - j
            if 0 <= d < limit:
                steps[j](base + d, d % 2)

    for r in range(-depth, 0):
        turn(0, r, n)
    with eng.Fori(0, (n - depth) // 2) as i:
        turn(2 * i, 0, n)
        turn(2 * i, 1, n)
    done = (n - depth) // 2 * 2
    for r in range(n - done):
        turn(done, r, n - done)


def ringed(eng, n, ring, steps):
    assert n % ring == 0
    depth = len(steps) - 1
    steps = [s if s else (lambda t, r, i: None) for s in steps]

    def turn(base, i, r, limit):
        for j, step in enumerate(steps):
            d = r + depth - j
            if d >= 0 and d < limit:
                step(base + d, d % ring, i + d // ring)

    for r in range(-depth, 0):
        turn(0, 0, r, n)
    with eng.Fori(0, n // ring - 1) as i:
        for r in range(ring):
            turn(i * ring, i, r, n)
    for r in range(ring):
        turn(n - ring, n // ring - 1, r, ring)


class Kit:

    def __init__(self, nc, ctx, ins, out):
        self.nc, self.ctx, self.ins, self.out = nc, ctx, ins, out
        sb, dram = self.sb, self.dram
        self.ps = [ctx.enter_context(nc.psum_tensor(f"ps{i}", [P, 512], F32)) for i in range(8)]
        self.ident = sb("ident", [P, P], F32)
        self.ones = sb("ones", [P, P], F32)
        self.before = sb("before", [P, P], F32)
        self.iota_row = sb("iota_row", [P, 256], F32)
        self.iota_p = sb("iota_p", [P, 1], F32)
        self.x = sb("x", [P, TILES, C], F32)
        self.h = sb("h", [P, TILES, TABW], F32)
        self.acc = sb("acc", [P, TILES, ACCW], F32)
        self.item_tile = sb("item_tile", [1, ITEMS + 8], I32)
        self.src_of = sb("src_of", [P, SUBP], I32)
        self.dst_in = sb("dst_in", [P, SUBP], F32)
        self.src_hi = sb("src_hi", [P, SUBP], F32)
        self.is_last = sb("is_last", [P, SUBP], F32)
        self.dst_rows = dram("dst_rows", [SUBP, P], BF16)
        self.src_rows = dram("src_rows", [SUBP, P], BF16)
        self.key_rows = dram("key_rows", [SUBP + 1, P], F32)
        self.off_rows = dram("off_rows", [SUBP, P], F32)
        self.kv_table = dram("kv_table", [TILES * P, 512], F32)
        self.h_table = dram("h_table", [TILES * P, TABW], F32)
        self.h_table3 = dram("h_table3", [TILES * P, 257], F32)
        self.routed_in = dram("routed_in", [SLOTS_X * P, C], F32)
        self.routed_out = dram("routed_out", [SLOTS_X * P, C], F32)

    def sb(self, name, shape, dt):
        return self.ctx.enter_context(self.nc.sbuf_tensor(name, shape, dt))

    def dram(self, name, shape, dt):
        return self.nc.dram_tensor(name, shape, dt, kind="Internal").ap()


class Phase:

    def __init__(self, k, name):
        self.k, self.name, self.ctx, self.sems = k, name, ExitStack(), []
        self.passes = self.sem("passes")

    def __enter__(self):
        return self

    def __exit__(self, *a):
        self.ctx.__exit__(*a)
        self.k.nc.clear_and_free_semaphores(self.sems)
        self.k.nc.all_engine_barrier()

    def sem(self, name):
        self.sems.append(self.k.nc.alloc_semaphore(name=f"{self.name}_{name}"))
        return self.sems[-1]

    def sb(self, name, shape, dt=F32):
        return self.ctx.enter_context(self.k.nc.sbuf_tensor(f"{self.name}_{name}", shape, dt))

    def block(self):
        return self.ctx.enter_context(self.k.nc.Block())


def wide(row):
    return row.rearrange("(a c) -> a c", a=1).to_broadcast([P, row.shape[0]])



def phase_constants(k, rstd, shift):
    nc = k.nc
    with Phase(k, "const") as ph:
        cleared, base, link = ph.sem("cleared"), ph.sem("base"), ph.sem("link")
        loaded = [ph.sem(f"loaded{g}") for g in range(TILES // 5)]
        m = Moments(k, ph, k.x, 1e-5, rstd, shift)
        block = ph.block()

        @block.gpsimd
        def _(pool):
            nc.gpsimd.memset(k.x[:, TILES - 1, :], 0.0).then_inc(cleared, 1)
            nc.gpsimd.iota(k.iota_row[:], pattern=[[1, 256]], base=0, channel_multiplier=0,
                           allow_small_or_imprecise_dtypes=True).then_inc(base, 1)
            nc.gpsimd.iota(k.iota_p[:], pattern=[[0, 1]], base=0, channel_multiplier=1,
                           allow_small_or_imprecise_dtypes=True).then_inc(base, 1)

        @block.vector
        def _(dve):
            v, c = nc.vector, Chain(dve, link)
            v.memset(k.ones[:], 1.0)
            v.memset(k.item_tile[:], 0)
            dve.wait_ge(base, 2)
            v.tensor_scalar(k.ident[:], k.iota_row[:, 0:P], k.iota_p[:, 0:1], None, ALU.is_equal)
            v.tensor_scalar(k.before[:], k.iota_row[:, 0:P], k.iota_p[:, 0:1], None, ALU.is_gt)
            for g in range(TILES // 5):
                dve.wait_ge(loaded[g], 32 if g == TILES // 5 - 1 else 16)
                m.tiles(v, c, 5 * g)
            m.finish(dve, v, c)

        @block.scalar
        def _(act):
            m.roots(act)

        @block.sync
        def _(sp):
            for g in range(TILES // 5):
                n = 5 if g < TILES // 5 - 1 else 4
                sp.dma_start(k.x[:, 5 * g:5 * g + n, :],
                             k.ins["x"][5 * g * P:(5 * g + n) * P, :].rearrange("(t p) c -> p t c", p=P)).then_inc(loaded[g], 16)
            sp.wait_ge(cleared, 1)
            sp.dma_start(k.x[0:LAST, TILES - 1, :], k.ins["x"][(TILES - 1) * P:N, :]).then_inc(loaded[-1], 16)
            sp.wait_ge(loaded[-1], 32)


def phase_items(k):
    nc = k.nc
    tail = EDGES - (PAIRS - 1) * 2 * P
    with Phase(k, "items") as ph:
        dst_i, src_i = ph.sb("dst_i", [P, 2, 256], I32), ph.sb("src_i", [P, 2, 256], I32)
        dst, src = ph.sb("dst", [P, 2, 256]), ph.sb("src", [P, 2, 256])
        lim = ph.sb("lim", [P, TILES - 1])
        passed = ph.sb("passed", [P, 2, TILES - 1])
        turn = ph.sb("turn", [P, 1])
        iota_k = ph.sb("iota_k", [P, ITEMS])
        stepped = ph.sb("stepped", [P, ITEMS])
        tile_of, pair_of = ph.sb("tile_of", [P, ITEMS]), ph.sb("pair_of", [P, ITEMS])
        sel = ph.sb("sel", [P, 2, ITEMS])
        src_f = ph.sb("src_f", [P, SUBP])
        dst_f = ph.sb("dst_f", [P, SUBP])
        hi_i = ph.sb("hi_i", [P, SUBP], I32)
        keys, offs = ph.sb("keys", [P, 2, 256]), ph.sb("offs", [P, 2, 256])
        nrow = ph.sb("nrow", [P, 2])
        lo_i = ph.sb("lo_i", [P, 2, 256], I32)
        lo_b, off_b = ph.sb("lo_b", [P, 2, 256], BF16), ph.sb("off_b", [P, 2, 256], BF16)
        padf, padb = ph.sb("padf", [P, P]), ph.sb("padb", [P, P], BF16)
        filled, loaded, iotas = ph.sem("filled"), ph.sem("loaded"), ph.sem("iotas")
        fed, made, link, stored, rows_out = ph.sem("fed"), ph.sem("made"), ph.sem("link"), ph.sem("stored"), ph.sem("rows_out")
        block = ph.block()
        kb = [(0, P), (P, ITEMS - P)]

        @block.gpsimd
        def _(pool):
            nc.gpsimd.memset(dst_i[:], NOWHERE).then_inc(filled, 1)
            nc.gpsimd.memset(src_i[:], 0).then_inc(filled, 1)
            nc.gpsimd.iota(iota_k[:], pattern=[[1, ITEMS]], base=0, channel_multiplier=0,
                           allow_small_or_imprecise_dtypes=True).then_inc(iotas, 1)
            nc.gpsimd.iota(lim[:], pattern=[[P, TILES - 1]], base=P, channel_multiplier=0,
                           allow_small_or_imprecise_dtypes=True).then_inc(iotas, 1)

        @block.sync
        def _(sp):
            sp.wait_ge(filled, 2)
            for tile, vec in ((dst_i, k.ins["dst"]), (src_i, k.ins["src"])):
                sp.dma_start(tile[0:GB, 0, :], vec[0:GB * 256].rearrange("(g e) -> g e", e=256)).then_inc(loaded, 16)
                sp.dma_start(tile[0:GB - 1, 1, :],
                             vec[GB * 256:(PAIRS - 1) * 256].rearrange("(g e) -> g e", e=256)).then_inc(loaded, 16)
                sp.dma_start(tile[GB - 1:GB, 1, 0:tail],
                             vec[(PAIRS - 1) * 256:EDGES].rearrange("(g e) -> g e", g=1)).then_inc(loaded, 16)
            sp.wait_ge(rows_out, 1)
            for tab, pad in ((k.dst_rows, padb), (k.src_rows, padb), (k.off_rows, padf)):
                sp.dma_start(tab[SUBS:SUBP, :], pad[0:SUBP - SUBS, :]).then_inc(stored, 16)
            sp.dma_start(k.key_rows[SUBS:SUBP + 1, :], padf[0:SUBP + 1 - SUBS, :]).then_inc(stored, 16)
            sp.wait_ge(rows_out, 2)
            for b, (k0, m) in enumerate(kb):
                for tab, tile in ((k.dst_rows, off_b), (k.src_rows, lo_b), (k.off_rows, offs), (k.key_rows, keys)):
                    sp.dma_start(tab[2 * k0:2 * (k0 + m), :].rearrange("(g s) e -> g (s e)", s=2), tile[0:m, b, :]).then_inc(stored, 16)
            sp.wait_ge(stored, 16 * 12)

        @block.tensor
        def _(pe):
            pe.wait_ge(fed, 1)
            for b in range(2):
                mm = nc.tensor.matmul(k.ps[0][0:TILES - 1, 0:1], passed[0:GB, b, :], k.ones[0:GB, 0:1],
                                      start=(b == 0), stop=(b == 1))
            mm.then_inc(made, 1)
            pe.wait_ge(fed, 2)
            nc.tensor.matmul(k.ps[1][:, 0:ITEMS], k.ones[0:TILES - 1, :], stepped[0:TILES - 1, :], start=True, stop=True)
            for b, (k0, m) in enumerate(kb):
                mm = nc.tensor.matmul(k.ps[2 + b][0:m, 0:1], stepped[0:TILES - 1, k0:k0 + m], k.ones[0:TILES - 1, 0:1],
                                      start=True, stop=True)
            mm.then_inc(made, 1)
            pe.wait_ge(fed, 3)
            for a, arr in enumerate((dst, src)):
                for s in range(2):
                    for b in range(2):
                        mm = nc.tensor.matmul(k.ps[4 + 2 * a + s][:, 0:ITEMS], arr[0:GB, b, s * P:(s + 1) * P],
                                              sel[0:GB, b, :], start=(b == 0), stop=(b == 1))
            mm.then_inc(made, 1)
            pe.wait_ge(fed, 4)
            for a, arr in enumerate((dst, src)):
                for q, (k0, m) in enumerate(kb):
                    for b in range(2):
                        mm = nc.tensor.matmul(k.ps[[0, 1][a]][0:m, q * 256:q * 256 + 256], sel[0:GB, b, k0:k0 + m],
                                              arr[0:GB, b, :], start=(b == 0), stop=(b == 1))
            mm.then_inc(made, 1)

        @block.vector
        def _(dve):
            v, c = nc.vector, Chain(dve, link)
            v.memset(padf[:], float(NOWHERE))
            c.mark(v.memset(src_f[:], 0.0))
            c.mark(v.memset(dst_f[:], float(NOWHERE)))
            c(v.memset(padb[:], float(NOWHERE)))
            v.memset(sel[:], 0.0).then_inc(rows_out, 1)
            dve.wait_ge(loaded, 96)
            dve.wait_ge(iotas, 2)
            c.mark(v.tensor_copy(dst[:], dst_i[:]))
            c(v.tensor_copy(src[:], src_i[:]))
            for b in range(2):
                last = v.tensor_scalar(passed[:, b, :], lim[:], dst[:, b, 255:256], None, ALU.is_gt)
                c.mark(last)
            c.wait()
            dve.sem_inc(fed, 1)
            dve.wait_ge(made, 1)
            c(v.tensor_scalar(turn[0:TILES - 1, :], k.ps[0][0:TILES - 1, 0:1], k.iota_p[0:TILES - 1, 0:1], None, ALU.add))
            v.tensor_scalar(stepped[0:TILES - 1, :], iota_k[0:TILES - 1, :], turn[0:TILES - 1, 0:1], None,
                            ALU.is_gt).then_inc(fed, 1)
            dve.wait_ge(made, 2)
            c(v.tensor_copy(tile_of[:], k.ps[1][:, 0:ITEMS]))
            c.mark(v.tensor_copy(k.item_tile[0:1, 0:ITEMS], tile_of[0:1, :]))
            c(v.tensor_tensor(pair_of[:], iota_k[:], tile_of[:], ALU.subtract))
            for b in range(2):
                c(v.tensor_scalar(sel[:, b, :], pair_of[:], float(-GB * b), k.iota_p[:, 0:1], ALU.add, ALU.is_equal))
                if b == 0:
                    for q, (k0, m) in enumerate(kb):
                        c(v.tensor_scalar(nrow[0:m, q:q + 1], k.ps[2 + q][0:m, 0:1], float(P), None, ALU.mult))
            dve.sem_inc(fed, 1)
            dve.wait_ge(made, 3)
            for s in range(2):
                c.mark(v.tensor_copy(dst_f[:, s:SUBS:2], k.ps[4 + s][:, 0:ITEMS]))
                c(v.tensor_copy(src_f[:, s:SUBS:2], k.ps[6 + s][:, 0:ITEMS]))
            dve.sem_inc(fed, 1)
            c(v.tensor_copy(k.src_of[:], src_f[:]))
            c(v.tensor_scalar(hi_i[:], k.src_of[:], 7, None, ALU.arith_shift_right))
            c(v.tensor_copy(k.src_hi[:], hi_i[:]))
            v.tensor_copy(k.dst_in[:, SUBS:SUBP], dst_f[:, SUBS:SUBP])
            for s in range(2):
                c(v.scalar_tensor_tensor(k.dst_in[:, s:SUBS:2], tile_of[:], float(-P), dst_f[:, s:SUBS:2], ALU.mult, ALU.add))
            dve.wait_ge(made, 4)
            for q, (k0, m) in enumerate(kb):
                c.mark(v.tensor_copy(keys[0:m, q, :], k.ps[0][0:m, q * 256:q * 256 + 256]))
                c(v.tensor_scalar(offs[0:m, q, :], k.ps[0][0:m, q * 256:q * 256 + 256], nrow[0:m, q:q + 1], None, ALU.subtract))
                c.mark(v.tensor_copy(off_b[0:m, q, :], offs[0:m, q, :]))
                c(v.tensor_copy(lo_i[0:m, q, :], k.ps[1][0:m, q * 256:q * 256 + 256]))
                c(v.tensor_scalar(lo_i[0:m, q, :], lo_i[0:m, q, :], 127, None, ALU.bitwise_and))
                c(v.tensor_copy(lo_b[0:m, q, :], lo_i[0:m, q, :]))
            dve.sem_inc(rows_out, 1)



class Moments:

    def __init__(self, k, ph, src, eps, rstd, shift):
        self.k, self.src, self.eps, self.rstd, self.shift = k, src, eps, rstd, shift
        self.stats, self.mv, self.both = ph.sb("stats", [P, 5, 6]), ph.sb("mv", [P, 5, 2]), ph.sb("both", [P, TILES, 2])
        self.var_ready, self.root_ready = ph.sem("var_ready"), ph.sem("root_ready")

    def tiles(self, v, c, t0):
        for j in range(5):
            c.mark(v.bn_stats(self.stats[:, j:j + 1, :], self.src[:, t0 + j:t0 + j + 1, 0:C]))
        c.wait()
        for j in range(5):
            c.mark(v.bn_aggr(self.both[:, t0 + j, :], self.stats[:, j, :]))
        c.wait()

    def finish(self, dve, v, c):
        v.tensor_scalar(self.rstd[:], self.both[:, :, 1], self.eps, None, ALU.add).then_inc(self.var_ready, 1)
        dve.wait_ge(self.root_ready, 1)
        c(v.reciprocal(self.rstd[:], self.shift[:]))
        v.scalar_tensor_tensor(self.shift[:], self.both[:, :, 0], -1.0, self.rstd[:], ALU.mult, ALU.mult)

    def roots(self, act):
        act.wait_ge(self.var_ready, 1)
        act.activation(self.shift[:], self.rstd[:], ACT.Sqrt).then_inc(self.root_ready, 1)


def phase_norm(k, name, src, eps, rstd, shift):
    nc = k.nc
    group = 5
    with Phase(k, name) as ph:
        m = Moments(k, ph, src, eps, rstd, shift)
        link = ph.sem("link")
        block = ph.block()

        @block.vector
        def _(dve):
            v, c = nc.vector, Chain(dve, link)
            turns = TILES // group
            c.loop(turns, 3 * group - group + 1)
            with dve.Fori(0, turns) as g:
                c.at(g)
                for j in range(group):
                    c.mark(v.bn_stats(m.stats[:, j:j + 1, :], src[:, bass.ds(g * group + j, 1), 0:C]))
                c.wait()
                apart(ph, dve)
                for j in range(group):
                    c.mark(v.bn_aggr(m.mv[:, j, :], m.stats[:, j, :]))
                c.wait()
                c(v.tensor_copy(m.both[:, bass.ds(g * group, group), :], m.mv[:]))
                c.full()
            c.over()
            m.finish(dve, v, c)

        @block.scalar
        def _(act):
            m.roots(act)


def phase_dense(k, name, kb, outs, stage, per_stage, evac, per_evac, loads=(), sb=(), stores=(), exps=None, evac_act=None, ahead=None):
    nc = k.nc
    with Phase(k, name) as ph:
        ph.buf = {n: ph.sb(n, shape, dt) for n, shape, dt in sb}
        staged_tile = ph.sb("staged_tile", [P, 2, kb * P])
        turned_tile = ph.sb("turned_tile", [P, 2, kb * P])
        loaded = ph.sem("loaded")
        staged, turned, copied, made, taken, act_taken = (
            ph.sem(s) for s in ("staged", "turned", "copied", "made", "taken", "act_taken"))
        link_s, link_e, stored = ph.sem("link_s"), ph.sem("link_e"), ph.sem("stored")
        ph.capped, ph.exped, ph.summed, ph.divided = (ph.sem(s) for s in ("capped", "exped", "summed", "divided"))
        pst = [k.ps[0], k.ps[1]]
        pso = [[k.ps[2 + s * len(outs) + j] for j in range(len(outs))] for s in range(2)]
        block = ph.block()
        nload = 0

        @block.sync
        def _(sp):
            for dst, src in loads:
                sp.dma_start(ph.buf[dst][:] if isinstance(dst, str) else dst, src).then_inc(loaded, 16)
            for last, dst, src in stores:
                sp.wait_ge(taken, ready(last))
                if evac_act:
                    sp.wait_ge(act_taken, ready(last))
                sp.dma_start(dst, src).then_inc(stored, 16)
            if loads:
                sp.wait_ge(loaded, 16 * len(loads))
            if stores:
                sp.wait_ge(stored, 16 * len(stores))

        @block.vector
        def _(dve):
            dve.sem_inc(staged, 2)
            dve.sem_inc(taken, 2)
            cs = Chain(dve, link_s).loop(TILES, per_stage)
            ce = Chain(dve, link_e).loop(TILES, per_evac)
            if loads:
                dve.wait_ge(loaded, 16 * len(loads))

            def stage_step(t, slot):
                dve.wait_ge(turned, free(t))
                cs.at(t)
                stage(ph, t, slot, staged_tile[:, slot, :], cs).then_inc(staged, 1)
                cs.full()

            def evac_step(t, slot):
                dve.wait_ge(made, ready(t))
                ce.at(t)
                evac(ph, t, slot, pso[slot], ce).then_inc(taken, 1)
                ce.full()

            ph.dve = dve
            if ahead:
                first, second = (lambda t, slot, f=f: f(ph, t, slot) for f in ahead)
                staggered(dve, TILES, [first, second, stage_step, None, evac_step], [2, 4, 1, 0])
            else:
                staggered(dve, TILES, [stage_step, None, evac_step])

        @block.scalar
        def _(act):
            act.sem_inc(copied, 2)

            def copy_step(t, slot):
                act.wait_ge(turned, ready(t))
                act.wait_ge(made, free(t))
                nc.scalar.copy(turned_tile[:, slot, :], pst[slot][:, 0:kb * P]).then_inc(copied, 1)

            def exp_step(t, slot):
                act.wait_ge(ph.capped, t + 1)
                act.activation(ph.buf[exps][:, slot, :], ph.buf[exps][:, slot, :], ACT.Exp).then_inc(ph.exped, 1)

            def evac_step(t, slot):
                act.wait_ge(made, ready(t))
                evac_act(t, pso[slot]).then_inc(act_taken, 1)

            if evac_act:
                act.sem_inc(act_taken, 2)
            staggered(act, TILES, ([exp_step] if exps else []) + [copy_step] + ([evac_step] if evac_act else []))

        @block.tensor
        def _(pe):
            pe.sem_inc(turned, 2)
            pe.sem_inc(made, 2)
            if loads:
                pe.wait_ge(loaded, 16 * len(loads))

            def turn_step(t, slot):
                pe.wait_ge(staged, ready(t))
                pe.wait_ge(copied, free(t))
                for b in range(kb):
                    mm = nc.tensor.transpose(pst[slot][:, b * P:(b + 1) * P], staged_tile[:, slot, b * P:(b + 1) * P],
                                             k.ident[:])
                mm.then_inc(turned, 1)

            def product_step(t, slot):
                pe.wait_ge(copied, ready(t))
                pe.wait_ge(taken, free(t))
                if evac_act:
                    pe.wait_ge(act_taken, free(t))
                for j, (w, width) in enumerate(outs):
                    wt = ph.buf[w] if isinstance(w, str) else w
                    for b in range(kb):
                        mm = nc.tensor.matmul(pso[slot][j][:, 0:width], turned_tile[:, slot, b * P:(b + 1) * P],
                                              wt[:, b, 0:width], start=(b == 0), stop=(b == kb - 1))
                mm.then_inc(made, 1)

            staggered(pe, TILES, [turn_step, product_step])


def weights(w):
    return w.rearrange("(b p) n -> p b n", p=P)


def stage_normed(k, src, rstd, shift):
    def stage(ph, t, slot, dst, c):
        return k.nc.vector.tensor_scalar(dst, src[:, bass.ds(t, 1), 0:C].rearrange("p a c -> p (a c)"),
                                         rstd[:, bass.ds(t, 1)], shift[:, bass.ds(t, 1)], ALU.mult, ALU.add)
    return stage


def row(buf, t, a, b):
    return buf[:, bass.ds(t, 1), a:b].rearrange("p a c -> p (a c)")


def tile_stores(table, src, width):
    out = []
    for g in range(0, TILES, 5):
        out.append((g + 4, table[g * P:(g + 5) * P, 0:width].rearrange("(t p) c -> p t c", p=P), src[:, g:g + 5, 0:width]))
    return out

def phase_qkv(k, rstd, shift):
    nc, a = k.nc, k.ins

    def evac(ph, t, slot, ps, c):
        c(nc.vector.tensor_tensor(row(k.h, t, 0, C), ps[0][:, 0:C], ph.buf["bq"][:], ALU.add))
        nc.vector.tensor_scalar(row(k.h, t, 0, C), row(k.h, t, 0, C), float(HD0) ** -0.5, None, ALU.mult)
        return nc.vector.tensor_tensor(row(k.acc, t, 0, 2 * C), ps[1][:, 0:2 * C], ph.buf["bkv"][:], ALU.add)

    phase_dense(
        k, "qkv", 2, [("wq", C), ("wkv", 2 * C)], stage_normed(k, k.x, rstd, shift), 0, evac, 1,
        sb=[("wq", [P, 2, C], F32), ("wkv", [P, 2, 2 * C], F32), ("bq", [P, C], F32), ("bkv", [P, 2 * C], F32)],
        loads=[("wq", weights(a["L0_gnn_Wq"])), ("wkv", weights(a["L0_gnn_Wkv"])),
               ("bq", wide(a["L0_gnn_bq"])), ("bkv", wide(a["L0_gnn_bkv"]))],
        stores=tile_stores(k.kv_table, k.acc, 2 * C))


def load_batches(sp, used, credits, tables, row_in, between=lambda: None):
    def load(b, slot):
        for table, tile in tables:
            sp.dma_start(tile[:, slot, :], item_rows(table, 4 * b, 4)).then_inc(row_in[slot], 16)

    load(0, 0)
    load(1, 1)
    between()
    with sp.Fori(0, ITEMS // 8 - 1) as i:
        for slot in range(2):
            sp.wait_ge(used, i * 8 + (4 * slot + 4 + credits))
            load(2 * i + (2 + slot), slot)


def phase_attention_edges(k):
    nc = k.nc
    RING = 8
    S = 4
    W = C + HEADS0
    with Phase(k, "edges0") as ph:
        rows = ph.sb("rows", [P, RING, 2, 2 * C])
        index = ph.sb("index", [P, RING, 2], I32)
        dst_row = ph.sb("dst_row", [P, 2, 4 * 256], BF16)
        minus_p, one_col, warm = ph.sb("minus_p", [P, 1]), ph.sb("one_col", [P, 1]), ph.sb("warm", [P, 1])
        hot_t = ph.sb("hot_t", [P, S, 256])
        hot = ph.sb("hot", [P, S, 2 * P])
        prod = ph.sb("prod", [P, 2, 2 * C])
        score = ph.sb("score", [P, S, 2 * HEADS0])
        out_rows = ph.sb("out_rows", [P, S, 2, W])
        per = 2
        ZERO_DMAS = SLOTS_X // per
        zero, zero_in = ph.sb("zero", [P, per * C]), ph.sem("zero_in")
        cleared, consts, indexed = ph.sem("cleared"), ph.sem("consts"), ph.sem("indexed")
        gathered = [ph.sem(f"gathered{r}") for r in range(RING)]
        row_in = [ph.sem(f"row_in{s}") for s in range(2)]
        hot_t_made, q_made, multiplied, reduced, clipped, exped, hot_made, weighted, summed, added = (
            ph.sem(s) for s in ("hot_t_made", "q_made", "multiplied", "reduced", "clipped", "exped", "hot_made",
                                "weighted", "summed", "added"))
        link_a, link_h = ph.sem("link_a"), ph.sem("link_h")
        psq, pso = k.ps[0:S], k.ps[S:2 * S]
        block = ph.block()

        @block.sync
        def _(sp):
            def clear_routed():
                sp.wait_ge(consts, 3)
                for j in range(ZERO_DMAS):
                    sp.dma_start(k.routed_in[j * P * per:(j + 1) * P * per, :].rearrange("(p r) c -> p (r c)", p=P),
                                 zero[:]).then_inc(zero_in, 16)

            load_batches(sp, hot_t_made, S, [(k.dst_rows, dst_row)], row_in, clear_routed)
            sp.wait_ge(zero_in, 16 * ZERO_DMAS)

        @block.gpsimd
        def _(pool):
            def gather(t, r, i):
                pool.wait_ge(indexed, t + 1)
                apart(ph, pool)
                for s in range(2):
                    nc.gpsimd.indirect_dma_start(rows[:, r, s, :], None, k.kv_table,
                                                 bass.IndirectOffsetOnAxis(ap=index[:, r, s:s + 1], axis=0)
                                                 ).then_inc(gathered[r], 16)
                if isinstance(t, int) and t == 1:
                    nc.gpsimd.memset(k.acc[:, :, 0:W], 0.0).then_inc(cleared, 1)
            for r in range(RING):
                gather(r, r, 0)
            with pool.Fori(1, ITEMS // RING) as i:
                for r in range(RING):
                    gather(i * RING + r, r, i)

        @block.scalar
        def _(act):
            act.sem_inc(hot_t_made, S)
            act.sem_inc(exped, S)
            act.sem_inc(hot_made, S)

            def one_hot_t(t, r, i):
                act.wait_ge(row_in[r // 4], (i + 1) * 16)
                act.wait_ge(q_made, free(t))
                act.activation(hot_t[:, r % S, :], dst_row[:, r // 4, r % 4 * 256:(r % 4 + 1) * 256], ACT.Abs,
                               bias=minus_p[:, 0:1]).then_inc(link_a, 1)
                act.wait_ge(link_a, t + 1)
                act.activation(hot_t[:, r % S, :], hot_t[:, r % S, :], ACT.Relu, bias=one_col[:, 0:1], scale=-1.0
                               ).then_inc(hot_t_made, 1)

            def exps(t, r, i):
                act.wait_ge(clipped, ready(t, S))
                act.wait_ge(summed, free(t))
                act.activation(out_rows[:, r % S, :, C:W], score[:, r % S, :].rearrange("p (s h) -> p s h", s=2),
                               ACT.Exp).then_inc(exped, 1)

            def one_hot(t, r, i):
                for s in range(2):
                    last = act.activation(hot[:, r % S, s * P:(s + 1) * P], k.iota_row[:, 0:P], ACT.Abs,
                                          bias=k.dst_in[:, bass.ds(2 * t + s, 1)], scale=-1.0)
                last.then_inc(link_h, 1)
                act.wait_ge(link_h, t + 1)
                act.activation(hot[:, r % S, :], hot[:, r % S, :], ACT.Relu, bias=one_col[:, 0:1], scale=-1.0
                               ).then_inc(hot_made, 1)

            def exps_and_one_hot(t, r, i):
                exps(t, r, i)
                one_hot(t, r, i)

            act.wait_ge(consts, 3)
            act.activation(warm[:], one_col[:], ACT.Exp)
            ringed(act, ITEMS, RING, [one_hot_t, None, None, None, exps_and_one_hot])

        @block.tensor
        def _(pe):
            pe.sem_inc(q_made, S)
            pe.sem_inc(summed, S)

            def q_of_edges(t, r, i):
                n = pe.value_load(k.item_tile[0:1, bass.ds(t, 1)], min_val=0, max_val=TILES - 1)
                pe.wait_ge(hot_t_made, ready(t, S))
                pe.wait_ge(multiplied, free(t))
                for s in range(2):
                    mm = nc.tensor.matmul(psq[r % S][:, s * C:(s + 1) * C], hot_t[:, r % S, s * P:(s + 1) * P],
                                          row(k.h, n, 0, C), start=True, stop=True)
                mm.then_inc(q_made, 1)

            def sums(t, r, i):
                pe.wait_ge(weighted, ready(t, S))
                pe.wait_ge(exped, ready(t, S))
                pe.wait_ge(hot_made, ready(t, S))
                pe.wait_ge(added, free(t))
                for s in range(2):
                    mm = nc.tensor.matmul(pso[r % S][:, 0:W], hot[:, r % S, s * P:(s + 1) * P], out_rows[:, r % S, s, :],
                                          start=(s == 0), stop=(s == 1))
                mm.then_inc(summed, 1)

            ringed(pe, ITEMS, RING, [q_of_edges, None, None, None, None, sums])

        @block.vector
        def _(dve):
            v = nc.vector
            v.memset(one_col[:], 1.0).then_inc(consts, 1)
            v.memset(zero[:], 0.0).then_inc(consts, 1)
            v.tensor_scalar(minus_p[:], k.iota_p[:], -1.0, None, ALU.mult).then_inc(consts, 1)
            for s in (multiplied, reduced, clipped, weighted, added):
                dve.sem_inc(s, S)

            def stage_index(t, r):
                v.tensor_copy(index[:, r, :], k.src_of[:, bass.ds(2 * t, 2)]).then_inc(indexed, 1)

            def multiply(t, r, i):
                dve.wait_ge(gathered[r], (i + 1) * 32)
                dve.wait_ge(q_made, ready(t, S))
                dve.wait_ge(reduced, t + S - 1)
                v.tensor_tensor(prod[:, r % 2, :], psq[r % S][:, 0:2 * C], rows[:, r, :, 0:C], ALU.mult).then_inc(multiplied, 1)

            def reduce(t, r, i):
                dve.wait_ge(multiplied, ready(t, S))
                dve.wait_ge(exped, free(t))
                v.tensor_reduce(score[:, r % S, :], prod[:, r % 2, :].rearrange("p (g d) -> p g d", d=HD0), AX.X, ALU.add
                                ).then_inc(reduced, 1)

            def clip(t, r, i):
                dve.wait_ge(reduced, ready(t, S))
                v.tensor_scalar(score[:, r % S, :], score[:, r % S, :], 10.0, -10.0, ALU.min, ALU.max).then_inc(clipped, 1)

            def weigh(t, r, i):
                dve.wait_ge(summed, free(t))
                dve.wait_ge(exped, ready(t, S))
                e = out_rows[:, r % S, :, C:W].rearrange("p s (h o) -> p s h o", o=1).to_broadcast([P, 2, HEADS0, HD0])
                v.tensor_tensor(out_rows[:, r % S, :, 0:C].rearrange("p s (h d) -> p s h d", d=HD0),
                                rows[:, r, :, C:2 * C].rearrange("p s (h d) -> p s h d", d=HD0), e, ALU.mult
                                ).then_inc(weighted, 1)

            def add(t, r, i):
                n = dve.value_load(k.item_tile[0:1, bass.ds(t, 1)], min_val=0, max_val=TILES - 1)
                dve.wait_ge(weighted, ready(t, S))
                stage_index(t + RING, r)
                dve.wait_ge(summed, ready(t, S))
                dve.wait_ge(cleared, 1)
                dve.wait_ge(added, t + S)
                v.tensor_tensor(row(k.acc, n, 0, W), row(k.acc, n, 0, W), pso[r % S][:, 0:W], ALU.add
                                ).then_inc(added, 1)

            for r in range(RING):
                stage_index(r, r)
            ringed(dve, ITEMS, RING, [multiply, reduce, clip, weigh, add])


def item_rows(table, t, n):
    return table[bass.ds(2 * t, 2 * n), :].rearrange("s e -> (s e)").rearrange("(a c) -> a c", a=1).to_broadcast([P, n * 256])


def phase_attention_out(k, rstd, shift):
    nc, a = k.nc, k.ins

    def stage(ph, t, slot, dst, c):
        v, den = nc.vector, ph.buf["den"]
        c(v.tensor_scalar(den[:, slot, :], row(k.acc, t, C, C + HEADS0), 1e-30, None, ALU.max))
        c(v.reciprocal(den[:, slot, :], den[:, slot, :]))
        return v.tensor_tensor(dst.rearrange("p (h d) -> p h d", d=HD0),
                               row(k.acc, t, 0, C).rearrange("p (h d) -> p h d", d=HD0),
                               den[:, slot, :].rearrange("p (h o) -> p h o", o=1).to_broadcast([P, HEADS0, HD0]), ALU.mult)

    def evac(ph, t, slot, ps, c):
        v, feat = nc.vector, ph.buf["feat"]
        c(v.tensor_scalar(feat[:, slot, :], row(k.x, t, 0, C), rstd[:, bass.ds(t, 1)], shift[:, bass.ds(t, 1)],
                          ALU.mult, ALU.add))
        c(v.tensor_tensor(feat[:, slot, :], feat[:, slot, :], ph.buf["bp"][:], ALU.add))
        return v.tensor_tensor(row(k.h, t, 0, C), ps[0][:, 0:C], feat[:, slot, :], ALU.add)

    phase_dense(k, "proj", 2, [("wp", C)], stage, 2, evac, 2,
                sb=[("wp", [P, 2, C], F32), ("bp", [P, C], F32), ("den", [P, 2, HEADS0], F32), ("feat", [P, 2, C], F32)],
                loads=[("wp", weights(a["L0_gnn_Wp"])), ("bp", wide(a["L0_gnn_bp"]))])



class Ffn:

    def __init__(self, ph, sets):
        self.w1, self.w2 = ph.sb("w1", [P, sets, 2, HID]), ph.sb("w2", [P, sets, HID // P, C])
        self.b1, self.b2 = ph.sb("b1", [P, sets, HID // P]), ph.sb("b2", [P, sets, C])
        self.g, self.b = ph.sb("g", [P, sets, 2]), ph.sb("b", [P, sets, 2])
        self.rows, self.turned = ph.sb("rows", [P, 2, C]), ph.sb("turned", [P, 2, 2, P])
        self.hidden = ph.sb("hidden", [P, 2, HID // P, P])
        self.rows_ready, self.turns, self.copies = ph.sem("rows_ready"), ph.sem("turns"), ph.sem("copies")
        self.ups, self.gelus, self.downs, self.taken = (ph.sem(s) for s in ("ups", "gelus", "downs", "taken"))
        self.rows_in, self.up_in, self.down_in = ([ph.sem(f"{n}{s}") for s in range(2)] for n in ("rows_in", "up_in", "down_in"))
        self.warm = ph.sb("warm", [P, 1])
        self.weights_in = ph.sem("weights_in")


def ffn_tensor(k, f, pe, n, wait_rows, wait_up, wait_down, multi):
    nc = k.nc
    pst, psh = [k.ps[0], k.ps[1]], [[k.ps[2], k.ps[3]], [k.ps[4], k.ps[5]]]
    pso = [k.ps[6], k.ps[7]]
    for s in (f.turns, f.ups, f.downs):
        pe.sem_inc(s, 2)

    def turn(t, slot):
        wait_rows(pe, t, slot)
        pe.wait_ge(f.copies, free(t))
        for b in range(2):
            mm = nc.tensor.transpose(pst[slot][:, b * P:(b + 1) * P], f.rows[:, slot, b:C:2], k.ident[:])
        mm.then_inc(f.turns, 1)

    def up(t, slot):
        wait_up(pe, t, slot)
        pe.wait_ge(f.copies, ready(t))
        pe.wait_ge(f.gelus, free(t))
        w = slot if multi else 0
        for j in range(HID // P):
            for b in range(2):
                mm = nc.tensor.matmul(psh[slot][j // 4][:, (j % 4) * P:(j % 4 + 1) * P], f.w1[:, w, b, j:HID:HID // P],
                                      f.turned[:, slot, b, :], start=(b == 0), stop=(b == 1))
        mm.then_inc(f.ups, 1)

    def down(t, slot):
        wait_down(pe, t, slot)
        pe.wait_ge(f.gelus, ready(t))
        pe.wait_ge(f.taken, free(t))
        w = slot if multi else 0
        for j in range(HID // P):
            mm = nc.tensor.matmul(pso[slot][:, 0:C], f.hidden[:, slot, j, :], f.w2[:, w, j, :],
                                  start=(j == 0), stop=(j == HID // P - 1))
        mm.then_inc(f.downs, 1)

    staggered(pe, n, [turn, up, down])


def turned_copy(k, f, dve, wait_up, multi, affine):
    v = k.nc.vector
    dve.sem_inc(f.copies, 2)

    def copy(t, slot):
        w = slot if multi else 0
        wait_up(dve, t, slot)
        dve.wait_ge(f.turns, ready(t))
        dve.wait_ge(f.ups, free(t))
        ps = k.ps[slot]
        if affine:
            for b in range(2):
                last = v.tensor_scalar(f.turned[:, slot, b, :], ps[:, b * P:(b + 1) * P], f.g[:, w, b:b + 1],
                                       f.b[:, w, b:b + 1], ALU.mult, ALU.add)
        else:
            last = v.tensor_copy(f.turned[:, slot, :, :], ps[:, 0:2 * P].rearrange("p (b n) -> p b n", b=2))
        last.then_inc(f.copies, 1)
    return copy


def ffn_scalar(k, f, act, n, wait_up, multi):
    act.sem_inc(f.gelus, 2)

    def gelu(t, slot):
        w = slot if multi else 0
        wait_up(act, t, slot)
        act.wait_ge(f.ups, ready(t))
        act.wait_ge(f.downs, free(t))
        for j in range(HID // P):
            last = act.activation(f.hidden[:, slot, j, :], k.ps[2 + 2 * slot + j // 4][:, (j % 4) * P:(j % 4 + 1) * P],
                                  ACT.Gelu, bias=f.b1[:, w, j:j + 1])
        last.then_inc(f.gelus, 1)

    act.activation(f.warm[:], k.ones[:, 0:1], ACT.Gelu)
    sweep(act, n, gelu)


def phase_node_ffn(k, rstd, shift):
    nc, a = k.nc, k.ins
    with Phase(k, "ffn0") as ph:
        f = Ffn(ph, 1)
        part = ph.sb("part", [P, 2, C])
        link = ph.sem("link")
        block = ph.block()
        loads = [(f.w1[:, 0], a["L0_gnn_W1"].rearrange("(p b) n -> p b n", b=2)),
                 (f.w2[:, 0], a["L0_gnn_W2"].rearrange("(p j) n -> p j n", p=P)),
                 (f.b1[:, 0, :], a["L0_gnn_b1"].rearrange("(p j) -> p j", p=P)), (f.b2[:, 0, :], wide(a["L0_gnn_b2"])),
                 (f.g[:, 0, :], a["L0_gnn_ln_g"].rearrange("(p b) -> p b", b=2)),
                 (f.b[:, 0, :], a["L0_gnn_ln_b"].rearrange("(p b) -> p b", b=2))]

        @block.sync
        def _(sp):
            for dst, src in loads:
                sp.dma_start(dst, src).then_inc(f.weights_in, 16)
            sp.wait_ge(f.weights_in, 16 * len(loads))

        @block.tensor
        def _(pe):
            pe.wait_ge(f.weights_in, 16 * len(loads))
            ffn_tensor(k, f, pe, TILES, lambda e, t, s: e.wait_ge(f.rows_ready, ready(t)),
                       lambda e, t, s: None, lambda e, t, s: None, False)

        @block.scalar
        def _(act):
            act.wait_ge(f.weights_in, 16 * len(loads))
            ffn_scalar(k, f, act, TILES, lambda e, t, s: None, False)

        @block.vector
        def _(dve):
            v = nc.vector
            dve.sem_inc(f.rows_ready, 2)
            dve.sem_inc(f.taken, 2)
            dve.wait_ge(f.weights_in, 16 * len(loads))
            c = Chain(dve, link).loop(TILES, 2)

            def stage(t, slot):
                dve.wait_ge(f.turns, free(t))
                v.tensor_scalar(f.rows[:, slot, :], row(k.h, t, 0, C), rstd[:, bass.ds(t, 1)], shift[:, bass.ds(t, 1)],
                                ALU.mult, ALU.add).then_inc(f.rows_ready, 1)

            def take(t, slot):
                c.at(t)
                c(v.tensor_tensor(part[:, slot, :], row(k.h, t, 0, C), f.b2[:, 0, :], ALU.add))
                dve.wait_ge(f.downs, ready(t))
                c(v.tensor_tensor(part[:, slot, :], part[:, slot, :], k.ps[6 + slot][:, 0:C], ALU.add))
                v.tensor_tensor(row(k.x, t, 0, C), row(k.x, t, 0, C), part[:, slot, :], ALU.add).then_inc(f.taken, 1)

            staggered(dve, TILES, [stage, turned_copy(k, f, dve, lambda e, t, s: None, False, True), None, take])



class Route:

    def __init__(self, k, ctx, name):
        def sb(n, shape, dt):
            return ctx.enter_context(k.nc.sbuf_tensor(f"{name}_{n}", shape, dt))
        self.logits = sb("logits", [P, TILES, EXPERTS], F32)
        self.share = sb("share", [P, TILES, 2], F32)
        self.place = sb("place", [P, TILES, 2], I32)
        self.expert = sb("expert", [P, 64], I32)


def phase_gate(k, name, r, wg, bg, rstd, shift):
    nc = k.nc

    def stage(ph, t, slot, dst, c):
        for d in (row(k.h, t, 0, C), dst):
            last = nc.vector.tensor_scalar(d, row(k.x, t, 0, C), rstd[:, bass.ds(t, 1)], shift[:, bass.ds(t, 1)],
                                           ALU.mult, ALU.add)
        return last

    def evac(ph, t, slot, ps, c):
        return nc.vector.tensor_tensor(row(r.logits, t, 0, EXPERTS), ps[0][:, 0:EXPERTS], ph.buf["bg"][:], ALU.add)

    phase_dense(k, name, 2, [("wg", EXPERTS)], stage, 0, evac, 0,
                sb=[("wg", [P, 2, EXPERTS], F32), ("bg", [P, EXPERTS], F32)],
                loads=[("wg", weights(wg)), ("bg", wide(bg))])


def phase_route(k, name, r):
    nc = k.nc
    TE = TILES * EXPERTS
    with Phase(k, name) as ph:
        hot = ph.sb("hot", [P, 2, TILES, EXPERTS])
        mx = ph.sb("mx", [P, TILES, EXPERTS])
        ix = ph.sb("ix", [P, TILES, EXPERTS], U32)
        which = ph.sb("which", [P, TILES, 2])
        both, incl, pos, tmp = (ph.sb(n, [P, TILES, EXPERTS]) for n in ("both", "incl", "pos", "tmp"))
        zero = ph.sb("zero", [P, TILES])
        real = ph.sb("real", [P, TILES])
        e2, r1 = ph.sb("e2", [P, TILES]), ph.sb("r1", [P, TILES])
        count, tiles_f, ends = (ph.sb(n, [P, EXPERTS]) for n in ("count", "tiles_f", "ends"))
        count_i = ph.sb("count_i", [P, EXPERTS], I32)
        placef = ph.sb("placef", [P, TILES, 2])
        of_tile = ph.sb("of_tile", [P, 2, 64])
        link, diff, exped, masked, counted, placed = (ph.sem(s) for s in ("link", "diff", "exped", "masked", "counted", "placed"))
        zeroed, scattered = ph.sem("zeroed"), ph.sem("scattered")
        block = ph.block()

        @block.scalar
        def _(act):
            act.wait_ge(diff, 1)
            act.activation(e2[:], r1[:], ACT.Exp).then_inc(exped, 1)

        @block.tensor
        def _(pe):
            pe.wait_ge(masked, 1)
            nc.tensor.matmul(k.ps[0][:, 0:TE], k.before[:], both[:].rearrange("p t e -> p (t e)"), start=True, stop=True)
            nc.tensor.matmul(k.ps[1][:, 0:TE], k.ones[:], both[:].rearrange("p t e -> p (t e)"),
                             start=True, stop=True).then_inc(counted, 1)

        @block.vector
        def _(dve):
            v, c = nc.vector, Chain(dve, link)
            v.memset(zero[:], 0.0).then_inc(zeroed, 1)
            for t in range(TILES):
                c.mark(v.max(mx[:, t, :], r.logits[:, t, :]))
            c.wait()
            for t in range(TILES):
                c.mark(v.max_index(ix[:, t, :], mx[:, t, :], r.logits[:, t, :]))
            c.wait()
            c(v.tensor_copy(which[:], ix[:, :, 0:2]))
            v.tensor_tensor(r1[:], mx[:, :, 1], mx[:, :, 0], ALU.subtract).then_inc(diff, 1)
            c(v.memset(real[:], 1.0))
            c(v.tensor_scalar(real[:, TILES - 1:TILES], k.iota_p[:], float(LAST), None, ALU.is_lt))
            for j in range(2):
                c(v.tensor_tensor(hot[:, j], k.iota_row[:, 0:EXPERTS].rearrange("p (a e) -> p a e", a=1).to_broadcast([P, TILES, EXPERTS]),
                                  which[:, :, j:j + 1].to_broadcast([P, TILES, EXPERTS]), ALU.is_equal))
            c(v.tensor_tensor(both[:], hot[:, 0], hot[:, 1], ALU.add))
            c(v.tensor_tensor(both[:], both[:], real[:].rearrange("p (t a) -> p t a", a=1).to_broadcast([P, TILES, EXPERTS]), ALU.mult))
            dve.sem_inc(masked, 1)
            dve.wait_ge(exped, 1)
            c(v.tensor_scalar(r1[:], e2[:], 1.0, None, ALU.add))
            c(v.reciprocal(r1[:], r1[:]))
            v.tensor_copy(r.share[:, :, 0], r1[:])
            v.tensor_tensor(r.share[:, :, 1], r1[:], e2[:], ALU.mult)
            dve.wait_ge(counted, 1)
            total = k.ps[1][:, 0:TE].rearrange("p (t e) -> p t e", e=EXPERTS)
            inner = k.ps[0][:, 0:TE].rearrange("p (t e) -> p t e", e=EXPERTS)
            dve.wait_ge(zeroed, 1)
            for e in range(EXPERTS):
                c.mark(v.tensor_tensor_scan(incl[:, :, e], total[:, :, e], zero[:, 0:TILES], 0.0, ALU.add, ALU.add))
            c.wait()
            c(v.tensor_tensor(pos[:], incl[:], total, ALU.subtract))
            c(v.tensor_tensor(pos[:], pos[:], inner, ALU.add))
            c(v.tensor_scalar(count[:], incl[:, TILES - 1, :], float(P - 1), None, ALU.add))
            c(v.tensor_copy(count_i[:], count[:]))
            c(v.tensor_scalar(count_i[:], count_i[:], 7, None, ALU.arith_shift_right))
            c(v.tensor_copy(tiles_f[:], count_i[:]))
            c(v.tensor_tensor_scan(ends[:], tiles_f[:], zero[:, 0:EXPERTS], 0.0, ALU.add, ALU.add))
            c(v.tensor_tensor(count[:], ends[:], tiles_f[:], ALU.subtract))
            c(v.tensor_scalar(count[:], count[:], float(P), None, ALU.mult))
            c(v.tensor_tensor(pos[:], pos[:], count[:].rearrange("p (a e) -> p a e", a=1).to_broadcast([P, TILES, EXPERTS]), ALU.add))
            for j in range(2):
                c(v.tensor_tensor(tmp[:], pos[:], hot[:, j], ALU.mult))
                c(v.tensor_reduce(placef[:, :, j], tmp[:], AX.X, ALU.add))
            c(v.tensor_copy(r.place[:], placef[:]))
            dve.sem_inc(placed, 1)
            c(v.tensor_scalar(of_tile[:, 0, :], k.iota_row[:, 0:64], ends[:, 0:1], None, ALU.is_ge))
            for e in range(1, EXPERTS - 1):
                c(v.scalar_tensor_tensor(of_tile[:, e % 2, :], k.iota_row[:, 0:64], ends[:, e:e + 1], of_tile[:, (e - 1) % 2, :],
                                         ALU.is_ge, ALU.add))
            v.tensor_copy(r.expert[:], of_tile[:, (EXPERTS - 2) % 2, :])

        @block.gpsimd
        def _(pool):
            pool.wait_ge(placed, 1)
            for t in range(TILES):
                m = P if t < TILES - 1 else LAST
                for j in range(2):
                    nc.gpsimd.indirect_dma_start(k.routed_in, bass.IndirectOffsetOnAxis(ap=r.place[0:m, t, j:j + 1], axis=0),
                                                 k.h[0:m, t, 0:C], None).then_inc(scattered, 16)
            pool.wait_ge(scattered, 16 * 2 * TILES)


def phase_experts(k, name, r, prefix, norm):
    nc, a = k.nc, k.ins
    w = {n: a[f"{prefix}_{n}"] for n in ("W1", "b1", "W2", "b2")}
    if norm:
        w |= {n: a[f"{prefix}_{n}"] for n in ("ln_g", "ln_b")}
    with Phase(k, name) as ph:
        f = Ffn(ph, 2)
        result = ph.sb("result", [P, 2, C])
        stored, drained = ph.sem("stored"), ph.sem("drained")
        block = ph.block()
        up_dmas = 4 if norm else 2

        def rows_there(e, t, slot):
            e.wait_ge(f.rows_in[slot], (t // 2 + 1) * 16)

        def up_there(e, t, slot):
            e.wait_ge(f.up_in[slot], (t // 2 + 1) * (16 * up_dmas))

        def down_there(e, t, slot):
            e.wait_ge(f.down_in[slot], (t // 2 + 1) * 32)

        @block.sync
        def _(sp):
            def expert(t):
                return sp.value_load(r.expert[0:1, bass.ds(t, 1)], min_val=0, max_val=EXPERTS - 1)

            def load_rows(t, slot):
                sp.wait_ge(f.turns, free(t))
                sp.dma_start(f.rows[:, slot, :], k.routed_in[bass.ds(t * P, P), :]).then_inc(f.rows_in[slot], 16)

            def load_up(t, slot):
                n, s = expert(t), f.up_in[slot]
                sp.wait_ge(f.gelus, free(t))
                sp.dma_start(f.w1[:, slot], w["W1"][bass.ds(n, 1)].rearrange("a (p b) n -> p (a b) n", b=2)).then_inc(s, 16)
                sp.dma_start(f.b1[:, slot, :], w["b1"][bass.ds(n, 1)].rearrange("a (p j) -> p (a j)", p=P)).then_inc(s, 16)
                if norm:
                    for tile, n_ in ((f.g, "ln_g"), (f.b, "ln_b")):
                        sp.dma_start(tile[:, slot, :], w[n_][bass.ds(n, 1)].rearrange("a (p b) -> p (a b)", b=2)).then_inc(s, 16)

            def load_down(t, slot):
                n, s = expert(t), f.down_in[slot]
                sp.wait_ge(f.taken, free(t))
                sp.dma_start(f.w2[:, slot], w["W2"][bass.ds(n, 1)].rearrange("a (p j) n -> p (a j) n", p=P)).then_inc(s, 16)
                sp.dma_start(f.b2[:, slot, :], w["b2"][bass.ds(n, 1)].to_broadcast([P, C])).then_inc(s, 16)

            staggered(sp, SLOTS_X, [load_rows, load_up, load_down])

        @block.tensor
        def _(pe):
            ffn_tensor(k, f, pe, SLOTS_X, rows_there, up_there, down_there, True)

        @block.scalar
        def _(act):
            ffn_scalar(k, f, act, SLOTS_X, up_there, True)

        @block.vector
        def _(dve):
            dve.sem_inc(f.taken, 2)

            def take(t, slot):
                down_there(dve, t, slot)
                dve.wait_ge(f.downs, ready(t))
                dve.wait_ge(drained, free(t))
                nc.vector.tensor_tensor(result[:, slot, :], k.ps[6 + slot][:, 0:C], f.b2[:, slot, :], ALU.add).then_inc(f.taken, 1)
            staggered(dve, SLOTS_X, [turned_copy(k, f, dve, up_there, True, norm), None, take])

        @block.gpsimd
        def _(pool):
            pool.sem_inc(drained, 2)

            def store(t, slot):
                pool.wait_ge(f.taken, ready(t))
                pool.dma_start(k.routed_out[bass.ds(t * P, P), :], result[:, slot, :]).then_inc(stored, 16)
                pool.wait_ge(stored, (t + 1) * 16)
                pool.sem_inc(drained, 1)
            sweep(pool, SLOTS_X, store)


def phase_combine(k, name, r, rstd, shift, last):
    nc = k.nc
    RING = 8
    with Phase(k, name) as ph:
        got = ph.sb("got", [P, RING, C])
        gathered = [ph.sem(f"gathered{i}") for i in range(RING)]
        added, link, stored = ph.sem("added"), ph.sem("link"), ph.sem("stored")
        m = None if last else Moments(k, ph, k.x, 1e-5, rstd, shift)
        block = ph.block()
        steps = [(t, j) for t in range(TILES) for j in range(2)]

        @block.gpsimd
        def _(pool):
            for i, (t, j) in enumerate(steps):
                m_ = P if t < TILES - 1 else LAST
                if i >= RING:
                    pool.wait_ge(added, i - RING + 1)
                nc.gpsimd.indirect_dma_start(got[0:m_, i % RING, :], None, k.routed_out,
                                             bass.IndirectOffsetOnAxis(ap=r.place[0:m_, t, j:j + 1], axis=0)
                                             ).then_inc(gathered[i % RING], 16)

        @block.vector
        def _(dve):
            v, c = nc.vector, Chain(dve, link)
            for i, (t, j) in enumerate(steps):
                m_ = P if t < TILES - 1 else LAST
                dve.wait_ge(gathered[i % RING], 16 * (i // RING + 1))
                if i:
                    dve.wait_ge(added, i)
                v.scalar_tensor_tensor(k.x[0:m_, t, :], got[0:m_, i % RING, :], r.share[0:m_, t, j:j + 1], k.x[0:m_, t, :],
                                       ALU.mult, ALU.add).then_inc(added, 1)
                if m and t % 5 == 4 and j == 1:
                    dve.wait_ge(added, i + 1)
                    m.tiles(v, c, t - 4)
            if m:
                m.finish(dve, v, c)

        @block.scalar
        def _(act):
            if m:
                m.roots(act)

        @block.sync
        def _(sp):
            if last:
                for g in range(TILES // 5):
                    n = 5 if g < TILES // 5 - 1 else 4
                    sp.wait_ge(added, 2 * (5 * g + n))
                    sp.dma_start(k.out[5 * g * P:(5 * g + n) * P, :].rearrange("(t p) c -> p t c", p=P),
                                 k.x[:, 5 * g:5 * g + n, :]).then_inc(stored, 16)
                sp.wait_ge(added, 2 * TILES)
                sp.dma_start(k.out[(TILES - 1) * P:N, :], k.x[0:LAST, TILES - 1, :]).then_inc(stored, 16)
                sp.wait_ge(stored, 16 * (TILES // 5 + 1))


def routed_layer(k, name, prefix, wg, bg, norm, rstd, shift, last):
    with ExitStack() as ctx:
        r = Route(k, ctx, name)
        phase_gate(k, name + "_gate", r, wg, bg, rstd, shift)
        phase_route(k, name + "_route", r)
        phase_experts(k, name + "_experts", r, prefix, norm)
        phase_combine(k, name + "_combine", r, rstd, shift, last)



class Spans:

    def __init__(self, k, ctx):
        def sb(n, shape):
            return ctx.enter_context(k.nc.sbuf_tensor(f"span_{n}", shape, BF16))
        self.prev = sb("prev", [P, BLK, P])
        self.next = sb("next", [P, BLK, P])
        self.head = sb("head", [P, BLK, P])
        self.tail = sb("tail", [P, BLK, P])
        self.in_item = sb("in_item", [P, BLK, P])
        self.carry = sb("carry", [4, SUBP + 1])
        self.down = sb("down", [4, SUBP])
        self.up = sb("up", [4, SUBP])


def phase_spans(k, s, layers):
    nc = k.nc
    flat, at, parts = k.h[:].rearrange("p t c -> p (t c)"), 0, []

    def take(*shape):
        nonlocal at
        n = int(np.prod(shape))
        at += n
        return flat[:, at - n:at].rearrange("p (a b) -> p a b", a=shape[0])

    for w, vecs, wa in layers:
        parts.append((w, vecs, wa, take(w.shape[0] // P, w.shape[1]), take(2, w.shape[1])))
    prod = take(1, 512)
    with Phase(k, "spans") as ph:
        key, off = ph.sb("key", [P, BLK, P]), ph.sb("off", [P, BLK, P])
        first_next = ph.sb("first_next", [P, BLK])
        first, last_ = ph.sb("first", [4, SUBP + 1]), ph.sb("last", [4, SUBP + 1])
        same, low = ph.sb("same", [P, BLK, P]), ph.sb("low", [P, BLK, P])
        loaded, link, flagged, turned = ph.sem("loaded"), ph.sem("link"), ph.sem("flagged"), ph.sem("turned")
        w_loaded = ph.sem("w_loaded")
        block = ph.block()

        @block.sync
        def _(sp):
            with nc.allow_non_contiguous_dma(reason="one key of each edge tile"):
                sp.dma_start(key[:], k.key_rows[0:SUBP, :].rearrange("(b p) e -> p b e", p=P)).then_inc(loaded, 16)
                sp.dma_start(off[:], k.off_rows.rearrange("(b p) e -> p b e", p=P)).then_inc(loaded, 16)
                for b in range(BLK):
                    sp.dma_start(first_next[:, b:b + 1], k.key_rows[b * P + 1:(b + 1) * P + 1, 0:1]).then_inc(loaded, 16)
                for tile, col in ((first, 0), (last_, P - 1)):
                    for h in range(4):
                        sp.dma_start(tile[h:h + 1, :], k.key_rows[:, col:col + 1].rearrange("r o -> o r")).then_inc(loaded, 16)
            for w, vecs, _, wt, av in parts:
                sp.dma_start(wt, weights(w)).then_inc(w_loaded, 16)
                for i, vec in enumerate(vecs):
                    sp.dma_start(av[:, i, :], wide(vec.rearrange("h d -> (h d)"))).then_inc(w_loaded, 16)
            sp.wait_ge(loaded, 16 * (2 + BLK + 8))
            sp.wait_ge(w_loaded, 48 * len(parts))

        @block.vector
        def _(dve):
            v, c = nc.vector, Chain(dve, link)
            dve.wait_ge(loaded, 16 * (2 + BLK + 8))

            def penalty(dst, flag):
                c(v.tensor_scalar(dst, flag, 1.0, BIG, ALU.subtract, ALU.mult))

            c(v.memset(same[:, :, 0:1], 0.0))
            c(v.tensor_tensor(same[:, :, 1:P], key[:, :, 1:P], key[:, :, 0:P - 1], ALU.is_equal))
            penalty(s.prev[:], same[:])
            c(v.tensor_tensor(same[:, :, 0:P - 1], key[:, :, 1:P], key[:, :, 0:P - 1], ALU.is_equal))
            c(v.memset(same[:, :, P - 1:P], 0.0))
            penalty(s.next[:], same[:])
            c(v.tensor_tensor(same[:, :, P - 1], key[:, :, P - 1], first_next[:], ALU.is_equal))
            c(v.tensor_scalar(same[:], same[:], -1.0, 1.0, ALU.mult, ALU.add))
            c(v.tensor_scalar(low[:], off[:], 0.0, None, ALU.is_ge))
            c(v.tensor_scalar(off[:], off[:], float(P), None, ALU.is_lt))
            c(v.tensor_tensor(low[:], low[:], off[:], ALU.mult))
            penalty(s.in_item[:], low[:])
            c(v.tensor_tensor(same[:], same[:], low[:], ALU.mult))
            dve.sem_inc(flagged, 1)
            for b in range(BLK):
                c(v.tensor_scalar(off[:, b, :], key[:, b, :], key[:, b, 0:1], None, ALU.is_equal))
                c(v.tensor_scalar(low[:, b, :], key[:, b, :], key[:, b, P - 1:P], None, ALU.is_equal))
            penalty(s.head[:], off[:])
            penalty(s.tail[:], low[:])
            c(v.tensor_tensor(s.carry[:, 1:SUBP + 1], first[:, 1:SUBP + 1], last_[:, 0:SUBP], ALU.is_equal))
            c(v.memset(s.carry[:, 0:1], 0.0))
            c(v.memset(s.carry[:, SUBP:SUBP + 1], 0.0))
            penalty(s.carry[:], s.carry[:])
            c(v.tensor_tensor(first[:], first[:], last_[:], ALU.is_equal))
            penalty(first[:], first[:])
            c(v.tensor_tensor(s.down[:], s.carry[:, 0:SUBP], first[:, 0:SUBP], ALU.add))
            c(v.tensor_tensor(s.up[:], s.carry[:, 1:SUBP + 1], first[:, 0:SUBP], ALU.add))
            dve.wait_ge(turned, 1)
            v.tensor_copy(k.is_last[:], k.ps[0][:, 0:SUBP])
            dve.wait_ge(w_loaded, 48 * len(parts))
            for w, (vec, _), wa, wt, av in parts:
                heads, width = vec.shape
                for b in range(wt.shape[1]):
                    for i in range(2):
                        p = prod[:, 0, 0:heads * width]
                        c(v.tensor_tensor(p, wt[:, b, :], av[:, i, :], ALU.mult))
                        c(v.tensor_reduce(wa[:, b, i * heads:(i + 1) * heads], p.rearrange("p (h d) -> p h d", d=width), AX.X, ALU.add))

        @block.tensor
        def _(pe):
            pe.wait_ge(flagged, 1)
            for b in range(BLK):
                mm = nc.tensor.transpose(k.ps[0][:, b * P:(b + 1) * P], same[:, b, :], k.ident[:])
            mm.then_inc(turned, 1)


class Gat:

    def __init__(self, buf, n, heads, width, table):
        self.n, self.H, self.D, self.table = n, heads, width, table
        self.W = heads * (width + 1)
        self.of_node = buf["of_node"][:, 0:2 * heads, :]
        self.of_src = buf["of_src"][:, 0:heads, :]
        self.of_dst = buf["shared"][:, 0:2 * heads * SUBP].rearrange("p (h e) -> p h e", e=SUBP)
        ring = 8 if heads == 1 else 4
        self.rows = buf["shared"][:, 0:ring * 2 * self.W].rearrange("p (r s w) -> p r s w", s=2, w=self.W)
        self.last_max = buf["last_max"][:, :, 0:heads + 1]
        self.own = buf["own"][:, 0:heads, :]
        self.inv = buf["inv"][:, 0:heads, :]

    @staticmethod
    def buffers(k, ctx, heads):
        shapes = {"of_node": [P, 2 * heads, TILES], "of_src": [P, heads, SUBP], "shared": [P, max(2 * heads * SUBP, 8 * ACCW)],
                  "last_max": [P, SUBS, heads + 1], "own": [P, heads, TILES], "inv": [P, heads, TILES]}
        return {n: ctx.enter_context(k.nc.sbuf_tensor(f"gat_{n}", s, F32)) for n, s in shapes.items()}


def phase_gat_dense(k, g, kb, w, wa, ahead, stage, sb, loads):
    nc = k.nc
    H, D = g.H, g.D

    def node(t):
        return k.h[:, bass.ds(t, 1), 0:g.W].rearrange("p a (h d) -> p (a h) d", d=D + 1)

    def evac(ph, t, slot, ps, c):
        v = nc.vector
        apart(ph, c.eng)
        v.tensor_copy(node(t)[:, :, D], k.ones[:, 0:H])
        return v.tensor_copy(g.of_node[:, :, bass.ds(t, 1)].rearrange("p h a -> p (h a)"), ps[1][:, 0:2 * H])

    def evac_act(t, ps):
        return nc.scalar.copy(node(t)[:, :, 0:D], ps[0][:, 0:H * D].rearrange("p (h d) -> p h d", d=D))

    phase_dense(k, f"gat{g.n}", kb, [("w", H * D), (wa, 2 * H)], stage, 0, evac, 0,
                sb=sb + [("w", [P, kb, H * D], F32)], loads=loads + [("w", weights(w))],
                exps="neg" if ahead else None, evac_act=evac_act, ahead=ahead,
                stores=tile_stores(g.table, k.h, g.W))


def phase_gat_scores(k, g):
    nc, H = k.nc, g.H
    RING = 8
    HT = H * TILES
    with Phase(k, f"gat{g.n}_scores") as ph:
        rows = ph.sb("rows", [P, 2, 2, 4 * 256], BF16)
        hot = ph.sb("hot", [P, 4, 2, 256], BF16)
        parts = ph.sb("parts", [P, 3, 2 * HT], BF16)
        of_item = ph.sb("of_item", [P, 4, 3, 2 * H], BF16)
        rest = ph.sb("rest", [P, 2 * HT])
        tile_hot = ph.sb("tile_hot", [P, 2, 8, TILES])
        picked = ph.sb("picked", [P, 2, 2, H, TILES])
        row_in = [ph.sem(f"row_in{s}") for s in range(2)]
        hots, chosen, made, masked, picks, dst_taken, cut, link = (
            ph.sem(s) for s in ("hots", "chosen", "made", "masked", "picks", "dst_taken", "cut", "link"))
        block = ph.block()
        bank, dst_bank = k.ps[0:4], k.ps[4:8]

        @block.sync
        def _(sp):
            load_batches(sp, hots, 4, [(k.src_rows, rows[:, 0]), (k.dst_rows, rows[:, 1])], row_in)

        @block.gpsimd
        def _(pool):
            pool.sem_inc(chosen, 4)
            pool.wait_ge(cut, 1)

            def choose(t, r, i):
                n = pool.value_load(k.item_tile[0:1, bass.ds(t, 1)], min_val=0, max_val=TILES - 1)
                pool.wait_ge(made, free(t))
                apart(ph, pool)
                nc.gpsimd.tensor_copy(of_item[:, r % 4, :, :],
                                      parts[:].rearrange("p c (h t) -> p c h t", t=TILES)[:, :, :, bass.ds(n, 1)]
                                      .rearrange("p c h a -> p c (h a)")).then_inc(chosen, 1)
            ringed(pool, ITEMS, RING, [choose])

        @block.tensor
        def _(pe):
            pe.sem_inc(made, 4)
            pe.wait_ge(cut, 1)

            def products(t, r, i):
                slot = r % 4
                pe.wait_ge(hots, ready(t, 4))
                pe.wait_ge(chosen, ready(t, 4))
                pe.wait_ge(masked, free(t))
                pe.wait_ge(dst_taken, free(t))
                for s in range(2):
                    for p in range(3):
                        nc.tensor.matmul(bank[slot][:, s * HT:(s + 1) * HT], hot[:, slot, 0, s * P:(s + 1) * P],
                                         parts[:, p, 0:HT], start=(p == 0), stop=(p == 2))
                for s in range(2):
                    for p in range(3):
                        mm = nc.tensor.matmul(dst_bank[slot][:, s * 2 * H:(s + 1) * 2 * H],
                                              hot[:, slot, 1, s * P:(s + 1) * P],
                                              of_item[:, slot, p, :], start=(p == 0), stop=(p == 2))
                mm.then_inc(made, 1)
            ringed(pe, ITEMS, RING, [products])

        @block.scalar
        def _(act):
            act.sem_inc(dst_taken, 4)

            def take(t, r, i):
                act.wait_ge(made, ready(t, 4))
                act.copy(g.of_dst[:, :, bass.ds(2 * t, 2)],
                         dst_bank[r % 4][:, 0:4 * H].rearrange("p (s h) -> p h s", s=2)).then_inc(dst_taken, 1)
            ringed(act, ITEMS, RING, [take])

        @block.vector
        def _(dve):
            v, c = nc.vector, Chain(dve, link)
            dve.sem_inc(hots, 4)
            dve.sem_inc(masked, 4)
            dve.sem_inc(picks, 2)
            v.memset(g.of_src[:, :, SUBS:SUBP], 0.0)
            v.memset(g.of_dst[:, :, SUBS:SUBP], 0.0)
            flat = g.of_node.rearrange("p h t -> p (h t)")
            c(v.tensor_copy(parts[:, 0, :], flat))
            c(v.tensor_tensor(rest[:], flat, parts[:, 0, :], ALU.subtract))
            c(v.tensor_copy(parts[:, 1, :], rest[:]))
            c(v.tensor_tensor(rest[:], rest[:], parts[:, 1, :], ALU.subtract))
            v.tensor_copy(parts[:, 2, :], rest[:]).then_inc(cut, 1)

            def one_hots(t, r, i):
                dve.wait_ge(row_in[r // 4], (i + 1) * 32)
                dve.wait_ge(made, free(t))
                if r % 4 == 0:
                    v.tensor_tensor(tile_hot[:, r // 4], k.iota_row[:, 0:TILES].rearrange("p (a n) -> p a n", a=1).to_broadcast([P, 8, TILES]),
                                    k.src_hi[:, bass.ds(2 * t, 8)].rearrange("p (s a) -> p s a", a=1).to_broadcast([P, 8, TILES]),
                                    ALU.is_equal)
                v.tensor_scalar(hot[:, r % 4, :, :], rows[:, :, r // 4, r % 4 * 256:(r % 4 + 1) * 256], k.iota_p[:, 0:1], None,
                                ALU.is_equal).then_inc(hots, 1)

            def mask(t, r, i):
                dve.wait_ge(hots, ready(t, 4))
                dve.wait_ge(made, ready(t, 4))
                dve.wait_ge(picks, free(t))
                v.tensor_tensor(picked[:, r % 2], bank[r % 4][:, 0:2 * HT].rearrange("p (s h n) -> p s h n", s=2, h=H),
                                tile_hot[:, r // 4, r % 4 * 2:r % 4 * 2 + 2].rearrange("p s (a n) -> p s a n", a=1).to_broadcast([P, 2, H, TILES]), ALU.mult
                                ).then_inc(masked, 1)

            def pick(t, r, i):
                dve.wait_ge(masked, ready(t, 4))
                v.tensor_reduce(g.of_src[:, :, bass.ds(2 * t, 2)].rearrange("p h s -> p s h"), picked[:, r % 2], AX.X, ALU.add
                                ).then_inc(picks, 1)

            ringed(dve, ITEMS, RING, [one_hots, None, mask, pick])


def phase_gat_softmax(k, g, s):
    nc, H = k.nc, g.H
    with Phase(k, f"gat{g.n}_softmax") as ph:
        run, back = ph.sb("run", [P, H, BLK, P]), ph.sb("back", [P, H, BLK, P])
        ends, into = ph.sb("ends", [4, SUBP]), ph.sb("into", [4, SUBP])
        cin = ph.sb("cin", [P, BLK, H])
        turned, masked, scanned, ends_in, carried, cins, passed, back_out, taken, shifted, exped, link = (
            ph.sem(n) for n in ("turned", "masked", "scanned", "ends_in", "carried", "cins", "passed", "back_out", "taken",
                                "shifted", "exped", "link"))
        z = back[:].rearrange("p h b e -> p h (b e)")
        block = ph.block()

        @block.tensor
        def _(pe):
            for h in range(H):
                for b in range(BLK):
                    mm = nc.tensor.transpose(k.ps[h][:, b * P:(b + 1) * P], g.of_src[:, h, b * P:(b + 1) * P], k.ident[:])
                mm.then_inc(turned, 1)
            for way, (data, col) in enumerate(((run, P - 1), (back, 0))):
                pe.wait_ge(scanned, way + 1)
                for b in range(BLK):
                    mm = nc.tensor.transpose(k.ps[4][0:H, b * P:(b + 1) * P], data[:, :, b, col], k.ident[:])
                mm.then_inc(ends_in, 1)
                pe.wait_ge(carried, way + 1)
                for b in range(BLK):
                    mm = nc.tensor.transpose(k.ps[5][:, b * H:(b + 1) * H], into[0:H, b * P:(b + 1) * P], k.ident[0:H, 0:H])
                mm.then_inc(cins, 1)
            pe.wait_ge(passed, 1)
            for h in range(H):
                for b in range(BLK):
                    mm = nc.tensor.transpose(k.ps[h][:, b * P:(b + 1) * P], back[:, h, b, :], k.ident[:])
                mm.then_inc(back_out, 1)

        @block.gpsimd
        def _(pool):
            nc.gpsimd.memset(k.acc[:, :, 0:g.W + H + 1], 0.0)

        @block.scalar
        def _(act):
            act.wait_ge(shifted, 1)
            act.activation(g.of_src[:], z, ACT.Exp).then_inc(exped, 1)

        @block.vector
        def _(dve):
            v, c = nc.vector, Chain(dve, link)

            def flat(a):
                return a.rearrange("p b e -> p (b e)")

            for h in range(H):
                dve.wait_ge(turned, h + 1)
                c(v.tensor_tensor(flat(back[:, h]), k.ps[h][:, 0:SUBP], flat(s.in_item[:]), ALU.add))
                c.mark(v.tensor_tensor_scan(flat(run[:, h]), flat(s.prev[:]), flat(back[:, h]), -BIG, ALU.add, ALU.max))
            c.wait()
            dve.sem_inc(scanned, 1)
            dve.wait_ge(ends_in, 1)
            c(v.tensor_tensor_scan(ends[0:H, :], s.down[0:H, :], k.ps[4][0:H, 0:SUBP], -BIG, ALU.add, ALU.max))
            c.mark(v.memset(into[0:H, 0:1], -BIG))
            c(v.tensor_tensor(into[0:H, 1:SUBP], ends[0:H, 0:SUBP - 1], s.carry[0:H, 1:SUBP], ALU.add))
            dve.sem_inc(carried, 1)
            dve.wait_ge(cins, 1)
            c(v.tensor_copy(cin[:], k.ps[5][:, 0:BLK * H].rearrange("p (b h) -> p b h", h=H)))
            for h in range(H):
                for b in range(BLK):
                    c.mark(v.scalar_tensor_tensor(run[:, h, b, :], s.head[:, b, :], cin[:, b, h:h + 1], run[:, h, b, :],
                                                  ALU.add, ALU.max))
            c.wait()
            for h in range(H):
                c.mark(v.tensor_tensor_scan(flat(back[:, h])[:, ::-1], flat(s.next[:])[:, ::-1], flat(run[:, h])[:, ::-1], -BIG,
                                            ALU.add, ALU.max))
            c.wait()
            dve.sem_inc(scanned, 1)
            dve.wait_ge(ends_in, 2)
            c(v.tensor_tensor_scan(ends[0:H, ::-1], s.up[0:H, ::-1], k.ps[4][0:H, 0:SUBP][:, ::-1], -BIG, ALU.add, ALU.max))
            c.mark(v.memset(into[0:H, SUBP - 1:SUBP], -BIG))
            c(v.tensor_tensor(into[0:H, 0:SUBP - 1], ends[0:H, 1:SUBP], s.carry[0:H, 1:SUBP], ALU.add))
            dve.sem_inc(carried, 1)
            dve.wait_ge(cins, 2)
            c(v.tensor_copy(cin[:], k.ps[5][:, 0:BLK * H].rearrange("p (b h) -> p b h", h=H)))
            for h in range(H):
                for b in range(BLK):
                    c.mark(v.scalar_tensor_tensor(back[:, h, b, :], s.tail[:, b, :], cin[:, b, h:h + 1], back[:, h, b, :],
                                                  ALU.add, ALU.max))
            c.wait()
            dve.sem_inc(passed, 1)
            top, al_s, al_d = run[:].rearrange("p h b e -> p h (b e)"), g.of_dst[:, 0:H, :], g.of_dst[:, H:2 * H, :]
            for h in range(H):
                dve.wait_ge(back_out, h + 1)
                c(v.tensor_tensor(top[:, h, :], k.ps[h][:, 0:SUBP], al_s[:, h, :], ALU.max))
                c(v.tensor_tensor(g.last_max[:, :, h], top[:, h, 0:SUBS], k.is_last[:, 0:SUBS], ALU.mult))
            c(v.tensor_copy(g.last_max[:, :, H], k.is_last[:, 0:SUBS]))
            c(v.tensor_tensor(top, top, al_d, ALU.add))
            c(v.scalar_tensor_tensor(top, top, 0.2, top, ALU.mult, ALU.max))
            c(v.tensor_tensor(z, g.of_src[:], al_d, ALU.add))
            c(v.scalar_tensor_tensor(z, z, 0.2, z, ALU.mult, ALU.max))
            c(v.tensor_tensor(z, z, top, ALU.subtract))
            v.tensor_scalar(z, z, 0.0, None, ALU.min).then_inc(shifted, 1)


def phase_gat_edges(k, g):
    nc, H, D = k.nc, g.H, g.D
    S = 4
    RING = 2 * S if H == 1 else S
    by_act = H * 3 // 4
    lo_heads = max(1, H // 2)
    A = lo_heads * (D + 1)
    B = g.W - A + H + 1
    with Phase(k, f"gat{g.n}_edges") as ph:
        rows = [g.rows[:, r] for r in range(RING)]
        index = ph.sb("index", [P, RING, 2], I32)
        hot = ph.sb("hot", [P, S, 2, H + 1, P])
        indexed = ph.sem("indexed")
        gathered = [ph.sem(f"gathered{r}") for r in range(RING)]
        bare, weighed, scaled, summed, added = (ph.sem(n) for n in ("bare", "weighed", "scaled", "summed", "added"))
        psa, psb = k.ps[0:S], k.ps[S:2 * S]
        block = ph.block()

        @block.gpsimd
        def _(pool):
            with pool.Fori(0, ITEMS // RING) as i:
                for r in range(RING):
                    pool.wait_ge(indexed, i * RING + r + 1)
                    apart(ph, pool)
                    for s in range(2):
                        nc.gpsimd.indirect_dma_start(rows[r][:, s, :], None, g.table,
                                                     bass.IndirectOffsetOnAxis(ap=index[:, r, s:s + 1], axis=0)
                                                     ).then_inc(gathered[r], 16)

        @block.scalar
        def _(act):
            act.sem_inc(scaled, S)

            def scale(t, r, i):
                slot = r % S
                act.wait_ge(bare, ready(t, S))
                act.wait_ge(summed, free(t))
                for s in range(2):
                    for h in range(H - by_act, H):
                        last = act.mul(hot[:, slot, s, h, :], hot[:, slot, s, H, :],
                                       g.of_src[:, h, bass.ds(2 * t + s, 1)])
                last.then_inc(scaled, 1)
            if by_act:
                ringed(act, ITEMS, RING, [scale])

        @block.tensor
        def _(pe):
            pe.sem_inc(summed, S)

            def sums(t, r, i):
                slot = r % S
                pe.wait_ge(gathered[r], (i + 1) * 32)
                pe.wait_ge(weighed, ready(t, S))
                if by_act:
                    pe.wait_ge(scaled, ready(t, S))
                pe.wait_ge(added, free(t))
                for h in range(H):
                    out = psa[slot][:, h * (D + 1):(h + 1) * (D + 1)] if h < lo_heads else \
                        psb[slot][:, (h - lo_heads) * (D + 1):(h - lo_heads + 1) * (D + 1)]
                    for s in range(2):
                        nc.tensor.matmul(out, hot[:, slot, s, h, :], rows[r][:, s, h * (D + 1):(h + 1) * (D + 1)],
                                         start=(s == 0), stop=(s == 1))
                for s in range(2):
                    mm = nc.tensor.matmul(psb[slot][:, B - H - 1:B], hot[:, slot, s, H, :],
                                          g.last_max[:, bass.ds(2 * t + s, 1), :].rearrange("p a h -> p (a h)"),
                                          start=(s == 0), stop=(s == 1))
                mm.then_inc(summed, 1)

            ringed(pe, ITEMS, RING, [sums])

        @block.vector
        def _(dve):
            v = nc.vector
            for n in (bare, weighed, added):
                dve.sem_inc(n, S)

            def stage_index(t, r):
                v.tensor_copy(index[:, r, :], k.src_of[:, bass.ds(2 * t, 2)]).then_inc(indexed, 1)

            def one_hots(t, r, i):
                slot = r % S
                dve.wait_ge(summed, free(t))
                dve.wait_ge(scaled, free(t)) if by_act else None
                for s in range(2):
                    last = v.tensor_scalar(hot[:, slot, s, H, :], k.iota_row[:, 0:P], k.dst_in[:, bass.ds(2 * t + s, 1)],
                                           None, ALU.is_equal)
                last.then_inc(bare, 1)
                for s in range(2):
                    for h in range(H - by_act):
                        last = v.tensor_scalar(hot[:, slot, s, h, :], k.iota_row[:, 0:P], k.dst_in[:, bass.ds(2 * t + s, 1)],
                                               g.of_src[:, h, bass.ds(2 * t + s, 1)], ALU.is_equal, ALU.mult)
                last.then_inc(weighed, 1)

            def add(t, r, i):
                slot = r % S
                n = dve.value_load(k.item_tile[0:1, bass.ds(t, 1)], min_val=0, max_val=TILES - 1)
                dve.wait_ge(summed, ready(t, S))
                stage_index(t + RING, r)
                dve.wait_ge(added, t + S)
                v.tensor_tensor(row(k.acc, n, 0, A), row(k.acc, n, 0, A), psa[slot][:, 0:A], ALU.add)
                v.tensor_tensor(row(k.acc, n, A, A + B), row(k.acc, n, A, A + B), psb[slot][:, 0:B], ALU.add
                                ).then_inc(added, 1)

            for r in range(RING):
                stage_index(r, r)
            ringed(dve, ITEMS, RING, [one_hots, None, add])


def phase_gat_nodes(k, g):
    nc, H, D = k.nc, g.H, g.D
    with Phase(k, f"gat{g.n}_nodes") as ph:
        alone = ph.sb("alone", [P, 1, TILES])
        top, e = (ph.sb(n, [P, 4, TILES])[:, 0:H, :] for n in ("top", "e"))
        link, shifted, exped = ph.sem("link"), ph.sem("shifted"), ph.sem("exped")
        block = ph.block()

        @block.scalar
        def _(act):
            act.wait_ge(shifted, 1)
            act.activation(g.own[:], e, ACT.Exp).then_inc(exped, 1)

        @block.vector
        def _(dve):
            v, c = nc.vector, Chain(dve, link)
            acc = k.acc[:].rearrange("p t w -> p w t")
            al_s, al_d = g.of_node[:, 0:H, :], g.of_node[:, H:2 * H, :]
            c(v.tensor_scalar(alone[:], acc[:, g.W + H:g.W + H + 1, :], -1.0, 1.0, ALU.mult, ALU.add))
            c(v.tensor_tensor(top, al_s, alone[:].to_broadcast([P, H, TILES]), ALU.mult))
            c(v.tensor_tensor(top, top, acc[:, g.W:g.W + H, :], ALU.add))
            c(v.tensor_tensor(top, top, al_s, ALU.max))
            c(v.tensor_tensor(top, top, al_d, ALU.add))
            c(v.scalar_tensor_tensor(top, top, 0.2, top, ALU.mult, ALU.max))
            c(v.tensor_tensor(e, al_s, al_d, ALU.add))
            c(v.scalar_tensor_tensor(e, e, 0.2, e, ALU.mult, ALU.max))
            c(v.tensor_tensor(e, e, top, ALU.subtract))
            v.tensor_scalar(e, e, 0.0, None, ALU.min).then_inc(shifted, 1)
            dve.wait_ge(exped, 1)
            c(v.tensor_tensor(top, g.own[:], acc[:, D:g.W:D + 1, :], ALU.add))
            c(v.tensor_scalar(top, top, 1e-16, None, ALU.add))
            v.reciprocal(g.inv[:], top)


def stage_attended(k, g):
    nc, H, D = k.nc, g.H, g.D

    def stage(ph, t, slot, dst, c):
        v, part = nc.vector, ph.buf["part"]
        for h in range(H):
            a, b = h * (D + 1), h * (D + 1) + D
            c.mark(v.scalar_tensor_tensor(part[:, slot, h * D:(h + 1) * D], row(k.h, t, a, b), g.own[:, h, bass.ds(t, 1)],
                                          row(k.acc, t, a, b), ALU.mult, ALU.add))
        c.wait()
        for h in range(H):
            last = v.scalar_tensor_tensor(dst[:, h * D:(h + 1) * D], part[:, slot, h * D:(h + 1) * D], g.inv[:, h, bass.ds(t, 1)],
                                          ph.buf["bias"][:, h * D:(h + 1) * D], ALU.mult, ALU.add)
        return last
    return stage


def elu_attended(k, g):
    nc, H, D = k.nc, g.H, g.D
    v = nc.vector

    def add_own(ph, t, slot):
        for h in range(H):
            a, b = h * (D + 1), h * (D + 1) + D
            last = v.scalar_tensor_tensor(ph.buf["part"][:, slot, h * D:(h + 1) * D], row(k.h, t, a, b), g.own[:, h, bass.ds(t, 1)],
                                          row(k.acc, t, a, b), ALU.mult, ALU.add)
        last.then_inc(ph.summed, 1)

    def divide(ph, t, slot):
        part = ph.buf["part"][:, slot, :]
        ph.dve.wait_ge(ph.summed, t + 1)
        for h in range(H):
            cols = slice(h * D, (h + 1) * D)
            last = v.scalar_tensor_tensor(part[:, cols], part[:, cols], g.inv[:, h, bass.ds(t, 1)],
                                          ph.buf["bias"][:, cols], ALU.mult, ALU.add)
        last.then_inc(ph.divided, 1)
        ph.dve.wait_ge(ph.divided, 2 * t + 1)
        v.tensor_scalar(ph.buf["neg"][:, slot, :], part, 0.0, None, ALU.min).then_inc(ph.capped, 1)
        v.tensor_scalar(part, part, 0.0, -1.0, ALU.max, ALU.add).then_inc(ph.divided, 1)

    def stage(ph, t, slot, dst, c):
        c.eng.wait_ge(ph.divided, 2 * t + 2)
        c.eng.wait_ge(ph.exped, t + 1)
        return v.tensor_tensor(dst, ph.buf["part"][:, slot, :], ph.buf["neg"][:, slot, :], ALU.add)

    return (add_own, divide), stage


def phase_mlp(k, g):
    nc, a = k.nc, k.ins
    HIDDEN2 = a["L1_gnn_M2"].shape[1]

    def relu_to_h(width):
        def evac(ph, t, slot, ps, c):
            tmp = ph.buf["tmp"]
            c(nc.vector.tensor_tensor(tmp[:, slot, :], ps[0][:, 0:width], ph.buf["mb"][:], ALU.add))
            return nc.vector.tensor_scalar(row(k.h, t, 0, width), tmp[:, slot, :], 0.0, None, ALU.max)
        return evac

    def stage_h(width):
        def stage(ph, t, slot, dst, c):
            return nc.vector.tensor_copy(dst, row(k.h, t, 0, width))
        return stage

    def add_to_x(ph, t, slot, ps, c):
        tmp = ph.buf["tmp"]
        c(nc.vector.tensor_tensor(tmp[:, slot, :], ps[0][:, 0:C], ph.buf["mb"][:], ALU.add))
        return nc.vector.tensor_tensor(row(k.x, t, 0, C), row(k.x, t, 0, C), tmp[:, slot, :], ALU.add)

    def bufs(kb, width):
        return [("w", [P, kb, width], F32), ("mb", [P, width], F32), ("tmp", [P, 2, width], F32)]

    phase_dense(k, "mlp1", 2, [("w", 2 * P)], stage_attended(k, g), g.H, relu_to_h(2 * P), 1,
                sb=bufs(2, 2 * P) + [("part", [P, 2, C], F32), ("bias", [P, C], F32)],
                loads=[("w", weights(a["L1_gnn_M1"])), ("mb", wide(a["L1_gnn_mb1"])), ("bias", wide(a["L1_gnn_b3"]))])
    phase_dense(k, "mlp2", 2, [("w", HIDDEN2)], stage_h(2 * P), 0, relu_to_h(HIDDEN2), 1, sb=bufs(2, HIDDEN2),
                loads=[("w", weights(a["L1_gnn_M2"])), ("mb", wide(a["L1_gnn_mb2"]))])
    phase_dense(k, "mlp3", 1, [("w", C)], stage_h(HIDDEN2), 0, add_to_x, 1, sb=bufs(1, C),
                loads=[("w", weights(a["L1_gnn_M3"])), ("mb", wide(a["L1_gnn_mb3"]))])


def attention_layers(k, rstd, shift):
    a = k.ins
    heads, width = a["L1_gnn_a_src1"].shape
    with ExitStack() as ctx:
        s = Spans(k, ctx)
        buf = Gat.buffers(k, ctx, heads)
        layers = []
        for n in (1, 2, 3):
            w, vecs = a[f"L1_gnn_W{n}"], (a[f"L1_gnn_a_src{n}"], a[f"L1_gnn_a_dst{n}"])
            shape = [P, w.shape[0] // P, 2 * vecs[0].shape[0]]
            layers.append((w, vecs, ctx.enter_context(k.nc.sbuf_tensor(f"gat{n}_wa", shape, F32))))
        phase_spans(k, s, layers)
        ahead, stage, sb, loads, kb = None, stage_normed(k, k.x, rstd, shift), [], [], C // P
        for n, H, D, table in ((1, heads, width, k.h_table), (2, heads, width, k.h_table), (3, 1, C, k.h_table3)):
            g = Gat(buf, n, H, D, table)
            phase_gat_dense(k, g, kb, layers[n - 1][0], layers[n - 1][2], ahead, stage, sb, loads)
            phase_gat_scores(k, g)
            phase_gat_softmax(k, g, s)
            phase_gat_edges(k, g)
            phase_gat_nodes(k, g)
            (ahead, stage), kb = elu_attended(k, g), H * D // P
            sb = [("part", [P, 2, H * D], F32), ("neg", [P, 2, H * D], F32), ("bias", [P, H * D], F32)]
            loads = [("bias", wide(a[f"L1_gnn_b{n}"]))]
        phase_mlp(k, g)


def run_phases(k, stop=None):
    rstd, shift = k.sb("rstd", [P, TILES], F32), k.sb("shift", [P, TILES], F32)
    phase_constants(k, rstd, shift)
    phase_items(k)
    if stop != "skip0":
        phase_qkv(k, rstd, shift)
        phase_attention_edges(k)
        phase_attention_out(k, rstd, shift)
        phase_norm(k, "norm1", k.h, 1e-5, rstd, shift)
        phase_node_ffn(k, rstd, shift)
        phase_norm(k, "norm2", k.x, 1e-5, rstd, shift)
        routed_layer(k, "moe0", "L0_ffn", k.ins["L0_ffn_Wg"], k.ins["L0_ffn_bg"], False, rstd, shift, False)
    attention_layers(k, rstd, shift)
    phase_norm(k, "norm3", k.x, 1e-5, rstd, shift)
    routed_layer(k, "moe1", "L1_ffn", k.ins["L1_ffn_Wr"], k.ins["L1_ffn_br"], True, rstd, shift, True)


_OUT_SHAPE = (N, C)


def program(nc, ins, out, stop=None):
    with ExitStack() as ctx:
        k = Kit(nc, ctx, ins, out)
        run_phases(k, stop)


def host_arrays(inputs):
    import numpy as _np
    a = {n: _np.ascontiguousarray(v) for n, v in inputs.items()}
    for n in ("Wq", "Wk", "Wv", "Wp", "W1", "W2"):
        a["L0_gnn_" + n] = _np.ascontiguousarray(a["L0_gnn_" + n].T)
    a["L0_gnn_Wkv"] = _np.concatenate([a.pop("L0_gnn_Wk"), a.pop("L0_gnn_Wv")], axis=1)
    a["L0_gnn_bkv"] = _np.concatenate([a.pop("L0_gnn_bk"), a.pop("L0_gnn_bv")])
    return a


def declare(nc, arrays):
    return {n: nc.dram_tensor(f"in_{n}", v.shape, mybir.dt.from_np(v.dtype), kind="ExternalInput").ap()
            for n, v in arrays.items()}


def kernel(**inputs):
    import concourse.bacc as _bacc
    from concourse.bass_utils import run_bass_kernel_spmd as _run

    nc = _bacc.Bacc("TRN2", target_bir_lowering=False, num_devices=1)
    arrays = host_arrays(inputs)
    ins = declare(nc, arrays)
    out = nc.dram_tensor("out_x", _OUT_SHAPE, F32, kind="ExternalOutput").ap()
    program(nc, ins, out)
    r = _run(nc, [{f"in_{n}": v for n, v in arrays.items()}], core_ids=[0])
    return r.results[0]["out_x"]
```
